# Optimizing a Trainium2 kernel written in Bass

```python
import numpy as np
import jax
import jax.numpy as jnp

def _softmax(x, axis=-1):
    return jax.nn.softmax(x, axis=axis)

def _gelu(x):
    return jax.nn.gelu(x, approximate=True)

def _silu(x):
    return jax.nn.silu(x)

def _sigmoid(x):
    return jax.nn.sigmoid(x)

def _layernorm(x, axis=-1, eps=1e-05):
    m = jnp.mean(x, axis=axis, keepdims=True)
    v = jnp.var(x, axis=axis, keepdims=True)
    return (x - m) / jnp.sqrt(v + eps)

def _scatter_add(tgt, idx, src, axis=0):
    return tgt.at[idx].add(src)

def _segment_sum(src, seg, n):
    return jax.ops.segment_sum(src, seg, n)
kernel_name = 'mk_flamingo_gated_d2_seqx_r8_9a3f11'

def setup_inputs(seed: int=0):
    np.random.seed(seed)
    _w = jnp.asarray

    def _rec_inputs():
        import jax
        import jax.numpy as jnp
        _rk = jax.random.key(seed)
        x = -0.000125 + 0.9999 * jax.random.normal(jax.random.fold_in(_rk, 1), (32, 56, 128), jnp.float32)
        _lenS = 56 - jax.random.randint(jax.random.fold_in(_rk, 7), (32,), 0, max(1, 56 // 4) + 1, jnp.int32)
        _lenS2 = 1500 - jax.random.randint(jax.random.fold_in(_rk, 8), (32,), 0, max(1, 1500 // 4) + 1, jnp.int32)
        _ctx_1024P = jax.random.normal(jax.random.fold_in(_rk, 11), (32, 16, 128), jnp.float32)
        _ctx_1024c = jax.random.dirichlet(jax.random.fold_in(_rk, 511), 0.3 * jnp.ones((16,), jnp.float32), (32, 1500))
        _ctx_1024t = jnp.einsum('bsk,bkd->bsd', _ctx_1024c, _ctx_1024P)
        _ctx_1024t = _ctx_1024t * jax.lax.rsqrt(jnp.mean(jnp.square(_ctx_1024t)) + 1e-12) * 0.953939
        ctx_1024 = 0.00171412 + 0.999381 * (_ctx_1024t + 0.3 * jax.random.normal(jax.random.fold_in(_rk, 611), (32, 1500, 128), jnp.float32))
        _g = jax.random.normal(jax.random.fold_in(_rk, 9001), (2, 2), jnp.float32)
        _g = jnp.sign(_g) * jnp.maximum(jnp.abs(_g), 1.0) + (_g == 0) * 1.0
        g_xattn = _g[0]
        g_ffn = _g[1]
        return (x, ctx_1024, g_xattn, g_ffn)
    x, ctx_1024, g_xattn, g_ffn = _rec_inputs()

    def _L0_xattn_setup():
        import jax, jax.numpy as jnp
        import numpy as np
        C = 128
        B, HW, N = (8, 512, 77)
        key = jax.random.key(seed)
        ks = jax.random.split(key, 14)
        s = 1.0 / np.sqrt(C)
        inp = {'vis_features': jax.random.normal(ks[0], (B, HW, C), jnp.float32), 'lang_features': jax.random.normal(ks[1], (B, N, C), jnp.float32), 'W_vk': jax.random.uniform(ks[2], (C, C), jnp.float32, -s, s), 'b_vk': jax.random.uniform(ks[3], (C,), jnp.float32, -s, s), 'W_lk': jax.random.uniform(ks[4], (C, C), jnp.float32, -s, s), 'b_lk': jax.random.uniform(ks[5], (C,), jnp.float32, -s, s), 'W_vv': jax.random.uniform(ks[6], (C, C), jnp.float32, -s, s), 'b_vv': jax.random.uniform(ks[7], (C,), jnp.float32, -s, s), 'W_lv': jax.random.uniform(ks[8], (C, C), jnp.float32, -s, s), 'b_lv': jax.random.uniform(ks[9], (C,), jnp.float32, -s, s)}
        return inp
    _L0_xattn_all = _L0_xattn_setup()
    _L0_xattn_in = {k: v for k, v in _L0_xattn_all.items() if k in ('W_vk', 'b_vk', 'W_lk', 'b_lk', 'W_vv', 'b_vv', 'W_lv', 'b_lv')}
    del _L0_xattn_all

    def _L0_ffn_setup():
        import math
        import jax, jax.numpy as jnp
        import numpy as np
        NUM_EXPERTS = 16
        TOP_K = 2
        CAPACITY_FACTOR = 1.25
        key = jax.random.key(seed)
        k1, k2, k3, k4 = jax.random.split(key, 4)
        d, dff, E = (128, 512, NUM_EXPERTS)
        x = jax.random.normal(k1, (4, 256, d), dtype=jnp.float32)
        router_w = jax.random.normal(k2, (E, d), dtype=jnp.float32) * d ** (-0.5)
        router_b = jnp.zeros((E,), dtype=jnp.float32)
        w1 = jax.random.normal(k3, (E, d, dff), dtype=jnp.float32) * 0.02
        b1 = jnp.zeros((E, dff), dtype=jnp.float32)
        w2 = jax.random.normal(k4, (E, dff, d), dtype=jnp.float32) * 0.02
        b2 = jnp.zeros((E, d), dtype=jnp.float32)
        return {'x': x, 'router_w': router_w, 'router_b': router_b, 'w1': w1, 'b1': b1, 'w2': w2, 'b2': b2}
    _L0_ffn_all = _L0_ffn_setup()
    _L0_ffn_in = {k: v for k, v in _L0_ffn_all.items() if k in ('router_w', 'router_b', 'w1', 'b1', 'w2', 'b2')}
    del _L0_ffn_all

    def _L1_xattn_setup():
        import jax, jax.numpy as jnp
        import numpy as np
        EMBED_DIM = 128
        NUM_HEADS = 16
        HEAD_DIM = EMBED_DIM // NUM_HEADS
        B, N, M = (4, 256, 256)

        def _split_heads(x):
            b, t, _ = x.shape
            return x.reshape(b, t, NUM_HEADS, HEAD_DIM).transpose(0, 2, 1, 3)
        key = jax.random.key(seed)
        ks = jax.random.split(key, 10)
        s = 1.0 / np.sqrt(EMBED_DIM)
        return {'query_modal': jax.random.normal(ks[0], (B, N, EMBED_DIM), jnp.float32), 'key_value_modal': jax.random.normal(ks[1], (B, M, EMBED_DIM), jnp.float32), 'Wq': jax.random.normal(ks[2], (EMBED_DIM, EMBED_DIM), jnp.float32) * s, 'bq': jnp.zeros((EMBED_DIM,), jnp.float32), 'Wk': jax.random.normal(ks[3], (EMBED_DIM, EMBED_DIM), jnp.float32) * s, 'bk': jnp.zeros((EMBED_DIM,), jnp.float32), 'Wv': jax.random.normal(ks[4], (EMBED_DIM, EMBED_DIM), jnp.float32) * s, 'bv': jnp.zeros((EMBED_DIM,), jnp.float32), 'Wo': jax.random.normal(ks[5], (EMBED_DIM, EMBED_DIM), jnp.float32) * s, 'bo': jnp.zeros((EMBED_DIM,), jnp.float32)}
    _L1_xattn_all = _L1_xattn_setup()
    _L1_xattn_in = {k: v for k, v in _L1_xattn_all.items() if k in ('Wq', 'bq', 'Wk', 'bk', 'Wv', 'bv', 'Wo', 'bo')}
    del _L1_xattn_all

    def _L1_ffn_setup():
        import jax, jax.numpy as jnp
        import numpy as np
        DIM = 128
        HID = 352
        E = 8
        TOP_K = 2
        EPS = 1e-06

        def _rmsnorm(x, w):
            var = jnp.mean(jnp.square(x), axis=-1, keepdims=True)
            return x * jax.lax.rsqrt(var + EPS) * w
        key = jax.random.key(seed)
        ks = jax.random.split(key, 5)
        x = jax.random.normal(ks[0], (4, 256, DIM), dtype=jnp.float32)
        norm_weight = jnp.ones((DIM,), dtype=jnp.float32)
        router_weight = jax.random.normal(ks[1], (E, DIM), dtype=jnp.float32) * 0.02
        gate_up_weight = jax.random.normal(ks[2], (E, 2 * HID, DIM), dtype=jnp.float32) * (0.02 / np.sqrt(E))
        down_weight = jax.random.normal(ks[3], (E, DIM, HID), dtype=jnp.float32) * (0.02 / np.sqrt(E))
        residual_alpha = jnp.float32(1.0)
        return {'x': x, 'norm_weight': norm_weight, 'router_weight': router_weight, 'gate_up_weight': gate_up_weight, 'down_weight': down_weight, 'residual_alpha': residual_alpha}
    _L1_ffn_all = _L1_ffn_setup()
    _L1_ffn_in = {k: v for k, v in _L1_ffn_all.items() if k in ('norm_weight', 'router_weight', 'gate_up_weight', 'down_weight', 'residual_alpha')}
    del _L1_ffn_all
    return {'x': x, 'ctx_1024': ctx_1024, 'g_xattn': g_xattn, 'g_ffn': g_ffn, 'L0_xattn_W_vk': _L0_xattn_in['W_vk'], 'L0_xattn_b_vk': _L0_xattn_in['b_vk'], 'L0_xattn_W_lk': _L0_xattn_in['W_lk'], 'L0_xattn_b_lk': _L0_xattn_in['b_lk'], 'L0_xattn_W_vv': _L0_xattn_in['W_vv'], 'L0_xattn_b_vv': _L0_xattn_in['b_vv'], 'L0_xattn_W_lv': _L0_xattn_in['W_lv'], 'L0_xattn_b_lv': _L0_xattn_in['b_lv'], 'L0_ffn_router_w': _L0_ffn_in['router_w'], 'L0_ffn_router_b': _L0_ffn_in['router_b'], 'L0_ffn_w1': _L0_ffn_in['w1'], 'L0_ffn_b1': _L0_ffn_in['b1'], 'L0_ffn_w2': _L0_ffn_in['w2'], 'L0_ffn_b2': _L0_ffn_in['b2'], 'L1_xattn_Wq': _L1_xattn_in['Wq'], 'L1_xattn_bq': _L1_xattn_in['bq'], 'L1_xattn_Wk': _L1_xattn_in['Wk'], 'L1_xattn_bk': _L1_xattn_in['bk'], 'L1_xattn_Wv': _L1_xattn_in['Wv'], 'L1_xattn_bv': _L1_xattn_in['bv'], 'L1_xattn_Wo': _L1_xattn_in['Wo'], 'L1_xattn_bo': _L1_xattn_in['bo'], 'L1_ffn_norm_weight': _L1_ffn_in['norm_weight'], 'L1_ffn_router_weight': _L1_ffn_in['router_weight'], 'L1_ffn_gate_up_weight': _L1_ffn_in['gate_up_weight'], 'L1_ffn_down_weight': _L1_ffn_in['down_weight'], 'L1_ffn_residual_alpha': _L1_ffn_in['residual_alpha']}

def reference(x, ctx_1024, g_xattn, g_ffn, L0_xattn_W_vk, L0_xattn_b_vk, L0_xattn_W_lk, L0_xattn_b_lk, L0_xattn_W_vv, L0_xattn_b_vv, L0_xattn_W_lv, L0_xattn_b_lv, L0_ffn_router_w, L0_ffn_router_b, L0_ffn_w1, L0_ffn_b1, L0_ffn_w2, L0_ffn_b2, L1_xattn_Wq, L1_xattn_bq, L1_xattn_Wk, L1_xattn_bk, L1_xattn_Wv, L1_xattn_bv, L1_xattn_Wo, L1_xattn_bo, L1_ffn_norm_weight, L1_ffn_router_weight, L1_ffn_gate_up_weight, L1_ffn_down_weight, L1_ffn_residual_alpha):
    import jax
    import jax.numpy as jnp

    def _L0_xattn_ref(vis_features, lang_features, W_vk, b_vk, W_lk, b_lk, W_vv, b_vv, W_lv, b_lv):
        import jax, jax.numpy as jnp
        import numpy as np
        C = 128
        B, HW, N = (8, 512, 77)
        scale = jnp.asarray(C, vis_features.dtype) ** (-0.5)
        vis_key = jnp.einsum('bsc,dc->bsd', vis_features, W_vk) + b_vk
        lang_key = jnp.einsum('bnc,dc->bnd', lang_features, W_lk) + b_lk
        vis_value = jnp.einsum('bsc,dc->bsd', vis_features, W_vv) + b_vv
        lang_value = jnp.einsum('bnc,dc->bnd', lang_features, W_lv) + b_lv
        attn = jax.nn.softmax(jnp.einsum('bsd,bnd->bsn', vis_key, lang_key) * scale, axis=-1)
        lang_attended_vis = jnp.einsum('bsn,bnc->bsc', attn, lang_value)
        vision_attended_lang = jnp.einsum('bsn,bsc->bnc', attn, vis_value)
        projected = jnp.einsum('bsn,bnc->bsc', attn, vision_attended_lang)
        return lang_attended_vis + projected

    def _L0_ffn_ref(x, router_w, router_b, w1, b1, w2, b2):
        import math
        import jax, jax.numpy as jnp
        import numpy as np
        NUM_EXPERTS = 16
        TOP_K = 2
        CAPACITY_FACTOR = 1.25
        E, k = (NUM_EXPERTS, TOP_K)
        B, S, d = x.shape
        tokens = B * S
        capacity = max(1, int(math.ceil(CAPACITY_FACTOR * tokens * k / E)))
        x2d = x.reshape(tokens, d)
        logits = x2d @ router_w.T + router_b
        vals, idx = jax.lax.top_k(logits, k)
        gates = jax.nn.softmax(vals, axis=-1)
        flat_e = idx.reshape(-1)
        oh = (flat_e[:, None] == jnp.arange(E)[None, :]).astype(jnp.int32)
        pos = jnp.take_along_axis(jnp.cumsum(oh, axis=0) - 1, flat_e[:, None], axis=1)[:, 0]
        kept = pos < capacity
        kept2 = kept.reshape(tokens, k)
        denom = jnp.sum(gates * kept2, axis=-1, keepdims=True)
        gates = jnp.where(kept2, gates / (denom + 1e-09), 0.0)
        slot = flat_e * capacity + pos
        slot_safe = jnp.where(kept, slot, E * capacity)
        x_rep = jnp.repeat(x2d, k, axis=0)
        buf = jnp.zeros((E * capacity + 1, d), x.dtype).at[slot_safe].set(x_rep)
        packed = buf[:E * capacity].reshape(E, capacity, d)
        h = jax.nn.gelu(jnp.einsum('ecd,edf->ecf', packed, w1) + b1[:, None, :], approximate=False)
        expert_out = jnp.einsum('ecf,efd->ecd', h, w2) + b2[:, None, :]
        eflat = expert_out.reshape(E * capacity, d)
        gathered = eflat[jnp.clip(slot, 0, E * capacity - 1)]
        w = (gates.reshape(-1) * kept.astype(x.dtype))[:, None]
        out = (gathered * w).reshape(tokens, k, d).sum(axis=1)
        return out.reshape(B, S, d)

    def _L1_xattn_ref(query_modal, key_value_modal, Wq, bq, Wk, bk, Wv, bv, Wo, bo):
        import jax, jax.numpy as jnp
        import numpy as np
        EMBED_DIM = 128
        NUM_HEADS = 16
        HEAD_DIM = EMBED_DIM // NUM_HEADS
        B, N, M = (4, 256, 256)

        def _split_heads(x):
            b, t, _ = x.shape
            return x.reshape(b, t, NUM_HEADS, HEAD_DIM).transpose(0, 2, 1, 3)
        q = _split_heads(query_modal @ Wq.T + bq)
        k = _split_heads(key_value_modal @ Wk.T + bk)
        v = _split_heads(key_value_modal @ Wv.T + bv)
        scale = HEAD_DIM ** (-0.5)
        scores = jnp.einsum('bhnd,bhmd->bhnm', q, k) * scale
        attn = jax.nn.softmax(scores, axis=-1)
        x = jnp.einsum('bhnm,bhmd->bhnd', attn, v)
        x = x.transpose(0, 2, 1, 3).reshape(query_modal.shape)
        return x @ Wo.T + bo

    def _L1_ffn_ref(x, norm_weight, router_weight, gate_up_weight, down_weight, residual_alpha):
        import jax, jax.numpy as jnp
        import numpy as np
        DIM = 128
        HID = 352
        E = 8
        TOP_K = 2
        EPS = 1e-06

        def _rmsnorm(x, w):
            var = jnp.mean(jnp.square(x), axis=-1, keepdims=True)
            return x * jax.lax.rsqrt(var + EPS) * w
        normed = _rmsnorm(x, norm_weight)
        logits = jnp.einsum('bsd,ed->bse', normed, router_weight)
        probs = jax.nn.softmax(logits, axis=-1)
        topk_w, topk_idx = jax.lax.top_k(probs, TOP_K)
        topk_w = topk_w / jnp.sum(topk_w, axis=-1, keepdims=True)
        combine = jnp.sum(jax.nn.one_hot(topk_idx, E, dtype=normed.dtype) * topk_w[..., None], axis=-2)
        moe_out = jnp.zeros_like(x)
        for e in range(E):
            gu = jnp.einsum('bsd,hd->bsh', normed, gate_up_weight[e])
            gate, up = (gu[..., :HID], gu[..., HID:])
            hidden = jax.nn.silu(gate) * up
            out_e = jnp.einsum('bsh,dh->bsd', hidden, down_weight[e])
            moe_out = moe_out + combine[..., e, None] * out_e
        alpha = jnp.clip(residual_alpha, -0.5, 2.0)
        return x + alpha * moe_out
    x = x + jnp.tanh(g_xattn[0]) * _L0_xattn_ref(_layernorm(x, axis=-1), ctx_1024, L0_xattn_W_vk, L0_xattn_b_vk, L0_xattn_W_lk, L0_xattn_b_lk, L0_xattn_W_vv, L0_xattn_b_vv, L0_xattn_W_lv, L0_xattn_b_lv)
    x = x + jnp.tanh(g_ffn[0]) * _L0_ffn_ref(_layernorm(x, axis=-1), L0_ffn_router_w, L0_ffn_router_b, L0_ffn_w1, L0_ffn_b1, L0_ffn_w2, L0_ffn_b2)
    x = x + jnp.tanh(g_xattn[1]) * _L1_xattn_ref(_layernorm(x, axis=-1), ctx_1024, L1_xattn_Wq, L1_xattn_bq, L1_xattn_Wk, L1_xattn_bk, L1_xattn_Wv, L1_xattn_bv, L1_xattn_Wo, L1_xattn_bo)
    x = x + jnp.tanh(g_ffn[1]) * _L1_ffn_ref(_layernorm(x, axis=-1), L1_ffn_norm_weight, L1_ffn_router_weight, L1_ffn_gate_up_weight, L1_ffn_down_weight, L1_ffn_residual_alpha)
    return x

_drawn_inputs = setup_inputs


def setup_inputs(seed=0):
    import zlib

    import numpy as np

    out = dict(_drawn_inputs(seed))
    spreads = {'g_ffn': (-1.0, 0.2),
     'L0_ffn_router_b': (0.0, 0.379),
     'L0_ffn_b1': (0.0, 0.639),
     'L0_ffn_b2': (0.0, 0.1),
     'L1_xattn_bq': (0.0, 0.414),
     'L1_xattn_bk': (0.0, 0.8),
     'L1_xattn_bv': (0.0, 0.1),
     'L1_xattn_bo': (0.0, 0.1),
     'L1_ffn_norm_weight': (1.0, 0.6)}
    factors = {'L0_xattn_b_vk': 8.0,
     'L0_xattn_b_lk': 8.0,
     'L0_xattn_W_vv': 8.0,
     'L0_xattn_b_vv': 8.0,
     'L1_ffn_router_weight': 8.0,
     'L1_ffn_gate_up_weight': 8.0,
     'L1_ffn_down_weight': 8.0}
    for name, (base, spread) in spreads.items():
        noise = np.random.default_rng([zlib.crc32(name.encode()), seed]).standard_normal(out[name].shape)
        drawn = base * np.exp(spread * noise) if base else spread * noise
        out[name] = jnp.asarray(drawn.astype(out[name].dtype))
    for name, factor in factors.items():
        out[name] = (out[name] * factor).astype(out[name].dtype)
    return out
```

```python
from contextlib import ExitStack

import numpy as np
import concourse.bass as bass
from concourse import mybir

ALU = mybir.AluOpType
ACT = mybir.ActivationFunctionType
F32 = mybir.dt.float32
BF16 = mybir.dt.bfloat16
U32 = mybir.dt.uint32
AX_X = mybir.AxisListType.X

P = 128
B, T, C, S = 32, 56, 128, 1500
TP = 64
NT = B // 2
KC, NCH = 125, 12
KT, NTH = 500, 3
HALVES = ((0, 64), (64, 128))

E0, FF0, CAP = 16, 512, 280
SLOTS = E0 * CAP
FC0 = FF0 // P
NTILE = (2 * B * T + 8 * (P - 1)) // P
H, HD = 16, 8
NPAIR = H // 2
NG = 6
GW = 3 * T
E1, HID = 8, 352
HCH = ((0, 128), (128, 128), (256, 96))
TG = 8 * T

LN_EPS, RMS_EPS = 1e-5, 1e-6


class Steps:

    def __init__(self, engine, sem, base=0):
        self.engine, self.sem, self.base, self.n = engine, sem, base, 0

    def __call__(self, instruction):
        self.n += 1
        instruction.then_inc(self.sem, 1)

    def wait(self):
        self.engine.wait_ge(self.sem, self.base + self.n)

    def then(self, instruction):
        self(instruction)
        self.wait()


class Space:

    def __init__(self, nc, ctx, phase):
        self.nc, self.ctx, self.phase = nc, ctx, phase
        self.sems = []
        ctx.callback(self.close)

    def close(self):
        if self.sems:
            self.nc.clear_and_free_semaphores(self.sems)
            self.nc.all_engine_barrier()

    def sb(self, name, shape, dt=F32):
        return self.ctx.enter_context(self.nc.sbuf_tensor(f"{self.phase}_{name}", shape, dt))

    def ps(self, name, shape, dt=F32):
        return self.ctx.enter_context(self.nc.psum_tensor(f"{self.phase}_{name}", shape, dt))

    def sem(self, name):
        self.sems.append(self.nc.alloc_semaphore(f"{self.phase}_{name}"))
        return self.sems[-1]


def layer_norm(nc, phase, x, xn, xnT, ident):
    with ExitStack() as ctx:
        sp = Space(nc, ctx, phase)
        stats = sp.sb("stats", [P, NT, 6])
        mv = sp.sb("mv", [P, NT, 2])
        sd = sp.sb("sd", [P, NT])
        rs = sp.sb("rs", [P, NT])
        psT = sp.ps("psT", [P, 2, 512])
        s_dve, s_var, s_sd, s_xn, s_T, s_cp = (sp.sem(n) for n in ("dve", "var", "sd", "xn", "T", "cp"))
        block = ctx.enter_context(nc.Block())

        @block.vector
        def _(dve):
            step = Steps(dve, s_dve)
            for t in range(NT):
                step(nc.vector.bn_stats(stats[:, t, :], x[:, t, :]))
            step.wait()
            for t in range(NT):
                step(nc.vector.bn_aggr(mv[:, t, :], stats[:, t, :]))
            step.wait()
            nc.vector.tensor_scalar(sd[:], mv[:, :, 1], 1.0, LN_EPS, ALU.mult, ALU.add).then_inc(s_var, 1)
            dve.wait_ge(s_sd, 1)
            step.then(nc.vector.reciprocal(rs[:], sd[:]))
            for t in range(NT):
                nc.vector.tensor_scalar(xn[:, t, :], x[:, t, :], mv[:, t, 0:1], rs[:, t:t + 1],
                                        ALU.subtract, ALU.mult).then_inc(s_xn, 1)

        @block.scalar
        def _(act):
            act.wait_ge(s_var, 1)
            nc.scalar.activation(sd[:], sd[:], ACT.Sqrt).then_inc(s_sd, 1)
            for q in range(NT // 4):
                act.wait_ge(s_T, q + 1)
                nc.scalar.copy(xnT[:, 512 * q:512 * q + 512], psT[:, q % 2, :]).then_inc(s_cp, 1)

        @block.tensor
        def _(pe):
            for q in range(NT // 4):
                if q >= 2:
                    pe.wait_ge(s_cp, q - 1)
                pe.wait_ge(s_xn, 4 * q + 4)
                for r in range(4):
                    last = nc.tensor.transpose(psT[:, q % 2, P * r:P * r + P], xn[:, 4 * q + r, :], ident[:])
                last.then_inc(s_T, 1)


def vision_language_attention(nc, x, xnT, ident, tanh_g, rowmask, d):
    with ExitStack() as ctx:
        sp = Space(nc, ctx, "va")
        wvkT, wlk, wvvT, wlvT = (sp.sb(n, [P, C]) for n in ("wvkT", "wlk", "wvvT", "wlvT"))
        bvk, blk = (sp.sb(n, [P, 1]) for n in ("bvk", "blk"))
        bvv, blv = (sp.sb(n, [P, C]) for n in ("bvv", "blv"))
        vkT = sp.sb("vkT", [P, NT * P])
        qT = sp.sb("qT", [P, NT * P])
        vis = sp.sb("vis", [P, NT, C])
        cb = sp.sb("cb", [P, NT])
        ctxT = [sp.sb(f"ctxT{u}", [P, 2, S]) for u in range(2)]
        side = [sp.sb(f"side{u}", [KC, 2, NCH, C + TP]) for u in range(2)]
        q_now = [sp.sb(f"q_now{u}", [P, P]) for u in range(2)]
        prob = [sp.sb(f"prob{u}", [P, S]) for u in range(2)]
        rsum = [sp.sb(f"rsum{u}", [P, 1]) for u in range(2)]
        nmax, nb0, nb1 = (sp.sb(n, [P, 1]) for n in ("nmax", "nb0", "nb1"))
        rinv, rmask, rtg = (sp.sb(n, [P, 1]) for n in ("rinv", "rmask", "rtg"))
        ac, acT, gbd = (sp.sb(n, [P, P]) for n in ("ac", "acT", "gbd"))

        psS = sp.ps("psS", [P, NTH, 512])
        psT = [sp.ps(f"psT{r}", [P, 512]) for r in range(2)]
        psA = sp.ps("psA", [P, 512])
        psM = sp.ps("psM", [P, 512])
        psV = sp.ps("psV", [P, 512])

        s_w, s_cT, s_cN = sp.sem("w"), [sp.sem(f"cT{u}") for u in range(2)], [sp.sem(f"cN{u}") for u in range(2)]
        s_vk, s_vkc, s_q, s_qc, s_v, s_vc, s_cb, s_cbc = (
            sp.sem(n) for n in ("vk", "vkc", "q", "qc", "v", "vc", "cb", "cbc"))
        s_xb, s_gz = sp.sem("xb"), sp.sem("gz")
        s_now, s_sc, s_nb, s_ex, s_T, s_Tc, s_A, s_ac, s_gb, s_aT, s_aTc, s_o, s_x = (
            sp.sem(n) for n in ("now", "sc", "nb", "ex", "T", "Tc", "A", "ac", "gb", "aT", "aTc", "o", "x"))
        s_dve = sp.sem("dve")
        SCALE = float(C) ** -0.5
        TURNS = NT // 2

        block = nc.Block()
        with block:
            @block.sync
            def _(sync):
                for dst, src in ((wvkT, "L0_W_vkT"), (wlk, "L0_W_lk"), (wvvT, "L0_W_vvT"), (wlvT, "L0_W_lvT"),
                                 (bvk, "L0_b_vk"), (blk, "L0_b_lk"), (bvv, "L0_b_vv"), (blv, "L0_b_lv")):
                    sync.dma_start(dst[:], d[src]).then_inc(s_w, 16)

            @block.tensor
            def _(pe):
                pe.wait_ge(s_w, 128)
                for q in range(4):
                    if q:
                        pe.wait_ge(s_vkc, q)
                    nc.tensor.matmul(psS[:, 0, :], wvkT[:], xnT[:, 512 * q:512 * q + 512],
                                     start=True, stop=True).then_inc(s_vk, 1)
                for q in range(4):
                    pe.wait_ge(s_vkc, q + 1)
                    if q:
                        pe.wait_ge(s_qc, q)
                    nc.tensor.matmul(psS[:, 1, :], wlk[:], vkT[:, 512 * q:512 * q + 512],
                                     start=True, stop=True).then_inc(s_q, 1)
                for t in range(NT):
                    last = nc.tensor.matmul(psM[:, t:t + 1], vkT[:, P * t:P * t + P], blk[:], start=True, stop=True)
                last.then_inc(s_cb, 1)
                for t in range(NT):
                    if t >= 2:
                        pe.wait_ge(s_vc, t - 1)
                    nc.tensor.matmul(psT[t % 2][:, 0:C], xnT[:, P * t:P * t + P], wvvT[:],
                                     start=True, stop=True).then_inc(s_v, 1)

            @block.scalar
            def _(act):
                act.wait_ge(s_w, 128)
                for q in range(4):
                    act.wait_ge(s_vk, q + 1)
                    nc.scalar.activation(vkT[:, 512 * q:512 * q + 512], psS[:, 0, :], ACT.Identity,
                                         bias=bvk[:, 0:1]).then_inc(s_vkc, 1)
                for q in range(4):
                    act.wait_ge(s_q, q + 1)
                    nc.scalar.mul(qT[:, 512 * q:512 * q + 512], psS[:, 1, :], SCALE).then_inc(s_qc, 1)
                act.wait_ge(s_cb, 1)
                nc.scalar.mul(cb[:], psM[:, 0:NT], SCALE).then_inc(s_cbc, 1)

            @block.vector
            def _(dve):
                step = Steps(dve, s_dve)
                nc.vector.memset(gbd[:], 0.0).then_inc(s_gz, 1)
                dve.wait_ge(s_w, 128)
                step.then(nc.vector.tensor_scalar(ac[:], blv[:], tanh_g, None, ALU.mult))
                for t in range(NT):
                    nc.vector.tensor_tensor(x[:, t, :], x[:, t, :], ac[:], ALU.add).then_inc(s_xb, 1)
                for t in range(NT):
                    dve.wait_ge(s_v, t + 1)
                    nc.vector.tensor_tensor(vis[:, t, :], psT[t % 2][:, 0:C], bvv[:], ALU.add).then_inc(s_vc, 1)

        block = nc.Block()
        with block:
            @block.sync
            def _(sync):
                def load(i, u, first):
                    tile = 2 * i + u
                    if not first:
                        sync.wait_ge(s_sc, 2 * i + u - 1)
                    sync.dma_start(ctxT[u][:], d["ctxT"][bass.ds(2 * tile, 2)].rearrange("b c s -> c b s")
                                   ).then_inc(s_cT[u], 16)
                    if not first:
                        sync.wait_ge(s_A, 2 * i + u - 1)
                    for b in range(2):
                        sync.dma_start(side[u][:, b, :, 0:C],
                                       d["ctx"][bass.ds(2 * tile + b, 1)].rearrange("o (j k) c -> k (o j) c", k=KC)
                                       ).then_inc(s_cN[u], 16)
                for u in range(2):
                    load(0, u, True)
                with sync.Fori(1, TURNS) as i:
                    for u in range(2):
                        load(i, u, False)

            def turns(engine, body):
                for u in range(2):
                    body(0, u, u == 0, False)
                with engine.Fori(1, TURNS - 1) as i:
                    for u in range(2):
                        body(i, u, False, False)
                for u in range(2):
                    body(TURNS - 1, u, False, u == 1)

            @block.tensor
            def _(pe):
                def scores(i, u):
                    n = 2 * i + u
                    pe.wait_ge(s_cT[u], 16 * i + 16)
                    pe.wait_ge(s_now, n + 1)
                    for th in range(NTH):
                        for b, (lo, hi) in enumerate(HALVES):
                            last = nc.tensor.matmul(psS[lo:hi, th, 0:KT], q_now[u][:, lo:hi],
                                                    ctxT[u][:, b, KT * th:KT * th + KT], start=True, stop=True)
                    last.then_inc(s_sc, 1)

                def body(i, u, first, last_turn):
                    n = 2 * i + u
                    if first:
                        scores(i, u)
                    pe.wait_ge(s_ex, n + 1)
                    if not last_turn:
                        scores(i + u, 1 - u)
                    for r in range(3):
                        if not (first and r < 2):
                            pe.wait_ge(s_Tc, 3 * n + r - 1)
                        for q in range(4):
                            j = 4 * r + q
                            bank = psT[(r + u) % 2]
                            last = nc.tensor.transpose(bank[0:KC, P * q:P * q + P],
                                                       prob[u][:, KC * j:KC * j + KC], ident[:])
                        last.then_inc(s_T, 1)
                    pe.wait_ge(s_cN[u], 32 * i + 32)
                    if not first:
                        pe.wait_ge(s_gb, n)
                    for r in range(3):
                        pe.wait_ge(s_Tc, 3 * n + r + 1)
                        for q in range(4):
                            j = 4 * r + q
                            for b, (lo, hi) in enumerate(HALVES):
                                last = nc.tensor.matmul(psA[lo:hi, 0:C + TP], side[u][:, b, j, C:C + TP],
                                                        side[u][:, b, j, :], start=(j == 0), stop=(j == NCH - 1))
                    last.then_inc(s_A, 1)
                    pe.wait_ge(s_ac, n + 1)
                    if not first:
                        pe.wait_ge(s_x, n)
                    nc.tensor.transpose(psM[:, 0:P], ac[:], ident[:]).then_inc(s_aT, 1)
                    pe.wait_ge(s_aTc, n + 1)
                    pe.wait_ge(s_gb, n + 1)
                    nc.tensor.matmul(psV[:, 0:C], acT[:], wlvT[:], start=True, stop=False)
                    nc.tensor.matmul(psV[:, 0:C], gbd[:], vis[:, bass.ds(n, 1), :] if not isinstance(n, int)
                                     else vis[:, n, :], start=False, stop=True).then_inc(s_o, 1)
                turns(pe, body)

            @block.scalar
            def _(act):
                def body(i, u, first, last_turn):
                    n = 2 * i + u
                    act.wait_ge(s_nb, n + 1)
                    if not (first or (isinstance(n, int) and n == 1)):
                        act.wait_ge(s_T, 3 * n - 3)
                    nc.scalar.activation(prob[u][:].rearrange("p (h k) -> p h k", h=NTH), psS[:, :, 0:KT], ACT.Exp,
                                         bias=nb1[:, 0:1], accum_out=rsum[u][:]).then_inc(s_ex, 1)
                turns(act, body)

            @block.vector
            def _(dve):
                AHEAD, STEPS = 3, 5

                def row(buf, t):
                    return buf[:, t:t + 1] if isinstance(t, int) else buf[:, bass.ds(t, 1)]

                def now(i, u):
                    t = 2 * i + u
                    src = qT[:, P * t:P * t + P] if isinstance(t, int) else qT[:, bass.ds(P * t, P)]
                    nc.vector.tensor_copy(q_now[u][:], src).then_inc(s_now, 1)

                def biases(i, u, step):
                    t = 2 * i + u
                    dve.wait_ge(s_sc, t + 1)
                    step.then(nc.vector.tensor_reduce(nmax[:], psS[:, :, 0:KT], axis=mybir.AxisListType.XY,
                                                      op=ALU.max, negate=True))
                    step.then(nc.vector.tensor_tensor(nb0[:], nmax[:], row(cb, t), ALU.subtract))
                    nc.vector.tensor_tensor(nb1[:], nb0[:], row(cb, t), ALU.add).then_inc(s_nb, 1)

                now(0, 0)
                biases(0, 0, Steps(dve, s_dve, 1))

                def body(i, u, first, last_turn):
                    n = 2 * i + u
                    step = Steps(dve, s_dve, AHEAD + STEPS * n)
                    dve.wait_ge(s_ex, n + 1)
                    if not last_turn:
                        now(i + u, 1 - u)
                    step.then(nc.vector.reciprocal(rinv[:], rsum[u][:]))
                    step(nc.vector.tensor_scalar(rtg[:], rinv[:], tanh_g, None, ALU.mult))
                    step(nc.vector.tensor_scalar(rmask[:], rinv[:], rowmask, None, ALU.mult))
                    for r in range(3):
                        bank = psT[(r + u) % 2]
                        dve.wait_ge(s_T, 3 * n + r + 1)
                        for b, (lo, hi) in enumerate(HALVES):
                            src = bank[0:KC, :].rearrange("p (q s) -> p q s", q=4)[:, :, lo:hi]
                            last = nc.vector.tensor_copy(side[u][:, b, 4 * r:4 * r + 4, C:C + TP], src)
                        last.then_inc(s_Tc, 1)
                    if not last_turn:
                        biases(i + u, 1 - u, step)
                    dve.wait_ge(s_A, n + 1)
                    nc.vector.tensor_copy(ac[:], psA[:, 0:P]).then_inc(s_ac, 1)
                    step.wait()
                    for lo, hi in HALVES:
                        last = nc.vector.tensor_scalar(gbd[lo:hi, lo:hi], psA[lo:hi, C:C + TP], rmask[lo:hi, :], None,
                                                       ALU.mult)
                    last.then_inc(s_gb, 1)
                    dve.wait_ge(s_aT, n + 1)
                    nc.vector.tensor_copy(acT[:], psM[:, 0:P]).then_inc(s_aTc, 1)
                    dve.wait_ge(s_o, n + 1)
                    xt = x[:, n:n + 1, :] if isinstance(n, int) else x[:, bass.ds(n, 1), :]
                    nc.vector.scalar_tensor_tensor(out=xt, in0=psV[:, 0:C].unsqueeze(1), scalar=rtg[:, 0:1], in1=xt,
                                                   op0=ALU.mult, op1=ALU.add).then_inc(s_x, 1)
                    if not last_turn:
                        assert step.n == STEPS
                turns(dve, body)


def route(nc, phase, tokens, tokensT, experts_n, wT, bias, scale, index, weight, slots, zeros, d, tile_expert=None):
    E, capped = experts_n, tile_expert is None
    FAR = float(4 * SLOTS)
    with ExitStack() as ctx:
        r = Space(nc, ctx, phase)
        rwT = r.sb("rwT", [P, E])
        rb, experts = r.sb("rb", [P, NT, E]), r.sb("experts", [P, NT, E])
        before, ones = r.sb("before", [P, P]), r.sb("ones", [P, P])
        beforeb, onesb = r.sb("beforeb", [P, P], BF16), r.sb("onesb", [P, P], BF16)
        mask = r.sb("mask", [P, 1])
        logits, top = r.sb("logits", [P, NT, E]), r.sb("top", [P, NT, 8])
        which = r.sb("which", [P, NT, 8], U32)
        whichf = r.sb("whichf", [P, 2, NT])
        diff, ex, den, tmp = (r.sb(n, [P, NT]) for n in ("diff", "ex", "den", "tmp"))
        gate, kept, pos = (r.sb(n, [P, 2, NT]) for n in ("gate", "kept", "pos"))
        first = r.sb("first", [P, 2, NT])
        chosen = [r.sb(f"chosen{k}", [P, NT, E]) for k in range(2)]
        both = r.sb("both", [P, NT, E], BF16)
        place, prod, base = (r.sb(n, [P, NT, E]) for n in ("place", "prod", "base"))
        total = r.sb("total", [P, NT, E])
        count, tiles, start, end = (r.sb(n, [P, E]) for n in ("count", "tiles", "start", "end"))
        whole = r.sb("whole", [P, E], U32)
        tile_ids, ended = r.sb("tile_ids", [P, NTILE, E]), r.sb("ended", [P, NTILE, E])
        owner = r.sb("owner", [P, NTILE])
        psL, psC = r.ps("psL", [P, 512]), r.ps("psC", [P, 2, 256])
        s_w, s_L, s_both, s_C, s_d, s_ex, s_dve = (r.sem(n) for n in ("w", "L", "both", "C", "d", "ex", "dve"))
        s_zero, s_zd, s_idx, s_scat = (r.sem(n) for n in ("zero", "zd", "idx", "scat"))
        block = ctx.enter_context(nc.Block())
        sources = [(rwT, wT), (experts, f"expert_ids{E}"), (before, "before"), (ones, "ones"), (mask, "rowmask")]
        if bias is not None:
            sources.append((rb, bias))
        if not capped:
            sources.append((tile_ids, "tile_ids"))

        @block.sync
        def _(sync):
            sync.wait_ge(s_zero, 1)
            sync.dma_start(slots.rearrange("(i p) c -> p i c", p=P), zeros[:]).then_inc(s_zd, 16)
            for dst, src in sources:
                sync.dma_start(dst[:], d[src]).then_inc(s_w, 16)

        @block.tensor
        def _(pe):
            pe.wait_ge(s_w, 16 * len(sources))
            for t in range(NT):
                last = nc.tensor.matmul(psL[:, E * t:E * t + E], tokensT[:, P * t:P * t + P], rwT[:],
                                        start=True, stop=True)
            last.then_inc(s_L, 1)
            pe.wait_ge(s_both, 1)
            for k, m in enumerate((beforeb, onesb)):
                last = nc.tensor.matmul(psC[:, k, 0:NT * E], m[:], both[:].rearrange("p t e -> p (t e)"),
                                        start=True, stop=True)
            last.then_inc(s_C, 1)

        @block.scalar
        def _(act):
            act.wait_ge(s_d, 1)
            nc.scalar.activation(ex[:], diff[:], ACT.Exp).then_inc(s_ex, 1)

        @block.vector
        def _(dve):
            v = nc.vector
            step = Steps(dve, s_dve)
            v.memset(zeros[:], 0.0).then_inc(s_zero, 1)
            dve.wait_ge(s_w, 16 * len(sources))
            step(v.tensor_copy(beforeb[:], before[:]))
            step(v.tensor_copy(onesb[:], ones[:]))
            dve.wait_ge(s_L, 1)
            got = psL[:, 0:NT * E].rearrange("p (t e) -> p t e", e=E)
            if bias is not None:
                step.then(v.tensor_tensor(logits[:], got, rb[:], ALU.add))
            else:
                step.then(v.tensor_copy(logits[:], got))
            for t in range(NT):
                step(v.max(out=top[:, t, :], in_=logits[:, t, :]))
            step.wait()
            for t in range(NT):
                step(v.max_index(out=which[:, t, :], in_max=top[:, t, :], in_values=logits[:, t, :]))
            v.tensor_tensor(diff[:], top[:, :, 1], top[:, :, 0], ALU.subtract).then_inc(s_d, 1)
            step.wait()
            for k in range(2):
                step(v.tensor_copy(whichf[:, k, :], which[:, :, k]))
            step.wait()
            for k in range(2):
                step(v.tensor_tensor(chosen[k][:], experts[:],
                                     whichf[:, k, :].unsqueeze(2).broadcast_to([P, NT, E]), ALU.is_equal))
            step.wait()
            for k in range(2):
                step(v.tensor_scalar(chosen[k][:], chosen[k][:], mask[:, 0:1], None, ALU.mult))
            step.wait()
            v.tensor_tensor(both[:], chosen[0][:], chosen[1][:], ALU.add).then_inc(s_both, 1)
            dve.wait_ge(s_ex, 1)
            step.then(v.tensor_scalar(den[:], ex[:], 1.0, None, ALU.add))
            step.then(v.reciprocal(gate[:, 0, :], den[:]))
            step(v.tensor_tensor(gate[:, 1, :], gate[:, 0, :], ex[:], ALU.mult))
            dve.wait_ge(s_C, 1)
            step(v.tensor_copy(total[:], psC[:, 1, 0:NT * E].rearrange("p (t e) -> p t e", e=E)))
            step.then(v.memset(base[:, 0, :], 0.0))
            for t in range(1, NT):
                step.then(v.tensor_tensor(base[:, t, :], base[:, t - 1, :], total[:, t - 1, :], ALU.add))
            step.then(v.tensor_tensor(place[:], psC[:, 0, 0:NT * E].rearrange("p (t e) -> p t e", e=E), base[:],
                                      ALU.add))
            for k in range(2):
                step.then(v.tensor_tensor(prod[:], place[:], chosen[k][:], ALU.mult))
                step.then(v.reduce_sum(pos[:, k, :], prod[:], axis=AX_X))
            if capped:
                step.then(v.tensor_scalar(kept[:], pos[:], float(CAP), None, ALU.is_lt))
                step.then(v.tensor_scalar(kept[:], kept[:], mask[:, 0:1], None, ALU.mult))
                step.then(v.tensor_tensor(gate[:], gate[:], kept[:], ALU.mult))
                step.then(v.tensor_tensor(den[:], gate[:, 0, :], gate[:, 1, :], ALU.add))
                step.then(v.tensor_scalar(den[:], den[:], 1e-9, None, ALU.add))
                step.then(v.reciprocal(den[:], den[:]))
                step.then(v.tensor_tensor(gate[:], gate[:], den[:].unsqueeze(1).broadcast_to([P, 2, NT]), ALU.mult))
                step.then(v.tensor_scalar(first[:], whichf[:], float(CAP), None, ALU.mult))
            else:
                step(v.tensor_scalar(kept[:], pos[:], 0.0, mask[:, 0:1], ALU.mult, ALU.add))
                step.then(v.tensor_tensor(count[:], base[:, NT - 1, :], total[:, NT - 1, :], ALU.add))
                step.then(v.tensor_scalar(whole[:], count[:], float(P - 1), None, ALU.add))
                step.then(v.tensor_scalar(whole[:], whole[:], 7, None, ALU.logical_shift_right))
                step.then(v.tensor_copy(tiles[:], whole[:]))
                step.then(v.memset(start[:, 0:1], 0.0))
                for e in range(1, E):
                    step.then(v.tensor_tensor(start[:, e:e + 1], start[:, e - 1:e], tiles[:, e - 1:e], ALU.add))
                step.then(v.tensor_tensor(end[:], start[:], tiles[:], ALU.add))
                step.then(v.tensor_tensor(ended[:], tile_ids[:], end[:].unsqueeze(1).broadcast_to([P, NTILE, E]),
                                          ALU.is_ge))
                step.then(v.reduce_sum(owner[:], ended[:], axis=AX_X))
                step.then(v.tensor_scalar(tile_expert[:], owner[:], float(E - 1), None, ALU.min))
                for k in range(2):
                    step.then(v.tensor_tensor(prod[:], chosen[k][:], start[:].unsqueeze(1).broadcast_to([P, NT, E]),
                                              ALU.mult))
                    step.then(v.reduce_sum(first[:, k, :], prod[:], axis=AX_X))
                step.then(v.tensor_scalar(first[:], first[:], float(P), None, ALU.mult))
            for k in range(2):
                step.then(v.tensor_scalar(tmp[:], gate[:, k, :], scale, None, ALU.mult))
                step(v.tensor_tensor(weight[k][:], tmp[:], kept[:, k, :], ALU.mult))
                step.then(v.tensor_tensor(diff[:], first[:, k, :], pos[:, k, :], ALU.add))
                step.then(v.tensor_scalar(tmp[:], kept[:, k, :], -FAR, FAR, ALU.mult, ALU.add))
                step.then(v.tensor_tensor(diff[:], diff[:], tmp[:], ALU.add))
                v.tensor_copy(index[k][:], diff[:]).then_inc(s_idx, 1)

        @block.gpsimd
        def _(pool):
            pool.wait_ge(s_zd, 16)
            for k in range(2):
                pool.wait_ge(s_idx, k + 1)
                for t in range(NT):
                    nc.gpsimd.indirect_dma_start(
                        out=slots, out_offset=bass.IndirectOffsetOnAxis(index[k][:, t:t + 1], 0),
                        in_=tokens[:, t, :], in_offset=None, bounds_check=SLOTS - 1, oob_is_err=False
                    ).then_inc(s_scat, 16)
            pool.wait_ge(s_scat, 16 * 2 * NT)


def gather_results(nc, dve, pool, x, results, index, weight, got, s_got, s_used):
    def take():
        for t in range(NT):
            for k in range(2):
                n = 2 * t + k
                q = n % 4
                if n >= 4:
                    pool.wait_ge(s_used[q], n // 4)
                nc.gpsimd.indirect_dma_start(
                    out=got[q][:], out_offset=None, in_=results,
                    in_offset=bass.IndirectOffsetOnAxis(index[k][:, t:t + 1], 0),
                    bounds_check=SLOTS - 1, oob_is_err=False).then_inc(s_got[q], 16)

    def add():
        for t in range(NT):
            for k in range(2):
                n = 2 * t + k
                q = n % 4
                dve.wait_ge(s_got[q], 16 * (n // 4 + 1))
                if k:
                    dve.wait_ge(s_used[(n - 1) % 4], (n - 1) // 4 + 1)
                nc.vector.scalar_tensor_tensor(out=x[:, t, :], in0=got[q][:], scalar=weight[k][:, t:t + 1],
                                               in1=x[:, t, :], op0=ALU.mult, op1=ALU.add).then_inc(s_used[q], 1)
    if dve is not None:
        add()
    else:
        take()


def capacity_experts(nc, x, xn, xnT, ident, tanh_g, d):
    with ExitStack() as ctx:
        sp = Space(nc, ctx, "ce")
        slots = nc.dram_tensor("slots", (SLOTS, C), F32, kind="Internal").ap()
        results = nc.dram_tensor("results", (SLOTS, C), F32, kind="Internal").ap()
        index = [sp.sb(f"index{k}", [P, NT], U32) for k in range(2)]
        weight = [sp.sb(f"weight{k}", [P, NT]) for k in range(2)]
        NROW = SLOTS // P
        rows = sp.sb("rows", [P, NROW, C])
        slotT = sp.sb("slotT", [P, SLOTS])

        route(nc, "r0", xn, xnT, E0, "L0_router_wT", "L0_router_b", tanh_g, index, weight, slots, rows, d)

        with ExitStack() as inner:
            f = Space(nc, inner, "ff")
            w1 = [f.sb(f"w1{u}", [P, FF0]) for u in range(2)]
            w2 = [f.sb(f"w2{u}", [P, FC0, C]) for u in range(2)]
            b1, b2 = f.sb("b1", [P, E0, FC0]), f.sb("b2", [P, E0])
            b1now = [f.sb(f"b1now{u}", [P, FC0]) for u in range(2)]
            hT = [f.sb(f"hT{u}", [P, FC0, CAP]) for u in range(2)]
            outT = f.sb("outT", [P, SLOTS])
            got = [f.sb(f"got{q}", [P, C]) for q in range(4)]
            psT, psH = f.ps("psT", [P, 2, 512]), f.ps("psH", [P, 2, 512])
            psY, psR = f.ps("psY", [P, 2, 512]), f.ps("psR", [P, 2, 512])
            s_b, s_rows, s_T, s_Tc = (f.sem(n) for n in ("b", "rows", "T", "Tc"))
            s_w1, s_w2 = [f.sem(f"w1{u}") for u in range(2)], [f.sem(f"w2{u}") for u in range(2)]
            s_H, s_h, s_Y, s_y, s_bn, s_R, s_r, s_st, s_gz, s_dve = (
                f.sem(n) for n in ("H", "h", "Y", "y", "bn", "R", "r", "st", "gz", "dve"))
            s_got, s_used = [f.sem(f"got{q}") for q in range(4)], [f.sem(f"used{q}") for q in range(4)]
            block = inner.enter_context(nc.Block())
            QT = -(-NROW // 4)

            def at(buf, n, width):
                return buf[:, width * n:width * n + width] if isinstance(n, int) else buf[:, bass.ds(width * n, width)]

            @block.sync
            def _(sync):
                sync.dma_start(rows[:], slots.rearrange("(i p) c -> p i c", p=P)).then_inc(s_rows, 16)
                sync.dma_start(b1[:], d["L0_b1"]).then_inc(s_b, 16)
                sync.dma_start(b2[:], d["L0_b2"]).then_inc(s_b, 16)

                def load(i, u, first):
                    e = 2 * i + u
                    if not first:
                        sync.wait_ge(s_H, FC0 * (e - 1))
                    sync.dma_start(w1[u][:].unsqueeze(1), d["L0_w1"][bass.ds(e, 1)].rearrange("o c f -> c o f")
                                   ).then_inc(s_w1[u], 16)
                    if not first:
                        sync.wait_ge(s_Y, e - 1)
                    sync.dma_start(w2[u][:], d["L0_w2"][bass.ds(e, 1)].rearrange("o (q f) c -> f (o q) c", f=P)
                                   ).then_inc(s_w2[u], 16)
                for u in range(2):
                    load(0, u, True)
                with sync.Fori(1, E0 // 2) as i:
                    for u in range(2):
                        load(i, u, False)
                sync.wait_ge(s_r, NROW // 4 + 1)
                sync.dma_start(results.rearrange("(i p) c -> p i c", p=P), rows[:]).then_inc(s_st, 16)

            @block.tensor
            def _(pe):
                pe.wait_ge(s_rows, 16)
                for q in range(QT):
                    if q >= 2:
                        pe.wait_ge(s_Tc, q - 1)
                    for r in range(min(4, NROW - 4 * q)):
                        last = nc.tensor.transpose(psT[:, q % 2, P * r:P * r + P], rows[:, 4 * q + r, :], ident[:])
                    last.then_inc(s_T, 1)
                pe.wait_ge(s_Tc, QT)

                def expert(i, u, first):
                    e = 2 * i + u
                    pe.wait_ge(s_w1[u], 16 * i + 16)
                    for q in range(FC0):
                        if not (first and e == 0 and q < 2):
                            pe.wait_ge(s_h, FC0 * e + q - 1)
                        nc.tensor.matmul(psH[:, q % 2, 0:CAP], w1[u][:, P * q:P * q + P], at(slotT, e, CAP),
                                         start=True, stop=True).then_inc(s_H, 1)
                    pe.wait_ge(s_w2[u], 16 * i + 16)
                    if not first:
                        pe.wait_ge(s_y, e - 1)
                    for q in range(FC0):
                        pe.wait_ge(s_h, FC0 * e + q + 1)
                        last = nc.tensor.matmul(psY[:, u, 0:CAP], w2[u][:, q, :], hT[u][:, q, :],
                                                start=(q == 0), stop=(q == FC0 - 1))
                    last.then_inc(s_Y, 1)
                for u in range(2):
                    expert(0, u, True)
                with pe.Fori(1, E0 // 2) as i:
                    for u in range(2):
                        expert(i, u, False)
                pe.wait_ge(s_y, E0)
                for q in range(QT):
                    if q >= 2:
                        pe.wait_ge(s_r, q - 1)
                    for r in range(min(4, NROW - 4 * q)):
                        c0 = P * (4 * q + r)
                        last = nc.tensor.transpose(psR[:, q % 2, P * r:P * r + P], outT[:, c0:c0 + P], ident[:])
                    last.then_inc(s_R, 1)

            @block.scalar
            def _(act):
                for q in range(QT):
                    n = P * min(4, NROW - 4 * q)
                    act.wait_ge(s_T, q + 1)
                    nc.scalar.copy(slotT[:, 512 * q:512 * q + n], psT[:, q % 2, 0:n]).then_inc(s_Tc, 1)

                def expert(i, u, first):
                    e = 2 * i + u
                    act.wait_ge(s_bn, e + 1)
                    if not first:
                        act.wait_ge(s_Y, e - 1)
                    for q in range(FC0):
                        act.wait_ge(s_H, FC0 * e + q + 1)
                        nc.scalar.activation(hT[u][:, q, :], psH[:, q % 2, 0:CAP], ACT.Gelu,
                                             bias=b1now[u][:, q:q + 1]).then_inc(s_h, 1)
                for u in range(2):
                    expert(0, u, True)
                with act.Fori(1, E0 // 2) as i:
                    for u in range(2):
                        expert(i, u, False)

            @block.vector
            def _(dve):
                v = nc.vector
                for q in range(4):
                    last = v.memset(got[q][:], 0.0)
                last.then_inc(s_gz, 1)
                dve.wait_ge(s_b, 32)

                def expert(i, u, first):
                    e = 2 * i + u
                    if not first:
                        dve.wait_ge(s_h, FC0 * (e - 1))
                    b1e = b1[:, e:e + 1, :] if isinstance(e, int) else b1[:, bass.ds(e, 1), :]
                    v.tensor_copy(b1now[u][:].unsqueeze(1), b1e).then_inc(s_bn, 1)

                def result(i, u):
                    e = 2 * i + u
                    dve.wait_ge(s_Y, e + 1)
                    b2e = b2[:, e:e + 1] if isinstance(e, int) else b2[:, bass.ds(e, 1)]
                    v.tensor_scalar(at(outT, e, CAP), psY[:, u, 0:CAP], b2e, None, ALU.add).then_inc(s_y, 1)
                for u in range(2):
                    expert(0, u, True)
                with dve.Fori(1, E0 // 2) as i:
                    for u in range(2):
                        result(i - 1, u)
                        expert(i, u, False)
                for u in range(2):
                    result(E0 // 2 - 1, u)
                for q in range(QT):
                    n = min(4, NROW - 4 * q)
                    dve.wait_ge(s_R, q + 1)
                    v.tensor_copy(rows[:, 4 * q:4 * q + n, :],
                                  psR[:, q % 2, 0:P * n].rearrange("p (r c) -> p r c", r=n)).then_inc(s_r, 1)
                gather_results(nc, dve, None, x, results, index, weight, got, s_got, s_used)

            @block.gpsimd
            def _(pool):
                pool.wait_ge(s_gz, 1)
                pool.wait_ge(s_st, 16)
                gather_results(nc, None, pool, x, results, index, weight, got, s_got, s_used)


def attention(nc, x, xnT, tanh_g, identb, d):
    SCALE = float(HD) ** -0.5
    PARTS_K, PARTS_Q = (0, 1, 2, 0, 1, 0), (0, 0, 0, 1, 1, 2)
    SR, MR = 6 * 2 * HD, 3 * NPAIR
    PW, QW = 2 * T, H * T
    MAXIMA = (1, 1, 1, 3, 3, 3, 4, 4, 4, 0, 0, 0)
    VALUES = 2
    qd = nc.dram_tensor("q_parts", (NPAIR, 6, 2, HD, NT * P), BF16, kind="Internal").ap()
    kd = nc.dram_tensor("k_parts", (2, NTH, NPAIR, 3, 2, HD, KT), BF16, kind="Internal").ap()

    with ExitStack() as ctx:
        sp = Space(nc, ctx, "at")
        wkT, wvT = sp.sb("wkT", [P, C]), sp.sb("wvT", [P, NG * 24])
        bk = sp.sb("bk", [P, 1])
        woT = sp.sb("woT", [P, 2, C])
        sel, own = sp.sb("sel", [P, 3, P]), sp.sb("own", [P, 3])
        qmask = sp.sb("qmask", [SR, QW], BF16)
        own_pair = sp.sb("own_pair", [P, QW])
        kst = [sp.sb(f"kst{u}", [SR + MR, NPAIR, S], BF16) for u in range(2)]
        val = [sp.sb(f"val{u}", [KC, NCH, NG, 32]) for u in range(2)]
        prob = [sp.sb(f"prob{u}", [KC, NG * GW]) for u in range(2)]
        zeros = sp.sb("zeros", [P, KT])

        with ExitStack() as inner:
            q = Space(nc, inner, "aq")
            wqT, wo_plain, bvc = q.sb("wqT", [P, C]), q.sb("wo_plain", [P, C]), q.sb("bvc", [P, P])
            bq, bqs, bo = q.sb("bq", [P, 1]), q.sb("bqs", [P, 1]), q.sb("bo", [P, C])
            q32, rest = q.sb("q32", [P, NT * P]), q.sb("rest", [P, NT * P])
            parts = q.sb("parts", [P, 3, NT * P], BF16)
            mask32, out_b = q.sb("mask32", [SR, QW]), q.sb("out_b", [P, C])
            psQ, psB = q.ps("psQ", [P, 4, 512]), q.ps("psB", [P, 512])
            s_w, s_q, s_q32, s_B, s_parts, s_st, s_dve, s_bqs, s_pool = (
                q.sem(n) for n in ("w", "q", "q32", "B", "parts", "st", "dve", "bqs", "pool"))
            block = inner.enter_context(nc.Block())
            loads = ((own_pair, "pair_rows"), (wkT, "L1_W_kT"), (wvT, "L1_W_vT"), (bk, "L1_b_k"), (woT, "L1_W_oT"), (sel, "sum_rows"),
                     (own, "own_rows"), (mask32, "pair_mask"), (wqT, "L1_W_qT"), (wo_plain, "L1_W_oT_plain"),
                     (bvc, "L1_b_v"), (bq, "L1_b_q"), (bo, "L1_b_o"))

            @block.sync
            def _(sync):
                for dst, src in loads:
                    sync.dma_start(dst[:], d[src]).then_inc(s_w, 16)
                for k in range(3):
                    sync.wait_ge(s_parts, k + 1)
                    for c in range(6):
                        if PARTS_Q[c] == k:
                            sync.dma_start(qd[:, c], parts[:, k, :]).then_inc(s_st, 16)
                sync.wait_ge(s_st, 96)

            @block.tensor
            def _(pe):
                pe.wait_ge(s_w, 16 * len(loads))
                for k in range(4):
                    nc.tensor.matmul(psQ[:, k, :], wqT[:], xnT[:, 512 * k:512 * k + 512], start=True, stop=True
                                     ).then_inc(s_q, 1)
                nc.tensor.matmul(psB[:, 0:C], bvc[:], wo_plain[:], start=True, stop=True).then_inc(s_B, 1)

            @block.scalar
            def _(act):
                act.wait_ge(s_bqs, 1)
                for k in range(4):
                    act.wait_ge(s_q, k + 1)
                    nc.scalar.activation(q32[:, 512 * k:512 * k + 512], psQ[:, k, :], ACT.Identity, scale=SCALE,
                                         bias=bqs[:, 0:1]).then_inc(s_q32, 1)

            @block.vector
            def _(dve):
                v = nc.vector
                step = Steps(dve, s_dve)
                v.memset(kst[0][SR:SR + MR, :, :], 1.0)
                for u in range(2):
                    v.memset(prob[u][:, QW:NG * GW], 1.0)
                dve.wait_ge(s_w, 16 * len(loads))
                v.tensor_scalar(bqs[:], bq[:], SCALE, None, ALU.mult).then_inc(s_bqs, 1)
                step(v.tensor_copy(qmask[:], mask32[:]))
                dve.wait_ge(s_q32, 4)
                v.tensor_copy(parts[:, 0, :], q32[:]).then_inc(s_parts, 1)
                dve.wait_ge(s_parts, 1)
                step.then(v.tensor_tensor(rest[:], q32[:], parts[:, 0, :], ALU.subtract))
                v.tensor_copy(parts[:, 1, :], rest[:]).then_inc(s_parts, 1)
                dve.wait_ge(s_parts, 2)
                v.tensor_tensor(parts[:, 2, :], rest[:], parts[:, 1, :], ALU.subtract).then_inc(s_parts, 1)
                dve.wait_ge(s_B, 1)
                step.then(v.tensor_tensor(out_b[:], psB[:, 0:C], bo[:], ALU.add))
                for t in range(NT):
                    step(v.scalar_tensor_tensor(out=x[:, t, :], in0=out_b[:], scalar=tanh_g, in1=x[:, t, :],
                                                op0=ALU.mult, op1=ALU.add))

            @block.gpsimd
            def _(pool):
                step = Steps(pool, s_pool)
                step.then(nc.gpsimd.memset(val[0][:], 1.0))
                step.then(nc.gpsimd.memset(val[1][:], 1.0))
                step.then(nc.gpsimd.memset(zeros[:], 0.0))
                step.then(nc.gpsimd.memset(kst[1][SR:SR + MR, :, :], 1.0))

        ctxT = [sp.sb(f"ctxT{u}", [P, S]) for u in range(2)]
        kparts = sp.sb("kparts", [P, NTH, 3, KT], BF16)
        krest = sp.sb("krest", [P, NTH, KT])
        qraw = [sp.sb(f"qraw{u}", [SR, NPAIR, 2, T], BF16) for u in range(2)]
        qmx = [sp.sb(f"qmx{u}", [SR, QW], BF16) for u in range(2)]
        qst = [sp.sb(f"qst{u}", [SR + MR, QW], BF16) for u in range(2)]
        mx, nmx, mrest = sp.sb("mx", [PW, NTH, NPAIR]), sp.sb("nmx", [PW, NPAIR]), sp.sb("mrest", [PW, NPAIR])
        mparts = sp.sb("mparts", [PW, 3, NPAIR], BF16)
        sums = sp.sb("sums", [P, 2, 3, T])
        mine, recip, attn = (sp.sb(n, [P, 2, T]) for n in ("mine", "recip", "attn"))

        psS = sp.ps("psS", [P, 2, 2, 512])
        psO = sp.ps("psO", [P, 512])
        psV = sp.ps("psV", [P, 512])
        psR = [sp.ps(f"psR{r}", [P, 512]) for r in range(2)]

        s_ctx, s_ql = [sp.sem(f"ctx{u}") for u in range(2)], [sp.sem(f"ql{u}") for u in range(2)]
        s_kw, s_kl = [sp.sem(f"kw{i}") for i in range(NTH)], [sp.sem(f"kl{i}") for i in range(NTH)]
        (s_full, s_free, s_hi, s_kp, s_qm, s_qs, s_mp, s_S, s_exp, s_PV, s_V, s_Vc, s_ou, s_on, s_dm, s_do,
         s_pool, s_set) = (sp.sem(n) for n in (
            "full", "free", "hi", "kp", "qm", "qs", "mp", "S", "exp", "PV", "V", "Vc", "ou", "on", "dm", "do",
            "pool", "set"))

        def ring(b):
            known = isinstance(b, int)
            keys, maxima, ends = (not known or b <= B - 3), (not known or -1 <= b <= B - 2), (not known or b >= 1)
            units, m = [[] for _ in range(NCH)], 0
            for j in range(NCH):
                if keys and j < NTH:
                    units[j].append(("keys", j))
                if ends and j == 2:
                    units[j].append(("sums", 0))
                if maxima:
                    units[j] += [("max", m + r) for r in range(MAXIMA[j])]
                    m += MAXIMA[j]
                if ends and j == 5:
                    units[j].append(("out", 0))
                if maxima and j == 10:
                    units[j].append(("rows", 0))
            return units

        def size(b):
            return sum(len(u) for u in ring(b))

        UNITS = size(2)
        FIRST = sum(size(b) for b in range(-2, 2))
        assert UNITS % 2 == 0

        class Ring:

            def __init__(self, b):
                if isinstance(b, int):
                    self.n = sum(size(c) for c in range(-2, b))
                    self.parity = self.n % 2
                else:
                    self.n, self.parity = FIRST - 2 * UNITS + b * UNITS, FIRST % 2

            def chunks(self, b):
                local, out = 0, []
                for units in ring(b):
                    row = []
                    for kind, idx in units:
                        row.append((kind, idx, self.n + local, (self.parity + local) % 2))
                        local += 1
                    out.append(row)
                return out

        def steps(engine, body):
            for b in range(-2, 2):
                body(b // 2, b % 2)
            with engine.Fori(1, B // 2 - 1) as k:
                for u in range(2):
                    body(k, u)
            for b in range(B - 2, B + 1):
                body(b // 2, b % 2)

        def has(b, lo, hi):
            return not isinstance(b, int) or lo <= b <= hi

        block = ctx.enter_context(nc.Block())

        @block.sync
        def _(sync):
            def load_ctx(c, u):
                sync.dma_start(ctxT[u][:].unsqueeze(1), d["ctxT"][bass.ds(c, 1)].rearrange("o c s -> c o s")
                               ).then_inc(s_ctx[u], 16)

            def body(k, u):
                b, w = 2 * k + u, 1 - u
                if has(b, -2, B - 3):
                    if has(b, 0, B):
                        sync.wait_ge(s_qm, b + 1)
                    for r in range(2):
                        src = qd.rearrange("p c r d t -> (c r d) p t")[:, :, bass.ds((b + 2) * TP, T)]
                        sync.dma_start(qraw[u][:, :, r, :], src).then_inc(s_ql[u], 16)
                    if has(b, 0, B):
                        for i in range(NTH):
                            sync.wait_ge(s_kl[i], 48 * (b + 1))
                    for i in range(NTH):
                        sync.wait_ge(s_kp, 3 * (b + 2) + i + 1)
                        for c in range(3):
                            sync.dma_start(kd[u, i, :, c], kparts[:, i, c, :]).then_inc(s_kw[i], 16)

                def stack(i):
                    if has(b, 0, B):
                        sync.wait_ge(s_S, NCH * b + 4 * i + 4)
                    sync.wait_ge(s_kw[i], 48 * (b + 3))
                    for n, row in ((3, 0), (2, 48), (1, 80)):
                        src = kd[u, i][:, 0:n].rearrange("p c r d k -> (c r d) p k")
                        sync.dma_start(kst[u][row:row + 16 * n, :, KT * i:KT * i + KT], src).then_inc(s_kl[i], 16)
                if has(b, -2, B - 3):
                    stack(0)
                if has(b, -2, B - 4):
                    if has(b, -1, B):
                        sync.wait_ge(s_V, 6 * (b + 2))
                    load_ctx(b + 3, w)
                if has(b, -2, B - 3):
                    stack(1)
                if has(b, -2, B - 3):
                    stack(2)

            load_ctx(0, 0)
            sync.wait_ge(s_set, 1)
            for b in range(-2, 2):
                body(b // 2, b % 2)
            with sync.Fori(1, B // 2 - 2) as k:
                for u in range(2):
                    body(k, u)
            for b in range(B - 4, B + 1):
                body(b // 2, b % 2)

        @block.tensor
        def _(pe):
            pe.wait_ge(s_set, 1)

            def body(k, u):
                b, w = 2 * k + u, 1 - u
                units = Ring(b).chunks(b)
                def unit(kind, idx, n, bank):
                    if not (isinstance(n, int) and n < 2):
                        pe.wait_ge(s_free, n - 1)
                    R = psR[bank]
                    if kind == "keys":
                        if idx == 0:
                            pe.wait_ge(s_ctx[u], 16 * (k + 2))
                        last = nc.tensor.matmul(R[:, 0:KT], wkT[:], ctxT[u][:, KT * idx:KT * idx + KT],
                                                start=True, stop=True)
                    elif kind == "max":
                        i, p = idx // NPAIR, idx % NPAIR
                        if p == 0:
                            pe.wait_ge(s_kl[i], 48 * (b + 2))
                        if idx == 0:
                            pe.wait_ge(s_qm, b + 2)
                        last = nc.tensor.matmul(R[0:PW, 0:KT], qmx[w][:, PW * p:PW * p + PW],
                                                kst[w][0:SR, p, KT * i:KT * i + KT], start=True, stop=True)
                    elif kind == "sums":
                        pe.wait_ge(s_ou, b)
                        for r in range(3):
                            last = nc.tensor.matmul(R[:, 0:2 * T].rearrange("p (s t) -> p s t", s=2),
                                                    sel[:, r, :], sums[:, :, r, :], start=(r == 0), stop=(r == 2))
                    elif kind == "out":
                        pe.wait_ge(s_on, b)
                        for s in range(2):
                            last = nc.tensor.matmul(R[64 * w:64 * w + T, 0:C], attn[:, s, :], woT[:, s, :],
                                                    start=(s == 0), stop=(s == 1))
                    else:
                        pe.wait_ge(s_mp, b + 2)
                        last = nc.tensor.matmul(R[SR:SR + MR, 0:PW], mparts[:].rearrange("q c p -> q (c p)"),
                                                identb[0:PW, 0:PW], start=True, stop=True)
                    last.then_inc(s_full, 1)

                for j in range(NCH):
                    g = NCH * b + j
                    if has(b, 0, B - 1):
                        if j == 0:
                            pe.wait_ge(s_qs, b + 1)
                            pe.wait_ge(s_free, Ring(b).n)
                        if has(b, 1, B) or j >= 2:
                            pe.wait_ge(s_exp, g - 1)
                        for p in range(NPAIR):
                            last = nc.tensor.matmul(psS[0:KC, j % 2, p // 4, PW * (p % 4):PW * (p % 4) + PW],
                                                    kst[u][:, p, KC * j:KC * j + KC], qst[u][:, PW * p:PW * p + PW],
                                                    start=True, stop=True)
                        last.then_inc(s_S, 1)
                    for some in units[j][0:1]:
                        unit(*some)
                    if (j > 0 and has(b, 0, B - 1)) or (j == 0 and has(b, 1, B)):
                        jj, uu = (j - 1, u) if j else (NCH - 1, w)
                        pe.wait_ge(s_exp, g)
                        if jj == 0:
                            pe.wait_ge(s_Vc, 6 * (b + 1))
                            if has(b, 1, B):
                                pe.wait_ge(s_ou, b)
                        for G in range(NG):
                            r, s = G % 4, G // 4
                            last = nc.tensor.matmul(psO[32 * r:32 * r + 32, GW * s:GW * s + GW],
                                                    val[uu][:, jj, G, :], prob[jj % 2][:, GW * G:GW * G + GW],
                                                    start=(jj == 0 and s == 0), stop=(jj == NCH - 1),
                                                    skip_group_check=True)
                        last.then_inc(s_PV, 1)
                    for some in units[j][1:2]:
                        unit(*some)
                    m = j - VALUES
                    if 0 <= m < 6 and has(b, -1, B - 2):
                        if has(b, 0, B) or m:
                            pe.wait_ge(s_Vc, 6 * (b + 1) + m)
                        else:
                            pe.wait_ge(s_ctx[w], 16)
                        for r in range(2):
                            c0 = KC * (2 * m + r)
                            last = nc.tensor.matmul(psV[0:KC, 144 * r:144 * r + 144], ctxT[w][:, c0:c0 + KC], wvT[:],
                                                    start=True, stop=True)
                        last.then_inc(s_V, 1)
                    for some in units[j][2:]:
                        unit(*some)
            steps(pe, body)

        @block.scalar
        def _(act):
            act.wait_ge(s_set, 1)

            def body(k, u):
                b, w = 2 * k + u, 1 - u
                units = Ring(b).chunks(b)
                for j in range(NCH):
                    g = NCH * b + j
                    if has(b, 0, B - 1):
                        act.wait_ge(s_S, g + 1)
                        if has(b, 1, B) or j >= 2:
                            act.wait_ge(s_PV, g - 1)
                        nc.scalar.activation(prob[j % 2][:, 0:QW].rearrange("p (a q) -> p a q", a=2),
                                             psS[0:KC, j % 2, :, 0:QW // 2], ACT.Exp).then_inc(s_exp, 1)
                    for kind, idx, n, bank in units[j]:
                        if kind == "keys":
                            act.wait_ge(s_full, n + 1)
                            if has(b, -1, B):
                                act.wait_ge(s_kw[idx], 48 * (b + 2))
                            nc.scalar.activation(kparts[:, idx, 0, :], psR[bank][:, 0:KT], ACT.Identity,
                                                 bias=bk[:, 0:1]).then_inc(s_hi, 1)
                    m = j - VALUES
                    if 0 <= m < 6 and has(b, -1, B - 2):
                        act.wait_ge(s_V, 6 * (b + 1) + m + 1)
                        if m == 0 and has(b, 1, B):
                            act.wait_ge(s_PV, NCH * b)
                        dst = val[w][:, 2 * m:2 * m + 2, :, 0:24]
                        nc.scalar.copy(dst, psV[0:KC, 0:288].rearrange("p (r g e) -> p r g e", r=2, g=NG)
                                       ).then_inc(s_Vc, 1)
            steps(act, body)

        @block.vector
        def _(dve):
            v = nc.vector
            v.memset(psO[:], 1.0).then_inc(s_set, 1)

            def body(k, u):
                b, w = 2 * k + u, 1 - u
                units = Ring(b).chunks(b)
                for j in range(NCH):
                    if j == 0 and has(b, 1, B):
                        dve.wait_ge(s_PV, NCH * b)
                        v.tensor_copy(sums[:], psO[:, 0:2 * GW].rearrange("p (s r t) -> p s r t", s=2, r=3)
                                      ).then_inc(s_ou, 1)
                    if j == 1 and has(b, 1, B):
                        dve.wait_ge(s_ou, b)
                        v.tensor_scalar(mine[:], sums[:, :, 0, :], own[:, 0:1], None, ALU.mult).then_inc(s_do, 1)
                        for r in (1, 2):
                            dve.wait_ge(s_do, 3 * (b - 1) + r)
                            v.scalar_tensor_tensor(out=mine[:], in0=sums[:, :, r, :], scalar=own[:, r:r + 1],
                                                   in1=mine[:], op0=ALU.mult, op1=ALU.add).then_inc(s_do, 1)
                    for kind, idx, n, bank in units[j]:
                        R = psR[bank]
                        if kind == "keys":
                            dve.wait_ge(s_hi, 3 * (b + 2) + idx + 1)
                            if has(b, -1, B):
                                dve.wait_ge(s_kp, 3 * (b + 1) + idx + 1)
                            v.scalar_tensor_tensor(out=krest[:, idx, :], in0=R[:, 0:KT], scalar=bk[:, 0:1],
                                                   in1=kparts[:, idx, 0, :], op0=ALU.add, op1=ALU.subtract
                                                   ).then_inc(s_free, 1)
                            continue
                        dve.wait_ge(s_full, n + 1)
                        if kind == "max":
                            i, p = idx // NPAIR, idx % NPAIR
                            v.reduce_max(mx[:, i, p:p + 1], R[0:PW, 0:KT], axis=AX_X).then_inc(s_free, 1)
                        elif kind == "sums":
                            v.reciprocal(recip[:], R[:, 0:2 * T].rearrange("p (s t) -> p s t", s=2)
                                         ).then_inc(s_free, 1)
                            dve.wait_ge(s_free, n + 1)
                            dve.wait_ge(s_do, 3 * b)
                            v.tensor_tensor(attn[:], mine[:], recip[:], ALU.mult).then_inc(s_on, 1)
                        elif kind == "out":
                            t = k - 1 if u == 0 else k
                            rows = slice(64 * w, 64 * w + T)
                            xt = x[rows, bass.ds(t, 1), :] if not isinstance(t, int) else x[rows, t:t + 1, :]
                            v.scalar_tensor_tensor(out=xt, in0=R[rows, 0:C].unsqueeze(1), scalar=tanh_g[rows, :],
                                                   in1=xt, op0=ALU.mult, op1=ALU.add).then_inc(s_free, 1)
                        else:
                            rows = R[SR:SR + MR, 0:PW].unsqueeze(1).broadcast_to([MR, NPAIR, PW])
                            v.tensor_tensor(qst[w][SR:SR + MR, :].rearrange("q (p t) -> q p t", p=NPAIR), rows,
                                            own_pair[SR:SR + MR, :].rearrange("q (p t) -> q p t", p=NPAIR),
                                            ALU.mult).then_inc(s_free, 1)
                        if kind == "max" and idx == 3 * NPAIR - 1:
                            dve.wait_ge(s_free, n + 1)
                            at = 4 * (b + 1)
                            v.tensor_reduce(nmx[:], mx[:].rearrange("q i p -> q p i"), axis=AX_X, op=ALU.max,
                                            negate=True).then_inc(s_dm, 1)
                            dve.wait_ge(s_dm, at + 1)
                            v.tensor_copy(mparts[:, 0, :], nmx[:]).then_inc(s_dm, 1)
                            dve.wait_ge(s_dm, at + 2)
                            v.tensor_tensor(mrest[:], nmx[:], mparts[:, 0, :], ALU.subtract).then_inc(s_dm, 1)
                            dve.wait_ge(s_dm, at + 3)
                            v.tensor_copy(mparts[:, 1, :], mrest[:]).then_inc(s_dm, 1)
                            dve.wait_ge(s_dm, at + 4)
                            v.tensor_tensor(mparts[:, 2, :], mrest[:], mparts[:, 1, :], ALU.subtract
                                            ).then_inc(s_mp, 1)
                    if j == 6 and has(b, -1, B - 2):
                        if has(b, 1, B):
                            dve.wait_ge(s_S, NCH * b)
                        dve.wait_ge(s_qm, b + 2)
                        v.tensor_copy(qst[w][0:SR, :], qmx[w][:]).then_inc(s_qs, 1)
            steps(dve, body)

        @block.gpsimd
        def _(pool):
            def body(k, u):
                b, w = 2 * k + u, 1 - u
                if not has(b, -2, B - 3):
                    return
                for units in Ring(b).chunks(b):
                    for kind, idx, n, bank in units:
                        if kind == "keys":
                            pool.wait_ge(s_free, n + 1)
                            if has(b, -1, B):
                                pool.wait_ge(s_kw[idx], 48 * (b + 2))
                            nc.gpsimd.tensor_tensor(kparts[:, idx, 1, :], krest[:, idx, :], zeros[:], ALU.add
                                                    ).then_inc(s_pool, 1)
                            pool.wait_ge(s_pool, 3 * (b + 2) + idx + 1)
                            nc.gpsimd.tensor_tensor(kparts[:, idx, 2, :], krest[:, idx, :], kparts[:, idx, 1, :],
                                                    ALU.subtract).then_inc(s_kp, 1)
                pool.wait_ge(s_ql[u], 32 * (k + 2))
                if has(b, 0, B):
                    pool.wait_ge(s_S, NCH * b + 1)
                    pool.wait_ge(s_qs, b + 1)
                nc.gpsimd.tensor_tensor(qmx[u][:], qraw[u][:].rearrange("q p r t -> q (p r t)"), qmask[:], ALU.mult
                                        ).then_inc(s_qm, 1)
            steps(pool, body)


def gated_experts(nc, x, xn, xnT, ident, tanh_g, d):
    with ExitStack() as ctx:
        sp = Space(nc, ctx, "ge")
        slots = nc.dram_tensor("slots1", (SLOTS, C), F32, kind="Internal").ap()
        results = nc.dram_tensor("results1", (SLOTS, C), F32, kind="Internal").ap()
        index = [sp.sb(f"index{k}", [P, NT], U32) for k in range(2)]
        weight = [sp.sb(f"weight{k}", [P, NT]) for k in range(2)]
        tile_expert = sp.sb("tile_expert", [P, NTILE], U32)
        scale = sp.sb("scale", [P, 1])
        guT = sp.sb("guT", [P, E1 * 2 * HID])
        downT = sp.sb("downT", [P, E1 * 3 * C])
        s_wt = sp.sem("wt")

        with ExitStack() as inner:
            n = Space(nc, inner, "rms")
            normT = n.sb("normT", [P, NT * P])
            zeros = n.sb("zeros", [P, SLOTS // P, C])
            ss, sd, rs = (n.sb(k, [P, NT]) for k in ("ss", "sd", "rs"))
            wrow, alpha, sq = n.sb("wrow", [P, C]), n.sb("alpha", [P, 1]), n.sb("sq", [P, C])
            xr = n.sb("xr", [P, NT, C])
            psT = n.ps("psT", [P, 2, 512])
            s_w, s_ss, s_v, s_sd, s_x, s_T, s_Tc, s_dve, s_act = (
                n.sem(k) for k in ("w", "ss", "v", "sd", "x", "T", "Tc", "dve", "act"))
            with nc.Block() as block:
                @block.sync
                def _(sync):
                    sync.dma_start(wrow[:], d["L1_norm_weight"]).then_inc(s_w, 16)
                    sync.dma_start(alpha[:], d["L1_alpha"]).then_inc(s_w, 16)
                    sync.dma_start(guT[:].rearrange("c (e h) -> c e h", e=E1),
                                   d["L1_guT"].rearrange("e c h -> c e h")).then_inc(s_wt, 16)
                    sync.dma_start(downT[:], d["L1_downT"]).then_inc(s_wt, 16)
                    sync.wait_ge(s_wt, 32)

                @block.scalar
                def _(act):
                    for t in range(NT):
                        if t:
                            act.wait_ge(s_act, t)
                        nc.scalar.activation(sq[:], xn[:, t, :], ACT.Square, accum_out=ss[:, t:t + 1]
                                             ).then_inc(s_act, 1)
                    act.wait_ge(s_v, 1)
                    nc.scalar.activation(sd[:], sd[:], ACT.Sqrt).then_inc(s_sd, 1)
                    for q in range(NT // 4):
                        act.wait_ge(s_T, q + 1)
                        nc.scalar.copy(normT[:, 512 * q:512 * q + 512], psT[:, q % 2, :]).then_inc(s_Tc, 1)

                @block.vector
                def _(dve):
                    v = nc.vector
                    step = Steps(dve, s_dve)
                    dve.wait_ge(s_w, 32)
                    step.then(v.tensor_scalar(alpha[:], alpha[:], -0.5, 2.0, ALU.max, ALU.min))
                    step(v.tensor_scalar(scale[:], alpha[:], tanh_g, None, ALU.mult))
                    dve.wait_ge(s_act, NT)
                    v.tensor_scalar(sd[:], ss[:], 1.0 / C, RMS_EPS, ALU.mult, ALU.add).then_inc(s_v, 1)
                    dve.wait_ge(s_sd, 1)
                    step.then(v.reciprocal(rs[:], sd[:]))
                    for t in range(NT):
                        v.scalar_tensor_tensor(out=xr[:, t, :], in0=xn[:, t, :], scalar=rs[:, t:t + 1], in1=wrow[:],
                                               op0=ALU.mult, op1=ALU.mult).then_inc(s_x, 1)
                    for t in range(NT):
                        step(v.scalar_tensor_tensor(out=x[:, t, :], in0=xn[:, t, :], scalar=tanh_g, in1=x[:, t, :],
                                                    op0=ALU.mult, op1=ALU.add))

                @block.tensor
                def _(pe):
                    for q in range(NT // 4):
                        if q >= 2:
                            pe.wait_ge(s_Tc, q - 1)
                        pe.wait_ge(s_x, 4 * q + 4)
                        for r in range(4):
                            last = nc.tensor.transpose(psT[:, q % 2, P * r:P * r + P], xr[:, 4 * q + r, :], ident[:])
                        last.then_inc(s_T, 1)
            route(nc, "r1", xr, normT, E1, "L1_router_wT", None, scale[:, 0:1], index, weight, slots, zeros, d,
                  tile_expert)

        with ExitStack() as inner:
            f = Space(nc, inner, "gf")
            rows = [f.sb(f"rows{u}", [P, C]) for u in range(2)]
            tokT, hid = [f.sb(f"tokT{u}", [P, P]) for u in range(2)], [f.sb(f"hid{u}", [P, HID]) for u in range(2)]
            act_g = [f.sb(f"act_g{u}", [P, HID]) for u in range(2)]
            hidT = [f.sb(f"hidT{u}", [P, 3, P]) for u in range(2)]
            res = [f.sb(f"res{u}", [P, C]) for u in range(2)]
            got = [f.sb(f"got{q}", [P, C]) for q in range(4)]
            psX, psG, psU = f.ps("psX", [P, 512]), f.ps("psG", [P, 2, 512]), f.ps("psU", [P, 2, 512])
            psH, psY = f.ps("psH", [P, 512]), f.ps("psY", [P, 512])
            s_rows = [f.sem(f"rows{u}") for u in range(2)]
            s_X, s_x, s_G, s_U, s_g, s_h, s_H, s_Hc, s_Y, s_y, s_gz = (
                f.sem(k) for k in ("X", "x", "G", "U", "g", "h", "H", "Hc", "Y", "y", "gz"))
            s_res = [f.sem(f"res{u}") for u in range(2)]
            s_got, s_used = [f.sem(f"got{q}") for q in range(4)], [f.sem(f"used{q}") for q in range(4)]
            block = inner.enter_context(nc.Block())

            def turns(engine, body):
                body(0, 0, True, False)
                body(0, 1, False, False)
                with engine.Fori(1, NTILE // 2 - 1) as i:
                    for u in range(2):
                        body(i, u, False, False)
                for u in range(2):
                    body(NTILE // 2 - 1, u, False, False)
                body(NTILE // 2, 0, False, True)

            @block.sync
            def _(sync):
                def load(i, u, reuse):
                    n = 2 * i + u
                    if reuse:
                        sync.wait_ge(s_X, n - 1)
                    sync.dma_start(rows[u][:].unsqueeze(1), slots.rearrange("(i p) c -> p i c", p=P)[:, bass.ds(n, 1), :]
                                   ).then_inc(s_rows[u], 16)
                for n in range(4):
                    load(n // 2, n % 2, n >= 2)

                def body(i, u, ahead):
                    n = 2 * i + u
                    if ahead:
                        load(i + 2, u, True)
                    sync.wait_ge(s_y, n + 1)
                    sync.dma_start(results.rearrange("(i p) c -> p i c", p=P)[:, bass.ds(n, 1), :],
                                   res[u][:].unsqueeze(1)).then_inc(s_res[u], 16)
                with sync.Fori(0, NTILE // 2 - 2) as i:
                    for u in range(2):
                        body(i, u, True)
                for n in range(NTILE - 5, NTILE):
                    body(n // 2, n % 2, n + 4 < NTILE)
                for u in range(2):
                    sync.wait_ge(s_res[u], 16 * ((NTILE + 1 - u) // 2))

            @block.tensor
            def _(pe):
                def expert(n):
                    return pe.value_load(tile_expert[0:1, bass.ds(n, 1)], min_val=0, max_val=E1 - 1)

                def take(i, u):
                    n = 2 * i + u
                    pe.wait_ge(s_rows[u], 16 * i + 16)
                    if not (isinstance(n, int) and n == 0):
                        pe.wait_ge(s_x, n)
                    nc.tensor.transpose(psX[:, 0:P], rows[u][:], ident[:]).then_inc(s_X, 1)

                def up(i, u):
                    n = 2 * i + u
                    e = expert(n)
                    pe.wait_ge(s_x, n + 1)
                    if not (isinstance(n, int) and n < 2):
                        pe.wait_ge(s_h, n - 1)
                    nc.tensor.matmul(psG[:, u, 0:HID], tokT[u][:], guT[:, bass.ds(e * (2 * HID), HID)],
                                     start=True, stop=True).then_inc(s_G, 1)
                    nc.tensor.matmul(psU[:, u, 0:HID], tokT[u][:], guT[:, bass.ds(e * (2 * HID) + HID, HID)],
                                     start=True, stop=True).then_inc(s_U, 1)

                def body(i, u, first, last):
                    n = 2 * i + u
                    if first:
                        take(0, 0)
                        take(0, 1)
                        up(0, 0)
                    if not (isinstance(n, int) and n + 2 >= NTILE):
                        take(i + 1, u)
                    pe.wait_ge(s_h, n + 1)
                    if not first:
                        pe.wait_ge(s_Hc, n)
                    for q, (c0, w) in enumerate(HCH):
                        t = nc.tensor.transpose(psH[0:w, P * q:P * q + P], hid[u][:, c0:c0 + w], ident[:])
                    t.then_inc(s_H, 1)
                    if not last:
                        up(i + u, 1 - u)
                    e = expert(n)
                    pe.wait_ge(s_Hc, n + 1)
                    if not first:
                        pe.wait_ge(s_y, n)
                    for q, (c0, w) in enumerate(HCH):
                        t = nc.tensor.matmul(psY[:, 0:C], hidT[u][0:w, q, :], downT[0:w, bass.ds(e * (3 * C) + C * q, C)],
                                             start=(q == 0), stop=(q == 2))
                    t.then_inc(s_Y, 1)
                turns(pe, body)

            @block.scalar
            def _(act):
                def silu(i, u):
                    n = 2 * i + u
                    act.wait_ge(s_G, n + 1)
                    if not (isinstance(n, int) and n < 2):
                        act.wait_ge(s_h, n - 1)
                    nc.scalar.activation(act_g[u][:], psG[:, u, 0:HID], ACT.Silu).then_inc(s_g, 1)

                def body(i, u, first, last):
                    n = 2 * i + u
                    if first:
                        silu(i, u)
                    act.wait_ge(s_H, n + 1)
                    nc.scalar.copy(hidT[u][:, 0:2, :], psH[:, 0:2 * P].rearrange("p (q s) -> p q s", q=2))
                    nc.scalar.copy(hidT[u][0:HCH[2][1], 2, :], psH[0:HCH[2][1], 2 * P:3 * P]).then_inc(s_Hc, 1)
                    if not last:
                        silu(i + u, 1 - u)
                turns(act, body)

            @block.vector
            def _(dve):
                v = nc.vector
                for q in range(4):
                    t = v.memset(got[q][:], 0.0)
                t.then_inc(s_gz, 1)

                def tokens(i, u):
                    dve.wait_ge(s_X, 2 * i + u + 1)
                    v.tensor_copy(tokT[u][:], psX[:, 0:P]).then_inc(s_x, 1)

                def product(i, u):
                    n = 2 * i + u
                    dve.wait_ge(s_g, n + 1)
                    dve.wait_ge(s_U, n + 1)
                    v.tensor_tensor(hid[u][:], psU[:, u, 0:HID], act_g[u][:], ALU.mult).then_inc(s_h, 1)

                def body(i, u, first, last):
                    n = 2 * i + u
                    if first:
                        tokens(0, 0)
                        tokens(0, 1)
                        product(0, 0)
                    if not (isinstance(n, int) and n + 2 >= NTILE):
                        tokens(i + 1, u)
                    if not last:
                        product(i + u, 1 - u)
                    dve.wait_ge(s_Y, n + 1)
                    if not (isinstance(n, int) and n < 2):
                        dve.wait_ge(s_res[u], 16 * i)
                    v.tensor_copy(res[u][:], psY[:, 0:C]).then_inc(s_y, 1)
                turns(dve, body)
                gather_results(nc, dve, None, x, results, index, weight, got, s_got, s_used)

            @block.gpsimd
            def _(pool):
                pool.wait_ge(s_gz, 1)
                for u in range(2):
                    pool.wait_ge(s_res[u], 16 * ((NTILE + 1 - u) // 2))
                gather_results(nc, None, pool, x, results, index, weight, got, s_got, s_used)


def build(nc, d, out, phases=4, first=0):
    with ExitStack() as ctx:
        sp = Space(nc, ctx, "all")
        x = sp.sb("x", [P, NT, C])
        ident = sp.sb("ident", [P, P])
        identb = sp.sb("identb", [P, P], BF16)
        rowmask = sp.sb("rowmask", [P, 1])
        gates = sp.sb("gates", [P, 4])
        tg = sp.sb("tg", [P, 4])
        s_zero, s_in, s_tg, s_out = (sp.sem(n) for n in ("zero", "in", "tg", "out"))

        with nc.Block() as block:
            @block.vector
            def _(dve):
                nc.vector.memset(x[:], 0.0).then_inc(s_zero, 1)
                dve.wait_ge(s_in, 16 * 6)
                nc.vector.tensor_copy(identb[:], ident[:]).then_inc(s_zero, 1)

            @block.sync
            def _(sync):
                sync.dma_start(gates[:, 0:2], d["g_xattn"]).then_inc(s_in, 16)
                sync.dma_start(gates[:, 2:4], d["g_ffn"]).then_inc(s_in, 16)
                sync.dma_start(ident[:], d["ident"]).then_inc(s_in, 16)
                sync.dma_start(rowmask[:], d["rowmask"]).then_inc(s_in, 16)
                sync.wait_ge(s_zero, 1)
                tiles = d["x"].rearrange("(t b) s c -> b s t c", b=2)
                for b, (lo, _) in enumerate(HALVES):
                    sync.dma_start(x[lo:lo + T, :, :], tiles[b]).then_inc(s_in, 16)

            @block.scalar
            def _(act):
                act.wait_ge(s_in, 16 * 6)
                nc.scalar.activation(tg[:], gates[:], ACT.Tanh).then_inc(s_tg, 1)

        if phases > 0 and first <= 0:
            with nc.sbuf_tensor("xnT0", [P, NT * P], F32) as xnT:
                with nc.sbuf_tensor("xn0", [P, NT, C], F32) as xn:
                    layer_norm(nc, "n0", x, xn, xnT, ident)
                vision_language_attention(nc, x, xnT, ident, tg[:, 0:1], rowmask[:, 0:1], d)
        if phases > 1 and first <= 1:
            with nc.sbuf_tensor("xnT1", [P, NT * P], F32) as xnT, nc.sbuf_tensor("xn1", [P, NT, C], F32) as xn:
                layer_norm(nc, "n1", x, xn, xnT, ident)
                capacity_experts(nc, x, xn, xnT, ident, tg[:, 2:3], d)
        if phases > 2 and first <= 2:
            with nc.sbuf_tensor("xnT2", [P, NT * P], F32) as xnT:
                with nc.sbuf_tensor("xn2", [P, NT, C], F32) as xn:
                    layer_norm(nc, "n2", x, xn, xnT, ident)
                attention(nc, x, xnT, tg[:, 1:2], identb, d)
        if phases > 3:
            with nc.sbuf_tensor("xnT3", [P, NT * P], F32) as xnT, nc.sbuf_tensor("xn3", [P, NT, C], F32) as xn:
                layer_norm(nc, "n3", x, xn, xnT, ident)
                gated_experts(nc, x, xn, xnT, ident, tg[:, 3:4], d)

        with nc.Block() as block:
            @block.sync
            def _(sync):
                tiles = out.rearrange("(t b) s c -> b s t c", b=2)
                for b, (lo, _) in enumerate(HALVES):
                    sync.dma_start(tiles[b], x[lo:lo + T, :, :]).then_inc(s_out, 16)
                sync.wait_ge(s_out, 32)


def layouts(inputs):
    def col(a):
        return np.ascontiguousarray(a.reshape(-1, 1))

    def rows(a, n=P):
        return np.ascontiguousarray(np.broadcast_to(a.reshape(1, -1), (n, a.size)))

    i = {k: np.asarray(v) for k, v in inputs.items()}
    a = {"x": i["x"], "ctx": i["ctx_1024"], "ctxT": np.ascontiguousarray(i["ctx_1024"].transpose(0, 2, 1)),
         "g_xattn": rows(i["g_xattn"]), "g_ffn": rows(i["g_ffn"])}
    a["L0_W_vkT"] = np.ascontiguousarray(i["L0_xattn_W_vk"].T)
    a["L0_W_lk"] = i["L0_xattn_W_lk"]
    a["L0_W_vvT"] = np.ascontiguousarray(i["L0_xattn_W_vv"].T)
    a["L0_W_lvT"] = np.ascontiguousarray(i["L0_xattn_W_lv"].T)
    a["L0_b_vk"], a["L0_b_lk"] = col(i["L0_xattn_b_vk"]), col(i["L0_xattn_b_lk"])
    a["L0_b_vv"], a["L0_b_lv"] = rows(i["L0_xattn_b_vv"]), rows(i["L0_xattn_b_lv"])
    a["L0_router_wT"] = np.ascontiguousarray(i["L0_ffn_router_w"].T)
    a["L0_router_b"] = rows(np.tile(i["L0_ffn_router_b"], NT)).reshape(P, NT, E0)
    a["L0_w1"], a["L0_w2"] = i["L0_ffn_w1"], i["L0_ffn_w2"]
    a["L0_b1"] = np.ascontiguousarray(i["L0_ffn_b1"].reshape(E0, FC0, P).transpose(2, 0, 1))
    a["L0_b2"] = np.ascontiguousarray(i["L0_ffn_b2"].T)
    a["L1_W_qT"], a["L1_W_kT"] = (np.ascontiguousarray(i[f"L1_xattn_W{k}"].T) for k in "qk")
    a["L1_b_q"], a["L1_b_k"] = col(i["L1_xattn_bq"]), col(i["L1_xattn_bk"])
    a["L1_b_v"] = np.ascontiguousarray(np.broadcast_to(i["L1_xattn_bv"].reshape(-1, 1), (P, P)))
    a["L1_b_o"] = rows(i["L1_xattn_bo"])
    a["L1_W_vT"] = np.ascontiguousarray(np.concatenate([i["L1_xattn_Wv"].T, np.zeros((C, 16), np.float32)], 1))
    woT = np.ascontiguousarray(i["L1_xattn_Wo"].T)
    a["L1_W_oT_plain"] = woT
    placed = np.zeros((P, 2, C), np.float32)
    for h in range(H):
        s, j, r = h // 12, h // 3 % 4, h % 3
        placed[32 * j + 8 * r:32 * j + 8 * r + HD, s] = woT[HD * h:HD * h + HD]
    a["L1_W_oT"] = placed
    own, sel = np.zeros((P, 3), np.float32), np.zeros((P, 3, P), np.float32)
    for j in range(4):
        for r in range(3):
            own[32 * j + 8 * r:32 * j + 8 * r + 8, r] = 1
            sel[32 * j + 24, r, 32 * j + 8 * r:32 * j + 8 * r + 8] = 1
        sel[32 * j + 24, 0, 32 * j + 24:32 * j + 32] = 1
    a["pair_rows"] = np.zeros((P, NPAIR, 2 * T), np.float32)
    for row in range(3 * NPAIR):
        a["pair_rows"][96 + row, row % NPAIR] = 1
    a["pair_rows"] = a["pair_rows"].reshape(P, -1)
    a["own_rows"], a["sum_rows"] = own, sel
    pair = np.zeros((6, 2, HD, NPAIR, 2, T), np.float32)
    for r in range(2):
        pair[:, r, :, :, r, :] = 1
    a["pair_mask"] = pair.reshape(6 * 2 * HD, -1)
    a["L1_norm_weight"] = rows(i["L1_ffn_norm_weight"])
    a["L1_alpha"] = rows(i["L1_ffn_residual_alpha"])
    a["L1_router_wT"] = np.ascontiguousarray(i["L1_ffn_router_weight"].T)
    a["L1_guT"] = np.ascontiguousarray(i["L1_ffn_gate_up_weight"].transpose(0, 2, 1))
    down = np.zeros((P, E1, 3, C), np.float32)
    for q, (c0, w) in enumerate(HCH):
        down[:w, :, q] = i["L1_ffn_down_weight"][:, :, c0:c0 + w].transpose(2, 0, 1)
    a["L1_downT"] = down.reshape(P, -1)
    a["tile_ids"] = rows(np.repeat(np.arange(NTILE, dtype=np.float32), E1)).reshape(P, NTILE, E1)
    for e in (E0, E1):
        a[f"expert_ids{e}"] = rows(np.tile(np.arange(e, dtype=np.float32), NT)).reshape(P, NT, e)
    a["before"] = np.triu(np.ones((P, P), np.float32), 1)
    a["ones"] = np.ones((P, P), np.float32)
    a["ident"] = np.eye(P, dtype=np.float32)
    a["rowmask"] = np.array([[float(p % TP < T)] for p in range(P)], np.float32)
    return a


def kernel(**inputs):
    import concourse.bacc as bacc
    from concourse.bass_utils import run_bass_kernel_spmd

    nc = bacc.Bacc("TRN2", target_bir_lowering=False, num_devices=1)
    arrays = {f"in_{k}": v for k, v in layouts(inputs).items()}
    d = {k[3:]: nc.dram_tensor(k, v.shape, mybir.dt.from_np(v.dtype), kind="ExternalInput").ap()
         for k, v in arrays.items()}
    out = nc.dram_tensor("out", (B, T, C), F32, kind="ExternalOutput").ap()
    build(nc, d, out)
    return run_bass_kernel_spmd(nc, [arrays], core_ids=[0]).results[0]["out"]
```

```python
from contextlib import ExitStack

import numpy as np
import concourse.bass as bass
from concourse import mybir

ALU = mybir.AluOpType
ACT = mybir.ActivationFunctionType
F32 = mybir.dt.float32
BF16 = mybir.dt.bfloat16
U32 = mybir.dt.uint32
AX_X = mybir.AxisListType.X

P = 128
B, T, C, S = 32, 56, 128, 1500
TP = 64
NT = B // 2
KC, NCH = 125, 12
KT, NTH = 500, 3
HALVES = ((0, 64), (64, 128))

E0, FF0, CAP = 16, 512, 280
SLOTS = E0 * CAP
FC0 = FF0 // P
NTILE = (2 * B * T + 8 * (P - 1)) // P
H, HD = 16, 8
NPAIR = H // 2
NG = 6
GW = 3 * T
E1, HID = 8, 352
HCH = ((0, 128), (128, 128), (256, 96))
TG = 8 * T

LN_EPS, RMS_EPS = 1e-5, 1e-6


class Steps:

    def __init__(self, engine, sem, base=0):
        self.engine, self.sem, self.base, self.n = engine, sem, base, 0

    def __call__(self, instruction):
        self.n += 1
        instruction.then_inc(self.sem, 1)

    def wait(self):
        self.engine.wait_ge(self.sem, self.base + self.n)

    def then(self, instruction):
        self(instruction)
        self.wait()


class Space:

    def __init__(self, nc, ctx, phase):
        self.nc, self.ctx, self.phase = nc, ctx, phase
        self.sems = []
        ctx.callback(self.close)

    def close(self):
        if self.sems:
            self.nc.clear_and_free_semaphores(self.sems)
            self.nc.all_engine_barrier()

    def sb(self, name, shape, dt=F32):
        return self.ctx.enter_context(self.nc.sbuf_tensor(f"{self.phase}_{name}", shape, dt))

    def ps(self, name, shape, dt=F32):
        return self.ctx.enter_context(self.nc.psum_tensor(f"{self.phase}_{name}", shape, dt))

    def sem(self, name):
        self.sems.append(self.nc.alloc_semaphore(f"{self.phase}_{name}"))
        return self.sems[-1]


def layer_norm(nc, phase, x, xn, xnT, ident):
    with ExitStack() as ctx:
        sp = Space(nc, ctx, phase)
        stats = sp.sb("stats", [P, NT, 6])
        mv = sp.sb("mv", [P, NT, 2])
        sd = sp.sb("sd", [P, NT])
        rs = sp.sb("rs", [P, NT])
        psT = sp.ps("psT", [P, 2, 512])
        s_dve, s_var, s_sd, s_xn, s_T, s_cp = (sp.sem(n) for n in ("dve", "var", "sd", "xn", "T", "cp"))
        block = ctx.enter_context(nc.Block())

        @block.vector
        def _(dve):
            step = Steps(dve, s_dve)
            for t in range(NT):
                step(nc.vector.bn_stats(stats[:, t, :], x[:, t, :]))
            step.wait()
            for t in range(NT):
                step(nc.vector.bn_aggr(mv[:, t, :], stats[:, t, :]))
            step.wait()
            nc.vector.tensor_scalar(sd[:], mv[:, :, 1], 1.0, LN_EPS, ALU.mult, ALU.add).then_inc(s_var, 1)
            dve.wait_ge(s_sd, 1)
            step.then(nc.vector.reciprocal(rs[:], sd[:]))
            for t in range(NT):
                nc.vector.tensor_scalar(xn[:, t, :], x[:, t, :], mv[:, t, 0:1], rs[:, t:t + 1],
                                        ALU.subtract, ALU.mult).then_inc(s_xn, 1)

        @block.scalar
        def _(act):
            act.wait_ge(s_var, 1)
            nc.scalar.activation(sd[:], sd[:], ACT.Sqrt).then_inc(s_sd, 1)
            for q in range(NT // 4):
                act.wait_ge(s_T, q + 1)
                nc.scalar.copy(xnT[:, 512 * q:512 * q + 512], psT[:, q % 2, :]).then_inc(s_cp, 1)

        @block.tensor
        def _(pe):
            for q in range(NT // 4):
                if q >= 2:
                    pe.wait_ge(s_cp, q - 1)
                pe.wait_ge(s_xn, 4 * q + 4)
                for r in range(4):
                    last = nc.tensor.transpose(psT[:, q % 2, P * r:P * r + P], xn[:, 4 * q + r, :], ident[:])
                last.then_inc(s_T, 1)


def vision_language_attention(nc, x, xnT, ident, tanh_g, rowmask, d):
    with ExitStack() as ctx:
        sp = Space(nc, ctx, "va")
        wvkT, wlk, wvvT, wlvT = (sp.sb(n, [P, C]) for n in ("wvkT", "wlk", "wvvT", "wlvT"))
        bvk, blk = (sp.sb(n, [P, 1]) for n in ("bvk", "blk"))
        bvv, blv = (sp.sb(n, [P, C]) for n in ("bvv", "blv"))
        vkT = sp.sb("vkT", [P, NT * P])
        qT = sp.sb("qT", [P, NT * P])
        vis = sp.sb("vis", [P, NT, C])
        cb = sp.sb("cb", [P, NT])
        ctxT = [sp.sb(f"ctxT{u}", [P, 2, S]) for u in range(2)]
        side = [sp.sb(f"side{u}", [KC, 2, NCH, C + TP]) for u in range(2)]
        q_now = [sp.sb(f"q_now{u}", [P, P]) for u in range(2)]
        prob = [sp.sb(f"prob{u}", [P, S]) for u in range(2)]
        rsum = [sp.sb(f"rsum{u}", [P, 1]) for u in range(2)]
        nmax, nb0, nb1 = (sp.sb(n, [P, 1]) for n in ("nmax", "nb0", "nb1"))
        rinv, rmask = (sp.sb(n, [P, 1]) for n in ("rinv", "rmask"))
        rtg = [sp.sb(f"rtg{u}", [P, 1]) for u in range(2)]
        ac, acT, gbd = (sp.sb(n, [P, P]) for n in ("ac", "acT", "gbd"))

        psS = sp.ps("psS", [P, NTH, 512])
        psT = [sp.ps(f"psT{r}", [P, 512]) for r in range(2)]
        psA = sp.ps("psA", [P, 512])
        psM = sp.ps("psM", [P, 512])
        psV = sp.ps("psV", [P, 512])

        s_w, s_cT, s_cN = sp.sem("w"), [sp.sem(f"cT{u}") for u in range(2)], [sp.sem(f"cN{u}") for u in range(2)]
        s_vk, s_vkc, s_q, s_qc, s_v, s_vc, s_cb, s_cbc = (
            sp.sem(n) for n in ("vk", "vkc", "q", "qc", "v", "vc", "cb", "cbc"))
        s_xb, s_gz = sp.sem("xb"), sp.sem("gz")
        s_now, s_sc, s_nb, s_ex, s_T, s_Tc, s_A, s_ac, s_gb, s_aT, s_aTc, s_o, s_x = (
            sp.sem(n) for n in ("now", "sc", "nb", "ex", "T", "Tc", "A", "ac", "gb", "aT", "aTc", "o", "x"))
        s_dve = sp.sem("dve")
        SCALE = float(C) ** -0.5
        TURNS = NT // 2

        block = nc.Block()
        with block:
            @block.sync
            def _(sync):
                for dst, src in ((wvkT, "L0_W_vkT"), (wlk, "L0_W_lk"), (wvvT, "L0_W_vvT"), (wlvT, "L0_W_lvT"),
                                 (bvk, "L0_b_vk"), (blk, "L0_b_lk"), (bvv, "L0_b_vv"), (blv, "L0_b_lv")):
                    sync.dma_start(dst[:], d[src]).then_inc(s_w, 16)

            @block.tensor
            def _(pe):
                pe.wait_ge(s_w, 128)
                for q in range(4):
                    if q:
                        pe.wait_ge(s_vkc, q)
                    nc.tensor.matmul(psS[:, 0, :], wvkT[:], xnT[:, 512 * q:512 * q + 512],
                                     start=True, stop=True).then_inc(s_vk, 1)
                for q in range(4):
                    pe.wait_ge(s_vkc, q + 1)
                    if q:
                        pe.wait_ge(s_qc, q)
                    nc.tensor.matmul(psS[:, 1, :], wlk[:], vkT[:, 512 * q:512 * q + 512],
                                     start=True, stop=True).then_inc(s_q, 1)
                for t in range(NT):
                    last = nc.tensor.matmul(psM[:, t:t + 1], vkT[:, P * t:P * t + P], blk[:], start=True, stop=True)
                last.then_inc(s_cb, 1)
                for t in range(NT):
                    if t >= 2:
                        pe.wait_ge(s_vc, t - 1)
                    nc.tensor.matmul(psT[t % 2][:, 0:C], xnT[:, P * t:P * t + P], wvvT[:],
                                     start=True, stop=True).then_inc(s_v, 1)

            @block.scalar
            def _(act):
                act.wait_ge(s_w, 128)
                for q in range(4):
                    act.wait_ge(s_vk, q + 1)
                    nc.scalar.activation(vkT[:, 512 * q:512 * q + 512], psS[:, 0, :], ACT.Identity,
                                         bias=bvk[:, 0:1]).then_inc(s_vkc, 1)
                for q in range(4):
                    act.wait_ge(s_q, q + 1)
                    nc.scalar.mul(qT[:, 512 * q:512 * q + 512], psS[:, 1, :], SCALE).then_inc(s_qc, 1)
                act.wait_ge(s_cb, 1)
                nc.scalar.mul(cb[:], psM[:, 0:NT], SCALE).then_inc(s_cbc, 1)

            @block.vector
            def _(dve):
                step = Steps(dve, s_dve)
                nc.vector.memset(gbd[:], 0.0).then_inc(s_gz, 1)
                dve.wait_ge(s_w, 128)
                step.then(nc.vector.tensor_scalar(ac[:], blv[:], tanh_g, None, ALU.mult))
                for t in range(NT):
                    nc.vector.tensor_tensor(x[:, t, :], x[:, t, :], ac[:], ALU.add).then_inc(s_xb, 1)
                for t in range(NT):
                    dve.wait_ge(s_v, t + 1)
                    nc.vector.tensor_tensor(vis[:, t, :], psT[t % 2][:, 0:C], bvv[:], ALU.add).then_inc(s_vc, 1)

        block = nc.Block()
        with block:
            @block.sync
            def _(sync):
                def load(i, u, first):
                    tile = 2 * i + u
                    if not first:
                        sync.wait_ge(s_sc, 2 * i + u - 1)
                    sync.dma_start(ctxT[u][:], d["ctxT"][bass.ds(2 * tile, 2)].rearrange("b c s -> c b s")
                                   ).then_inc(s_cT[u], 16)
                    if not first:
                        sync.wait_ge(s_A, 2 * i + u - 1)
                    for b in range(2):
                        sync.dma_start(side[u][:, b, :, 0:C],
                                       d["ctx"][bass.ds(2 * tile + b, 1)].rearrange("o (j k) c -> k (o j) c", k=KC)
                                       ).then_inc(s_cN[u], 16)
                for u in range(2):
                    load(0, u, True)
                with sync.Fori(1, TURNS) as i:
                    for u in range(2):
                        load(i, u, False)

            def turns(engine, body):
                for u in range(2):
                    body(0, u, u == 0, False)
                with engine.Fori(1, TURNS - 1) as i:
                    for u in range(2):
                        body(i, u, False, False)
                for u in range(2):
                    body(TURNS - 1, u, False, u == 1)

            @block.tensor
            def _(pe):
                def scores(i, u):
                    n = 2 * i + u
                    pe.wait_ge(s_cT[u], 16 * i + 16)
                    pe.wait_ge(s_now, n + 1)
                    for th in range(NTH):
                        for b, (lo, hi) in enumerate(HALVES):
                            last = nc.tensor.matmul(psS[lo:hi, th, 0:KT], q_now[u][:, lo:hi],
                                                    ctxT[u][:, b, KT * th:KT * th + KT], start=True, stop=True)
                    last.then_inc(s_sc, 1)

                def turned(n):
                    pe.wait_ge(s_ac, n + 1)
                    if not (isinstance(n, int) and n == 0):
                        pe.wait_ge(s_aTc, n)
                    nc.tensor.transpose(psM[:, 0:P], ac[:], ident[:]).then_inc(s_aT, 1)

                def products(n):
                    pe.wait_ge(s_aTc, n + 1)
                    pe.wait_ge(s_gb, n + 1)
                    if not (isinstance(n, int) and n == 0):
                        pe.wait_ge(s_x, n)
                    nc.tensor.matmul(psV[:, 0:C], acT[:], wlvT[:], start=True, stop=False)
                    nc.tensor.matmul(psV[:, 0:C], gbd[:], vis[:, bass.ds(n, 1), :] if not isinstance(n, int)
                                     else vis[:, n, :], start=False, stop=True).then_inc(s_o, 1)

                def body(i, u, first, last_turn):
                    n = 2 * i + u
                    if first:
                        scores(i, u)
                    pe.wait_ge(s_ex, n + 1)
                    if not last_turn:
                        scores(i + u, 1 - u)
                    if not first:
                        turned(n - 1)
                    for r in range(3):
                        if r == 2 and not first:
                            products(n - 1)
                        if not (first and r < 2):
                            pe.wait_ge(s_Tc, 3 * n + r - 1)
                        for q in range(4):
                            j = 4 * r + q
                            bank = psT[(r + u) % 2]
                            last = nc.tensor.transpose(bank[0:KC, P * q:P * q + P],
                                                       prob[u][:, KC * j:KC * j + KC], ident[:])
                        last.then_inc(s_T, 1)
                    pe.wait_ge(s_cN[u], 32 * i + 32)
                    if not first:
                        pe.wait_ge(s_gb, n)
                    for r in range(3):
                        pe.wait_ge(s_Tc, 3 * n + r + 1)
                        for q in range(4):
                            j = 4 * r + q
                            for b, (lo, hi) in enumerate(HALVES):
                                last = nc.tensor.matmul(psA[lo:hi, 0:C + TP], side[u][:, b, j, C:C + TP],
                                                        side[u][:, b, j, :], start=(j == 0), stop=(j == NCH - 1))
                    last.then_inc(s_A, 1)
                turns(pe, body)
                turned(NT - 1)
                products(NT - 1)

            @block.scalar
            def _(act):
                def body(i, u, first, last_turn):
                    n = 2 * i + u
                    act.wait_ge(s_nb, n + 1)
                    if not (first or (isinstance(n, int) and n == 1)):
                        act.wait_ge(s_T, 3 * n - 3)
                    nc.scalar.activation(prob[u][:].rearrange("p (h k) -> p h k", h=NTH), psS[:, :, 0:KT], ACT.Exp,
                                         bias=nb1[:, 0:1], accum_out=rsum[u][:]).then_inc(s_ex, 1)
                turns(act, body)

            @block.vector
            def _(dve):
                AHEAD, STEPS = 3, 5

                def row(buf, t):
                    return buf[:, t:t + 1] if isinstance(t, int) else buf[:, bass.ds(t, 1)]

                def now(i, u):
                    t = 2 * i + u
                    src = qT[:, P * t:P * t + P] if isinstance(t, int) else qT[:, bass.ds(P * t, P)]
                    nc.vector.tensor_copy(q_now[u][:], src).then_inc(s_now, 1)

                def biases(i, u, step):
                    t = 2 * i + u
                    dve.wait_ge(s_sc, t + 1)
                    step.then(nc.vector.tensor_reduce(nmax[:], psS[:, :, 0:KT], axis=mybir.AxisListType.XY,
                                                      op=ALU.max, negate=True))
                    step.then(nc.vector.tensor_tensor(nb0[:], nmax[:], row(cb, t), ALU.subtract))
                    nc.vector.tensor_tensor(nb1[:], nb0[:], row(cb, t), ALU.add).then_inc(s_nb, 1)

                def turned(n):
                    dve.wait_ge(s_aT, n + 1)
                    nc.vector.tensor_copy(acT[:], psM[:, 0:P]).then_inc(s_aTc, 1)

                def add(n, u):
                    dve.wait_ge(s_o, n + 1)
                    xt = x[:, n:n + 1, :] if isinstance(n, int) else x[:, bass.ds(n, 1), :]
                    nc.vector.scalar_tensor_tensor(out=xt, in0=psV[:, 0:C].unsqueeze(1), scalar=rtg[u][:, 0:1],
                                                   in1=xt, op0=ALU.mult, op1=ALU.add).then_inc(s_x, 1)

                now(0, 0)
                now(0, 1)
                biases(0, 0, Steps(dve, s_dve, 1))

                def body(i, u, first, last_turn):
                    n = 2 * i + u
                    step = Steps(dve, s_dve, AHEAD + STEPS * n)
                    dve.wait_ge(s_ex, n + 1)
                    step.then(nc.vector.reciprocal(rinv[:], rsum[u][:]))
                    step(nc.vector.tensor_scalar(rtg[u][:], rinv[:], tanh_g, None, ALU.mult))
                    step(nc.vector.tensor_scalar(rmask[:], rinv[:], rowmask, None, ALU.mult))
                    if not first:
                        turned(n - 1)
                    for r in range(3):
                        bank = psT[(r + u) % 2]
                        dve.wait_ge(s_T, 3 * n + r + 1)
                        for b, (lo, hi) in enumerate(HALVES):
                            src = bank[0:KC, :].rearrange("p (q s) -> p q s", q=4)[:, :, lo:hi]
                            last = nc.vector.tensor_copy(side[u][:, b, 4 * r:4 * r + 4, C:C + TP], src)
                        last.then_inc(s_Tc, 1)
                    if not first:
                        add(n - 1, 1 - u)
                    if not last_turn:
                        biases(i + u, 1 - u, step)
                        if not (isinstance(n, int) and n + 2 >= NT):
                            now(i + 1, u)
                    dve.wait_ge(s_A, n + 1)
                    nc.vector.tensor_copy(ac[:], psA[:, 0:P]).then_inc(s_ac, 1)
                    step.wait()
                    for lo, hi in HALVES:
                        last = nc.vector.tensor_scalar(gbd[lo:hi, lo:hi], psA[lo:hi, C:C + TP], rmask[lo:hi, :], None,
                                                       ALU.mult)
                    last.then_inc(s_gb, 1)
                    if not last_turn:
                        assert step.n == STEPS
                turns(dve, body)
                turned(NT - 1)
                add(NT - 1, 1)


def route(nc, phase, tokens, tokensT, experts_n, wT, bias, scale, index, weight, slots, zeros, d, tile_expert=None):
    E, capped = experts_n, tile_expert is None
    FAR = float(4 * SLOTS)
    with ExitStack() as ctx:
        r = Space(nc, ctx, phase)
        rwT = r.sb("rwT", [P, E])
        rb, experts = r.sb("rb", [P, NT, E]), r.sb("experts", [P, NT, E])
        before, ones = r.sb("before", [P, P]), r.sb("ones", [P, P])
        beforeb, onesb = r.sb("beforeb", [P, P], BF16), r.sb("onesb", [P, P], BF16)
        mask = r.sb("mask", [P, 1])
        logits, top = r.sb("logits", [P, NT, E]), r.sb("top", [P, NT, 8])
        which = r.sb("which", [P, NT, 8], U32)
        whichf = r.sb("whichf", [P, 2, NT])
        diff, ex, den = (r.sb(n, [P, NT]) for n in ("diff", "ex", "den"))
        gate, kept, pos, slot, tmp = (r.sb(n, [P, 2, NT]) for n in ("gate", "kept", "pos", "slot", "tmp"))
        first = r.sb("first", [P, 2, NT])
        chosen = [r.sb(f"chosen{k}", [P, NT, E]) for k in range(2)]
        both = r.sb("both", [P, NT, E], BF16)
        place, prod, base = (r.sb(n, [P, NT, E]) for n in ("place", "prod", "base"))
        total = r.sb("total", [P, NT, E])
        count, tiles, start, end = (r.sb(n, [P, E]) for n in ("count", "tiles", "start", "end"))
        whole = r.sb("whole", [P, E], U32)
        tile_ids, ended = r.sb("tile_ids", [P, NTILE, E]), r.sb("ended", [P, NTILE, E])
        owner = r.sb("owner", [P, NTILE])
        psL, psC = r.ps("psL", [P, 512]), r.ps("psC", [P, 2, 256])
        s_w, s_L, s_both, s_C, s_d, s_ex, s_dve = (r.sem(n) for n in ("w", "L", "both", "C", "d", "ex", "dve"))
        s_zero, s_zd, s_idx, s_scat = (r.sem(n) for n in ("zero", "zd", "idx", "scat"))
        block = ctx.enter_context(nc.Block())
        sources = [(rwT, wT), (experts, f"expert_ids{E}"), (before, "before"), (ones, "ones"), (mask, "rowmask")]
        if bias is not None:
            sources.append((rb, bias))
        if not capped:
            sources.append((tile_ids, "tile_ids"))

        @block.sync
        def _(sync):
            for dst, src in sources:
                sync.dma_start(dst[:], d[src]).then_inc(s_w, 16)
            sync.wait_ge(s_zero, 1)
            sync.dma_start(slots.rearrange("(i p) c -> p i c", p=P), zeros[:]).then_inc(s_zd, 16)

        @block.tensor
        def _(pe):
            pe.wait_ge(s_w, 16 * len(sources))
            for t in range(NT):
                last = nc.tensor.matmul(psL[:, E * t:E * t + E], tokensT[:, P * t:P * t + P], rwT[:],
                                        start=True, stop=True)
            last.then_inc(s_L, 1)
            pe.wait_ge(s_both, 1)
            for k, m in enumerate((beforeb, onesb)):
                last = nc.tensor.matmul(psC[:, k, 0:NT * E], m[:], both[:].rearrange("p t e -> p (t e)"),
                                        start=True, stop=True)
            last.then_inc(s_C, 1)

        @block.scalar
        def _(act):
            act.wait_ge(s_d, 1)
            nc.scalar.activation(ex[:], diff[:], ACT.Exp).then_inc(s_ex, 1)

        @block.vector
        def _(dve):
            v = nc.vector
            step = Steps(dve, s_dve)
            v.memset(zeros[:], 0.0).then_inc(s_zero, 1)
            dve.wait_ge(s_w, 16 * len(sources))
            step(v.tensor_copy(beforeb[:], before[:]))
            step(v.tensor_copy(onesb[:], ones[:]))
            dve.wait_ge(s_L, 1)
            got = psL[:, 0:NT * E].rearrange("p (t e) -> p t e", e=E)
            if bias is not None:
                step.then(v.tensor_tensor(logits[:], got, rb[:], ALU.add))
            else:
                step.then(v.tensor_copy(logits[:], got))
            for t in range(NT):
                step(v.max(out=top[:, t, :], in_=logits[:, t, :]))
            step.wait()
            for t in range(NT):
                step(v.max_index(out=which[:, t, :], in_max=top[:, t, :], in_values=logits[:, t, :]))
            v.tensor_tensor(diff[:], top[:, :, 1], top[:, :, 0], ALU.subtract).then_inc(s_d, 1)
            step.wait()
            for k in range(2):
                step(v.tensor_copy(whichf[:, k, :], which[:, :, k]))
            step.wait()
            for k in range(2):
                step(v.tensor_tensor(chosen[k][:], experts[:],
                                     whichf[:, k, :].unsqueeze(2).broadcast_to([P, NT, E]), ALU.is_equal))
            step.wait()
            for k in range(2):
                step(v.tensor_scalar(chosen[k][:], chosen[k][:], mask[:, 0:1], None, ALU.mult))
            step.wait()
            v.tensor_tensor(both[:], chosen[0][:], chosen[1][:], ALU.add).then_inc(s_both, 1)
            dve.wait_ge(s_C, 1)
            step(v.tensor_copy(total[:], psC[:, 1, 0:NT * E].rearrange("p (t e) -> p t e", e=E)))
            step.wait()
            step(v.memset(base[:, 0, :], 0.0))
            step.then(v.tensor_copy(base[:, 1:NT, :], total[:, 0:NT - 1, :]))
            src, dst, reach = base, prod, 1
            while reach < NT:
                step(v.tensor_copy(dst[:, 0:reach, :], src[:, 0:reach, :]))
                step.then(v.tensor_tensor(dst[:, reach:NT, :], src[:, reach:NT, :], src[:, 0:NT - reach, :], ALU.add))
                src, dst, reach = dst, src, 2 * reach
            assert src is base
            step.then(v.tensor_tensor(place[:], psC[:, 0, 0:NT * E].rearrange("p (t e) -> p t e", e=E), base[:],
                                      ALU.add))
            for k in range(2):
                step.then(v.tensor_tensor(prod[:], place[:], chosen[k][:], ALU.mult))
                step.then(v.reduce_sum(pos[:, k, :], prod[:], axis=AX_X))
            if capped:
                step.then(v.tensor_scalar(kept[:], pos[:], float(CAP), None, ALU.is_lt))
                step.then(v.tensor_scalar(kept[:], kept[:], mask[:, 0:1], None, ALU.mult))
                step.then(v.tensor_scalar(first[:], whichf[:], float(CAP), None, ALU.mult))
            else:
                step(v.tensor_scalar(kept[:], pos[:], 0.0, mask[:, 0:1], ALU.mult, ALU.add))
                step.then(v.tensor_tensor(count[:], base[:, NT - 1, :], total[:, NT - 1, :], ALU.add))
                step.then(v.tensor_scalar(whole[:], count[:], float(P - 1), None, ALU.add))
                step.then(v.tensor_scalar(whole[:], whole[:], 7, None, ALU.logical_shift_right))
                step.then(v.tensor_copy(tiles[:], whole[:]))
                step.then(v.memset(start[:, 0:1], 0.0))
                for e in range(1, E):
                    step.then(v.tensor_tensor(start[:, e:e + 1], start[:, e - 1:e], tiles[:, e - 1:e], ALU.add))
                step.then(v.tensor_tensor(end[:], start[:], tiles[:], ALU.add))
                step.then(v.tensor_tensor(ended[:], tile_ids[:], end[:].unsqueeze(1).broadcast_to([P, NTILE, E]),
                                          ALU.is_ge))
                step.then(v.reduce_sum(owner[:], ended[:], axis=AX_X))
                step.then(v.tensor_scalar(tile_expert[:], owner[:], float(E - 1), None, ALU.min))
                for k in range(2):
                    step.then(v.tensor_tensor(prod[:], chosen[k][:], start[:].unsqueeze(1).broadcast_to([P, NT, E]),
                                              ALU.mult))
                    step.then(v.reduce_sum(first[:, k, :], prod[:], axis=AX_X))
                step.then(v.tensor_scalar(first[:], first[:], float(P), None, ALU.mult))
            step(v.tensor_tensor(slot[:], first[:], pos[:], ALU.add))
            step.then(v.tensor_scalar(tmp[:], kept[:], -FAR, FAR, ALU.mult, ALU.add))
            step.then(v.tensor_tensor(slot[:], slot[:], tmp[:], ALU.add))
            for k in range(2):
                v.tensor_copy(index[k][:], slot[:, k, :]).then_inc(s_idx, 1)
            dve.wait_ge(s_ex, 1)
            step.then(v.tensor_scalar(den[:], ex[:], 1.0, None, ALU.add))
            step.then(v.reciprocal(gate[:, 0, :], den[:]))
            step(v.tensor_tensor(gate[:, 1, :], gate[:, 0, :], ex[:], ALU.mult))
            step.wait()
            if capped:
                step.then(v.tensor_tensor(gate[:], gate[:], kept[:], ALU.mult))
                step.then(v.tensor_tensor(den[:], gate[:, 0, :], gate[:, 1, :], ALU.add))
                step.then(v.tensor_scalar(den[:], den[:], 1e-9, None, ALU.add))
                step.then(v.reciprocal(den[:], den[:]))
                step.then(v.tensor_tensor(gate[:], gate[:], den[:].unsqueeze(1).broadcast_to([P, 2, NT]), ALU.mult))
            step.then(v.tensor_scalar(gate[:], gate[:], scale, None, ALU.mult))
            for k in range(2):
                step(v.tensor_tensor(weight[k][:], gate[:, k, :], kept[:, k, :], ALU.mult))

        @block.gpsimd
        def _(pool):
            pool.wait_ge(s_zd, 16)
            for k in range(2):
                pool.wait_ge(s_idx, k + 1)
                for t in range(NT):
                    nc.gpsimd.indirect_dma_start(
                        out=slots, out_offset=bass.IndirectOffsetOnAxis(index[k][:, t:t + 1], 0),
                        in_=tokens[:, t, :], in_offset=None, bounds_check=SLOTS - 1, oob_is_err=False
                    ).then_inc(s_scat, 16)
            pool.wait_ge(s_scat, 16 * 2 * NT)


def gather_results(nc, dve, pool, x, results, index, weight, got, s_got, s_used):
    def take():
        for t in range(NT):
            for k in range(2):
                n = 2 * t + k
                q = n % 4
                if n >= 4:
                    pool.wait_ge(s_used[q], n // 4)
                nc.gpsimd.indirect_dma_start(
                    out=got[q][:], out_offset=None, in_=results,
                    in_offset=bass.IndirectOffsetOnAxis(index[k][:, t:t + 1], 0),
                    bounds_check=SLOTS - 1, oob_is_err=False).then_inc(s_got[q], 16)

    def add():
        for t in range(NT):
            for k in range(2):
                n = 2 * t + k
                q = n % 4
                dve.wait_ge(s_got[q], 16 * (n // 4 + 1))
                if k:
                    dve.wait_ge(s_used[(n - 1) % 4], (n - 1) // 4 + 1)
                nc.vector.scalar_tensor_tensor(out=x[:, t, :], in0=got[q][:], scalar=weight[k][:, t:t + 1],
                                               in1=x[:, t, :], op0=ALU.mult, op1=ALU.add).then_inc(s_used[q], 1)
    if dve is not None:
        add()
    else:
        take()


def capacity_experts(nc, x, xn, xnT, ident, tanh_g, d):
    with ExitStack() as ctx:
        sp = Space(nc, ctx, "ce")
        slots = nc.dram_tensor("slots", (SLOTS, C), F32, kind="Internal").ap()
        results = nc.dram_tensor("results", (SLOTS, C), F32, kind="Internal").ap()
        index = [sp.sb(f"index{k}", [P, NT], U32) for k in range(2)]
        weight = [sp.sb(f"weight{k}", [P, NT]) for k in range(2)]
        NROW = SLOTS // P
        rows = sp.sb("rows", [P, NROW, C])
        slotT = sp.sb("slotT", [P, SLOTS])

        route(nc, "r0", xn, xnT, E0, "L0_router_wT", "L0_router_b", tanh_g, index, weight, slots, rows, d)

        with ExitStack() as inner:
            f = Space(nc, inner, "ff")
            w1 = [f.sb(f"w1{u}", [P, FF0]) for u in range(2)]
            w2 = [f.sb(f"w2{u}", [P, FC0, C]) for u in range(2)]
            b1, b2 = f.sb("b1", [P, E0, FC0]), f.sb("b2", [P, E0])
            b1now = [f.sb(f"b1now{u}", [P, FC0]) for u in range(2)]
            hT = [f.sb(f"hT{u}", [P, FC0, CAP]) for u in range(2)]
            outT = f.sb("outT", [P, SLOTS])
            got = [f.sb(f"got{q}", [P, C]) for q in range(4)]
            psT, psH = f.ps("psT", [P, 2, 512]), f.ps("psH", [P, 2, 512])
            psY, psR = f.ps("psY", [P, 2, 512]), f.ps("psR", [P, 2, 512])
            s_b, s_T, s_Tc = (f.sem(n) for n in ("b", "T", "Tc"))
            GROUPS = [(g, min(g + 12, NROW)) for g in range(0, NROW, 12)]
            s_rows = [f.sem(f"rows{g}") for g in range(len(GROUPS))]
            s_w1, s_w2 = [f.sem(f"w1{u}") for u in range(2)], [f.sem(f"w2{u}") for u in range(2)]
            s_H, s_h, s_Y, s_y, s_bn, s_R, s_r, s_st, s_gz, s_dve = (
                f.sem(n) for n in ("H", "h", "Y", "y", "bn", "R", "r", "st", "gz", "dve"))
            s_got, s_used = [f.sem(f"got{q}") for q in range(4)], [f.sem(f"used{q}") for q in range(4)]
            block = inner.enter_context(nc.Block())
            QT = -(-NROW // 4)

            def at(buf, n, width):
                return buf[:, width * n:width * n + width] if isinstance(n, int) else buf[:, bass.ds(width * n, width)]

            @block.sync
            def _(sync):
                for g, (lo, hi) in enumerate(GROUPS):
                    sync.dma_start(rows[:, lo:hi, :], slots.rearrange("(i p) c -> p i c", p=P)[:, lo:hi, :]
                                   ).then_inc(s_rows[g], 16)
                sync.dma_start(b1[:], d["L0_b1"]).then_inc(s_b, 16)
                sync.dma_start(b2[:], d["L0_b2"]).then_inc(s_b, 16)

                def load(i, u, first):
                    e = 2 * i + u
                    if not first:
                        sync.wait_ge(s_H, FC0 * (e - 1))
                    sync.dma_start(w1[u][:].unsqueeze(1), d["L0_w1"][bass.ds(e, 1)].rearrange("o c f -> c o f")
                                   ).then_inc(s_w1[u], 16)
                    if not first:
                        sync.wait_ge(s_Y, e - 1)
                    sync.dma_start(w2[u][:], d["L0_w2"][bass.ds(e, 1)].rearrange("o (q f) c -> f (o q) c", f=P)
                                   ).then_inc(s_w2[u], 16)
                for u in range(2):
                    load(0, u, True)
                with sync.Fori(1, E0 // 2) as i:
                    for u in range(2):
                        load(i, u, False)
                for lo, hi in GROUPS:
                    sync.wait_ge(s_r, -(-hi // 4))
                    sync.dma_start(results.rearrange("(i p) c -> p i c", p=P)[:, lo:hi, :], rows[:, lo:hi, :]
                                   ).then_inc(s_st, 16)

            @block.tensor
            def _(pe):
                for q in range(QT):
                    if 4 * q % 12 == 0:
                        pe.wait_ge(s_rows[q // 3], 16)
                    if q >= 2:
                        pe.wait_ge(s_Tc, q - 1)
                    for r in range(min(4, NROW - 4 * q)):
                        last = nc.tensor.transpose(psT[:, q % 2, P * r:P * r + P], rows[:, 4 * q + r, :], ident[:])
                    last.then_inc(s_T, 1)
                pe.wait_ge(s_Tc, QT)

                def expert(i, u, first):
                    e = 2 * i + u
                    pe.wait_ge(s_w1[u], 16 * i + 16)
                    for q in range(FC0):
                        if not (first and e == 0 and q < 2):
                            pe.wait_ge(s_h, FC0 * e + q - 1)
                        nc.tensor.matmul(psH[:, q % 2, 0:CAP], w1[u][:, P * q:P * q + P], at(slotT, e, CAP),
                                         start=True, stop=True).then_inc(s_H, 1)
                    pe.wait_ge(s_w2[u], 16 * i + 16)
                    if not first:
                        pe.wait_ge(s_y, e - 1)
                    for q in range(FC0):
                        pe.wait_ge(s_h, FC0 * e + q + 1)
                        last = nc.tensor.matmul(psY[:, u, 0:CAP], w2[u][:, q, :], hT[u][:, q, :],
                                                start=(q == 0), stop=(q == FC0 - 1))
                    last.then_inc(s_Y, 1)
                for u in range(2):
                    expert(0, u, True)
                with pe.Fori(1, E0 // 2) as i:
                    for u in range(2):
                        expert(i, u, False)
                pe.wait_ge(s_y, E0)
                for q in range(QT):
                    if q >= 2:
                        pe.wait_ge(s_r, q - 1)
                    for r in range(min(4, NROW - 4 * q)):
                        c0 = P * (4 * q + r)
                        last = nc.tensor.transpose(psR[:, q % 2, P * r:P * r + P], outT[:, c0:c0 + P], ident[:])
                    last.then_inc(s_R, 1)

            @block.scalar
            def _(act):
                for q in range(QT):
                    n = P * min(4, NROW - 4 * q)
                    act.wait_ge(s_T, q + 1)
                    nc.scalar.copy(slotT[:, 512 * q:512 * q + n], psT[:, q % 2, 0:n]).then_inc(s_Tc, 1)

                def expert(i, u, first):
                    e = 2 * i + u
                    act.wait_ge(s_bn, e + 1)
                    if not first:
                        act.wait_ge(s_Y, e - 1)
                    for q in range(FC0):
                        act.wait_ge(s_H, FC0 * e + q + 1)
                        nc.scalar.activation(hT[u][:, q, :], psH[:, q % 2, 0:CAP], ACT.Gelu,
                                             bias=b1now[u][:, q:q + 1]).then_inc(s_h, 1)
                for u in range(2):
                    expert(0, u, True)
                with act.Fori(1, E0 // 2) as i:
                    for u in range(2):
                        expert(i, u, False)

            @block.vector
            def _(dve):
                v = nc.vector
                for q in range(4):
                    last = v.memset(got[q][:], 0.0)
                last.then_inc(s_gz, 1)
                dve.wait_ge(s_b, 32)

                def expert(i, u, first):
                    e = 2 * i + u
                    if not first:
                        dve.wait_ge(s_h, FC0 * (e - 1))
                    b1e = b1[:, e:e + 1, :] if isinstance(e, int) else b1[:, bass.ds(e, 1), :]
                    v.tensor_copy(b1now[u][:].unsqueeze(1), b1e).then_inc(s_bn, 1)

                def result(i, u):
                    e = 2 * i + u
                    dve.wait_ge(s_Y, e + 1)
                    b2e = b2[:, e:e + 1] if isinstance(e, int) else b2[:, bass.ds(e, 1)]
                    v.tensor_scalar(at(outT, e, CAP), psY[:, u, 0:CAP], b2e, None, ALU.add).then_inc(s_y, 1)
                for u in range(2):
                    expert(0, u, True)
                with dve.Fori(1, E0 // 2) as i:
                    for u in range(2):
                        result(i - 1, u)
                        expert(i, u, False)
                for u in range(2):
                    result(E0 // 2 - 1, u)
                for q in range(QT):
                    n = min(4, NROW - 4 * q)
                    dve.wait_ge(s_R, q + 1)
                    v.tensor_copy(rows[:, 4 * q:4 * q + n, :],
                                  psR[:, q % 2, 0:P * n].rearrange("p (r c) -> p r c", r=n)).then_inc(s_r, 1)
                gather_results(nc, dve, None, x, results, index, weight, got, s_got, s_used)

            @block.gpsimd
            def _(pool):
                pool.wait_ge(s_gz, 1)
                pool.wait_ge(s_st, 16 * len(GROUPS))
                gather_results(nc, None, pool, x, results, index, weight, got, s_got, s_used)


def attention(nc, x, xnT, tanh_g, identb, ahead, s_ahead, d):
    SCALE = float(HD) ** -0.5
    PARTS_K, PARTS_Q = (0, 1, 2, 0, 1, 0), (0, 0, 0, 1, 1, 2)
    SR, MR = 6 * 2 * HD, 3 * NPAIR
    PW, QW = 2 * T, H * T
    MAXIMA = (1, 1, 1, 4, 4, 3, 4, 3, 3, 0, 0, 0)
    BANKS = 3
    VALUES = 2
    qd = nc.dram_tensor("q_parts", (NPAIR, 6, 2, HD, NT * P), BF16, kind="Internal").ap()
    kd = nc.dram_tensor("k_parts", (2, NTH, NPAIR, 3, 2, HD, KT), BF16, kind="Internal").ap()

    with ExitStack() as ctx:
        sp = Space(nc, ctx, "at")
        wkT, wvT = sp.sb("wkT", [P, C]), sp.sb("wvT", [P, NG * 24])
        bk = sp.sb("bk", [P, 1])
        woT = sp.sb("woT", [P, 2, C])
        sel, own = sp.sb("sel", [P, 3, P]), sp.sb("own", [P, 3])
        qmask = sp.sb("qmask", [SR, QW], BF16)
        own_pair = sp.sb("own_pair", [P, QW])
        kst = [sp.sb(f"kst{u}", [SR + MR, NPAIR, S], BF16) for u in range(2)]
        val = [sp.sb(f"val{u}", [KC, NCH, NG, 32]) for u in range(2)]
        prob = [sp.sb(f"prob{u}", [KC, NG * GW]) for u in range(2)]
        zeros = sp.sb("zeros", [P, KT])

        with ExitStack() as inner:
            q = Space(nc, inner, "aq")
            wqT, wo_plain, bvc = q.sb("wqT", [P, C]), q.sb("wo_plain", [P, C]), q.sb("bvc", [P, P])
            bq, bqs, bo = q.sb("bq", [P, 1]), q.sb("bqs", [P, 1]), q.sb("bo", [P, C])
            q32, rest = q.sb("q32", [P, NT * P]), q.sb("rest", [P, NT * P])
            parts = q.sb("parts", [P, 3, NT * P], BF16)
            mask32, out_b = q.sb("mask32", [SR, QW]), q.sb("out_b", [P, C])
            psQ, psB = q.ps("psQ", [P, 4, 512]), q.ps("psB", [P, 512])
            s_w, s_q, s_q32, s_B, s_parts, s_st, s_dve, s_bqs, s_pool = (
                q.sem(n) for n in ("w", "q", "q32", "B", "parts", "st", "dve", "bqs", "pool"))
            block = inner.enter_context(nc.Block())
            loads = ((own_pair, "pair_rows"), (wkT, "L1_W_kT"), (wvT, "L1_W_vT"), (bk, "L1_b_k"), (woT, "L1_W_oT"), (sel, "sum_rows"),
                     (own, "own_rows"), (mask32, "pair_mask"), (wqT, "L1_W_qT"), (wo_plain, "L1_W_oT_plain"),
                     (bvc, "L1_b_v"), (bq, "L1_b_q"), (bo, "L1_b_o"))

            @block.sync
            def _(sync):
                for dst, src in loads:
                    sync.dma_start(dst[:], d[src]).then_inc(s_w, 16)
                for half in range(2):
                    at = slice(NT * P // 2 * half, NT * P // 2 * (half + 1))
                    for k in range(3):
                        sync.wait_ge(s_parts, 3 * half + k + 1)
                        for c in range(6):
                            if PARTS_Q[c] == k:
                                sync.dma_start(qd[:, c, :, :, at], parts[:, k, at]).then_inc(s_st, 16)
                sync.wait_ge(s_st, 16 * 2 * 6)

            @block.tensor
            def _(pe):
                pe.wait_ge(s_w, 16 * len(loads))
                for k in range(4):
                    nc.tensor.matmul(psQ[:, k, :], wqT[:], xnT[:, 512 * k:512 * k + 512], start=True, stop=True
                                     ).then_inc(s_q, 1)
                nc.tensor.matmul(psB[:, 0:C], bvc[:], wo_plain[:], start=True, stop=True).then_inc(s_B, 1)

            @block.scalar
            def _(act):
                act.wait_ge(s_bqs, 1)
                for k in range(4):
                    act.wait_ge(s_q, k + 1)
                    nc.scalar.activation(q32[:, 512 * k:512 * k + 512], psQ[:, k, :], ACT.Identity, scale=SCALE,
                                         bias=bqs[:, 0:1]).then_inc(s_q32, 1)

            @block.vector
            def _(dve):
                v = nc.vector
                step = Steps(dve, s_dve)
                for u in range(2):
                    v.memset(prob[u][:, QW:NG * GW], 1.0)
                dve.wait_ge(s_w, 16 * len(loads))
                v.tensor_scalar(bqs[:], bq[:], SCALE, None, ALU.mult).then_inc(s_bqs, 1)
                step(v.tensor_copy(qmask[:], mask32[:]))
                for half in range(2):
                    at, n = slice(NT * P // 2 * half, NT * P // 2 * (half + 1)), 3 * half
                    dve.wait_ge(s_q32, 2 * half + 2)
                    v.tensor_copy(parts[:, 0, at], q32[:, at]).then_inc(s_parts, 1)
                    dve.wait_ge(s_parts, n + 1)
                    step.then(v.tensor_tensor(rest[:, at], q32[:, at], parts[:, 0, at], ALU.subtract))
                    v.tensor_copy(parts[:, 1, at], rest[:, at]).then_inc(s_parts, 1)
                    dve.wait_ge(s_parts, n + 2)
                    v.tensor_tensor(parts[:, 2, at], rest[:, at], parts[:, 1, at], ALU.subtract).then_inc(s_parts, 1)
                dve.wait_ge(s_B, 1)
                step.then(v.tensor_tensor(out_b[:], psB[:, 0:C], bo[:], ALU.add))
                for t in range(NT):
                    step(v.scalar_tensor_tensor(out=x[:, t, :], in0=out_b[:], scalar=tanh_g, in1=x[:, t, :],
                                                op0=ALU.mult, op1=ALU.add))

            @block.gpsimd
            def _(pool):
                step = Steps(pool, s_pool)
                step.then(nc.gpsimd.memset(val[0][:], 1.0))
                step.then(nc.gpsimd.memset(val[1][:], 1.0))
                step.then(nc.gpsimd.memset(zeros[:], 0.0))
                for u in range(2):
                    step.then(nc.gpsimd.memset(kst[u][SR:SR + MR, :, :], 1.0))

        ctxT = [sp.sb(f"ctxT{u}", [P, S]) for u in range(2)]
        kparts = sp.sb("kparts", [P, NTH, 3, KT], BF16)
        krest = sp.sb("krest", [P, NTH, KT])
        qraw = [sp.sb(f"qraw{u}", [SR, NPAIR, 2, T], BF16) for u in range(2)]
        qmx = [sp.sb(f"qmx{u}", [SR, QW], BF16) for u in range(2)]
        qst = [sp.sb(f"qst{u}", [SR + MR, QW], BF16) for u in range(2)]
        mx, nmx, mrest = sp.sb("mx", [PW, NTH, NPAIR]), sp.sb("nmx", [PW, NPAIR]), sp.sb("mrest", [PW, NPAIR])
        mparts = sp.sb("mparts", [PW, 3, NPAIR], BF16)
        sums = sp.sb("sums", [P, 2, 3, T])
        mine, recip, attn = (sp.sb(n, [P, 2, T]) for n in ("mine", "recip", "attn"))

        psS = sp.ps("psS", [P, 2, 2, 512])
        psO = sp.ps("psO", [P, 512])
        psR = [sp.ps(f"psR{r}", [P, 512]) for r in range(BANKS)]

        s_ctx, s_ql = [sp.sem(f"ctx{u}") for u in range(2)], [sp.sem(f"ql{u}") for u in range(2)]
        s_kw, s_kl = [sp.sem(f"kw{i}") for i in range(NTH)], [sp.sem(f"kl{i}") for i in range(NTH)]
        s_free = [sp.sem(f"free{r}") for r in range(BANKS)]
        s_full, s_hi, s_kp, s_qm, s_qs, s_mp, s_S, s_exp, s_PV, s_ou, s_on, s_dm, s_do, s_pool, s_set = (
            sp.sem(n) for n in ("full", "hi", "kp", "qm", "qs", "mp", "S", "exp", "PV", "ou", "on", "dm", "do",
                                "pool", "set"))

        def ring(b):
            known = isinstance(b, int)
            keys, maxima, ends = (not known or b <= B - 3), (not known or -1 <= b <= B - 2), (not known or b >= 1)
            units, m = [[] for _ in range(NCH)], 0
            for j in range(NCH):
                if keys and j < NTH:
                    units[j].append(("keys", j))
                if ends and j == 2:
                    units[j].append(("sums", 0))
                if maxima:
                    units[j] += [("max", m + r) for r in range(MAXIMA[j])]
                    m += MAXIMA[j]
                if maxima and 0 <= j - VALUES < 6:
                    units[j].insert(1, ("values", j - VALUES))
                if ends and j == 5:
                    units[j].append(("out", 0))
                if maxima and j == 10:
                    units[j].append(("rows", 0))
            return units

        def size(b):
            return sum(len(u) for u in ring(b))

        UNITS = size(2)
        FIRST = sum(size(b) for b in range(-2, 2))
        assert UNITS % BANKS == 0

        class Unit:

            def __init__(self, kind, idx, b, local):
                self.kind, self.idx = kind, idx
                if isinstance(b, int):
                    n = sum(size(c) for c in range(-2, b)) + local
                    self.before, self.turn, self.new = n, n // BANKS, n < BANKS
                else:
                    n = FIRST - 2 * UNITS + local
                    self.before, self.turn, self.new = b * UNITS + n, b * (UNITS // BANKS) + n // BANKS, False
                self.bank, self.ps = n % BANKS, psR[n % BANKS]

            def free(self, engine):
                if not self.new:
                    engine.wait_ge(s_free[self.bank], self.turn)

            def full(self, engine):
                engine.wait_ge(s_full, self.before + 1)

            def read(self, engine):
                engine.wait_ge(s_free[self.bank], self.turn + 1)

        def units_of(b):
            local, out = 0, []
            for row in ring(b):
                out.append([Unit(kind, idx, b, local + r) for r, (kind, idx) in enumerate(row)])
                local += len(row)
            return out

        def the_unit(b, kind, idx=0):
            return next(unit for row in units_of(b) for unit in row if (unit.kind, unit.idx) == (kind, idx))

        def steps(engine, body):
            for b in range(-2, 2):
                body(b // 2, b % 2)
            with engine.Fori(1, B // 2 - 1) as k:
                for u in range(2):
                    body(k, u)
            for b in range(B - 2, B + 1):
                body(b // 2, b % 2)

        def has(b, lo, hi):
            return not isinstance(b, int) or lo <= b <= hi

        block = ctx.enter_context(nc.Block())

        @block.sync
        def _(sync):
            def load_ctx(c, u):
                sync.dma_start(ctxT[u][:].unsqueeze(1), d["ctxT"][bass.ds(c, 1)].rearrange("o c s -> c o s")
                               ).then_inc(s_ctx[u], 16)

            def body(k, u):
                b, w = 2 * k + u, 1 - u
                if has(b, -2, B - 3):
                    if has(b, 0, B):
                        sync.wait_ge(s_qm, b + 1)
                    for r in range(2):
                        src = qd.rearrange("p c r d t -> (c r d) p t")[:, :, bass.ds((b + 2) * TP, T)]
                        sync.dma_start(qraw[u][:, :, r, :], src).then_inc(s_ql[u], 16)
                    if has(b, 0, B):
                        for i in range(NTH):
                            sync.wait_ge(s_kl[i], 48 * (b + 1))
                    for i in range(NTH):
                        sync.wait_ge(s_kp, 3 * (b + 2) + i + 1)
                        for c in range(3):
                            sync.dma_start(kd[u, i, :, c], kparts[:, i, c, :]).then_inc(s_kw[i], 16)

                def stack(i):
                    if has(b, 0, B):
                        sync.wait_ge(s_S, NCH * b + 4 * i + 4)
                    sync.wait_ge(s_kw[i], 48 * (b + 3))
                    for n, row in ((3, 0), (2, 48), (1, 80)):
                        src = kd[u, i][:, 0:n].rearrange("p c r d k -> (c r d) p k")
                        sync.dma_start(kst[u][row:row + 16 * n, :, KT * i:KT * i + KT], src).then_inc(s_kl[i], 16)
                if has(b, -2, B - 3):
                    stack(0)
                if has(b, -2, B - 4):
                    if has(b, -1, B):
                        the_unit(b, "values", 5).read(sync)
                    load_ctx(b + 3, w)
                if has(b, -2, B - 3):
                    stack(1)
                if has(b, -2, B - 3):
                    stack(2)

            load_ctx(0, 0)
            sync.wait_ge(s_set, 1)
            for b in range(-2, 2):
                body(b // 2, b % 2)
            for dst, src in ahead:
                sync.dma_start(dst, src).then_inc(s_ahead, 16)
            with sync.Fori(1, B // 2 - 2) as k:
                for u in range(2):
                    body(k, u)
            for b in range(B - 4, B + 1):
                body(b // 2, b % 2)

        @block.tensor
        def _(pe):
            pe.wait_ge(s_set, 1)

            def body(k, u):
                b, w = 2 * k + u, 1 - u
                units = units_of(b)
                def form(unit):
                    unit.free(pe)
                    R, kind, idx = unit.ps, unit.kind, unit.idx
                    if kind == "keys":
                        if idx == 0:
                            pe.wait_ge(s_ctx[u], 16 * (k + 2))
                        last = nc.tensor.matmul(R[:, 0:KT], wkT[:], ctxT[u][:, KT * idx:KT * idx + KT],
                                                start=True, stop=True)
                    elif kind == "max":
                        i, p = idx // NPAIR, idx % NPAIR
                        if p == 0:
                            pe.wait_ge(s_kl[i], 48 * (b + 2))
                        if idx == 0:
                            pe.wait_ge(s_qm, b + 2)
                        last = nc.tensor.matmul(R[0:PW, 0:KT], qmx[w][:, PW * p:PW * p + PW],
                                                kst[w][0:SR, p, KT * i:KT * i + KT], start=True, stop=True)
                    elif kind == "values":
                        for r in range(2):
                            c0 = KC * (2 * idx + r)
                            last = nc.tensor.matmul(R[0:KC, 144 * r:144 * r + 144], ctxT[w][:, c0:c0 + KC], wvT[:],
                                                    start=True, stop=True)
                    elif kind == "sums":
                        pe.wait_ge(s_ou, b)
                        for r in range(3):
                            last = nc.tensor.matmul(R[:, 0:2 * T].rearrange("p (s t) -> p s t", s=2),
                                                    sel[:, r, :], sums[:, :, r, :], start=(r == 0), stop=(r == 2))
                    elif kind == "out":
                        pe.wait_ge(s_on, b)
                        for s in range(2):
                            last = nc.tensor.matmul(R[64 * w:64 * w + T, 0:C], attn[:, s, :], woT[:, s, :],
                                                    start=(s == 0), stop=(s == 1))
                    else:
                        pe.wait_ge(s_mp, b + 2)
                        last = nc.tensor.matmul(R[SR:SR + MR, 0:PW], mparts[:].rearrange("q c p -> q (c p)"),
                                                identb[0:PW, 0:PW], start=True, stop=True)
                    last.then_inc(s_full, 1)

                for j in range(NCH):
                    g = NCH * b + j
                    if has(b, 0, B - 1):
                        if j == 0:
                            pe.wait_ge(s_qs, b + 1)
                            the_unit(b - 1, "rows").read(pe)
                        if has(b, 1, B) or j >= 2:
                            pe.wait_ge(s_exp, g - 1)
                        for p in range(NPAIR):
                            last = nc.tensor.matmul(psS[0:KC, j % 2, p // 4, PW * (p % 4):PW * (p % 4) + PW],
                                                    kst[u][:, p, KC * j:KC * j + KC], qst[u][:, PW * p:PW * p + PW],
                                                    start=True, stop=True)
                        last.then_inc(s_S, 1)
                    before = 1 if j < 10 else 0
                    for unit in units[j][:before]:
                        form(unit)
                    if (j > 0 and has(b, 0, B - 1)) or (j == 0 and has(b, 1, B)):
                        jj, uu = (j - 1, u) if j else (NCH - 1, w)
                        pe.wait_ge(s_exp, g)
                        if jj == 0:
                            the_unit(b - 1, "values", 5).read(pe)
                            if has(b, 1, B):
                                pe.wait_ge(s_ou, b)
                        for G in range(NG):
                            r, s = G % 4, G // 4
                            last = nc.tensor.matmul(psO[32 * r:32 * r + 32, GW * s:GW * s + GW],
                                                    val[uu][:, jj, G, :], prob[jj % 2][:, GW * G:GW * G + GW],
                                                    start=(jj == 0 and s == 0), stop=(jj == NCH - 1),
                                                    skip_group_check=True)
                        last.then_inc(s_PV, 1)
                    for unit in units[j][before:]:
                        form(unit)
            steps(pe, body)

        @block.scalar
        def _(act):
            act.wait_ge(s_set, 1)

            def body(k, u):
                b, w = 2 * k + u, 1 - u
                units = units_of(b)
                for j in range(NCH):
                    g = NCH * b + j
                    if has(b, 0, B - 1):
                        act.wait_ge(s_S, g + 1)
                        if has(b, 1, B) or j >= 2:
                            act.wait_ge(s_PV, g - 1)
                        nc.scalar.activation(prob[j % 2][:, 0:QW].rearrange("p (a q) -> p a q", a=2),
                                             psS[0:KC, j % 2, :, 0:QW // 2], ACT.Exp).then_inc(s_exp, 1)
                    for unit in units[j]:
                        idx = unit.idx
                        if unit.kind == "keys":
                            unit.full(act)
                            if has(b, -1, B):
                                act.wait_ge(s_kw[idx], 48 * (b + 2))
                            nc.scalar.activation(kparts[:, idx, 0, :], unit.ps[:, 0:KT], ACT.Identity,
                                                 bias=bk[:, 0:1]).then_inc(s_hi, 1)
                        if unit.kind == "values":
                            unit.full(act)
                            if idx == 0 and has(b, 1, B):
                                act.wait_ge(s_PV, NCH * b)
                            dst = val[w][:, 2 * idx:2 * idx + 2, :, 0:24]
                            nc.scalar.copy(dst, unit.ps[0:KC, 0:288].rearrange("p (r g e) -> p r g e", r=2, g=NG)
                                           ).then_inc(s_free[unit.bank], 1)
            steps(act, body)

        @block.vector
        def _(dve):
            v = nc.vector
            v.memset(psO[:], 1.0).then_inc(s_set, 1)

            def body(k, u):
                b, w = 2 * k + u, 1 - u
                units = units_of(b)
                for j in range(NCH):
                    if j == 0 and has(b, 1, B):
                        dve.wait_ge(s_PV, NCH * b)
                        v.tensor_copy(sums[:], psO[:, 0:2 * GW].rearrange("p (s r t) -> p s r t", s=2, r=3)
                                      ).then_inc(s_ou, 1)
                    if j == 1 and has(b, 1, B):
                        dve.wait_ge(s_ou, b)
                        v.tensor_scalar(mine[:], sums[:, :, 0, :], own[:, 0:1], None, ALU.mult).then_inc(s_do, 1)
                        for r in (1, 2):
                            dve.wait_ge(s_do, 3 * (b - 1) + r)
                            v.scalar_tensor_tensor(out=mine[:], in0=sums[:, :, r, :], scalar=own[:, r:r + 1],
                                                   in1=mine[:], op0=ALU.mult, op1=ALU.add).then_inc(s_do, 1)
                    for unit in units[j]:
                        R, kind, idx, freed = unit.ps, unit.kind, unit.idx, s_free[unit.bank]
                        if kind == "values":
                            continue
                        if kind == "keys":
                            dve.wait_ge(s_hi, 3 * (b + 2) + idx + 1)
                            if has(b, -1, B):
                                dve.wait_ge(s_kp, 3 * (b + 1) + idx + 1)
                            v.scalar_tensor_tensor(out=krest[:, idx, :], in0=R[:, 0:KT], scalar=bk[:, 0:1],
                                                   in1=kparts[:, idx, 0, :], op0=ALU.add, op1=ALU.subtract
                                                   ).then_inc(freed, 1)
                            continue
                        unit.full(dve)
                        if kind == "max":
                            i, p = idx // NPAIR, idx % NPAIR
                            v.reduce_max(mx[:, i, p:p + 1], R[0:PW, 0:KT], axis=AX_X).then_inc(freed, 1)
                        elif kind == "sums":
                            v.reciprocal(recip[:], R[:, 0:2 * T].rearrange("p (s t) -> p s t", s=2)
                                         ).then_inc(freed, 1)
                            unit.read(dve)
                            dve.wait_ge(s_do, 3 * b)
                            v.tensor_tensor(attn[:], mine[:], recip[:], ALU.mult).then_inc(s_on, 1)
                        elif kind == "out":
                            t = k - 1 if u == 0 else k
                            rows = slice(64 * w, 64 * w + T)
                            xt = x[rows, bass.ds(t, 1), :] if not isinstance(t, int) else x[rows, t:t + 1, :]
                            v.scalar_tensor_tensor(out=xt, in0=R[rows, 0:C].unsqueeze(1), scalar=tanh_g[rows, :],
                                                   in1=xt, op0=ALU.mult, op1=ALU.add).then_inc(freed, 1)
                        else:
                            rows = R[SR:SR + MR, 0:PW].unsqueeze(1).broadcast_to([MR, NPAIR, PW])
                            v.tensor_tensor(qst[w][SR:SR + MR, :].rearrange("q (p t) -> q p t", p=NPAIR), rows,
                                            own_pair[SR:SR + MR, :].rearrange("q (p t) -> q p t", p=NPAIR),
                                            ALU.mult).then_inc(freed, 1)
                        if kind == "max" and idx == 3 * NPAIR - 1:
                            unit.read(dve)
                            at = 4 * (b + 1)
                            v.tensor_reduce(nmx[:], mx[:].rearrange("q i p -> q p i"), axis=AX_X, op=ALU.max,
                                            negate=True).then_inc(s_dm, 1)
                            dve.wait_ge(s_dm, at + 1)
                            v.tensor_copy(mparts[:, 0, :], nmx[:]).then_inc(s_dm, 1)
                            dve.wait_ge(s_dm, at + 2)
                            v.tensor_tensor(mrest[:], nmx[:], mparts[:, 0, :], ALU.subtract).then_inc(s_dm, 1)
                            dve.wait_ge(s_dm, at + 3)
                            v.tensor_copy(mparts[:, 1, :], mrest[:]).then_inc(s_dm, 1)
                            dve.wait_ge(s_dm, at + 4)
                            v.tensor_tensor(mparts[:, 2, :], mrest[:], mparts[:, 1, :], ALU.subtract
                                            ).then_inc(s_mp, 1)
                    if j == 6 and has(b, -1, B - 2):
                        if has(b, 1, B):
                            dve.wait_ge(s_S, NCH * b)
                        dve.wait_ge(s_qm, b + 2)
                        v.tensor_copy(qst[w][0:SR, :], qmx[w][:]).then_inc(s_qs, 1)
            steps(dve, body)

        @block.gpsimd
        def _(pool):
            def body(k, u):
                b, w = 2 * k + u, 1 - u
                if not has(b, -2, B - 3):
                    return
                for units in units_of(b):
                    for unit in units:
                        idx = unit.idx
                        if unit.kind == "keys":
                            unit.read(pool)
                            if has(b, -1, B):
                                pool.wait_ge(s_kw[idx], 48 * (b + 2))
                            nc.gpsimd.tensor_tensor(kparts[:, idx, 1, :], krest[:, idx, :], zeros[:], ALU.add
                                                    ).then_inc(s_pool, 1)
                            pool.wait_ge(s_pool, 3 * (b + 2) + idx + 1)
                            nc.gpsimd.tensor_tensor(kparts[:, idx, 2, :], krest[:, idx, :], kparts[:, idx, 1, :],
                                                    ALU.subtract).then_inc(s_kp, 1)
                pool.wait_ge(s_ql[u], 32 * (k + 2))
                if has(b, 0, B):
                    pool.wait_ge(s_S, NCH * b + 1)
                    pool.wait_ge(s_qs, b + 1)
                nc.gpsimd.tensor_tensor(qmx[u][:], qraw[u][:].rearrange("q p r t -> q (p r t)"), qmask[:], ALU.mult
                                        ).then_inc(s_qm, 1)
            steps(pool, body)


def gated_experts(nc, x, xn, xnT, ident, tanh_g, guT, downT, s_wt, d):
    with ExitStack() as ctx:
        sp = Space(nc, ctx, "ge")
        slots = nc.dram_tensor("slots1", (SLOTS, C), F32, kind="Internal").ap()
        results = nc.dram_tensor("results1", (SLOTS, C), F32, kind="Internal").ap()
        index = [sp.sb(f"index{k}", [P, NT], U32) for k in range(2)]
        weight = [sp.sb(f"weight{k}", [P, NT]) for k in range(2)]
        tile_expert = sp.sb("tile_expert", [P, NTILE], U32)
        scale = sp.sb("scale", [P, 1])

        with ExitStack() as inner:
            n = Space(nc, inner, "rms")
            normT = n.sb("normT", [P, NT * P])
            zeros = n.sb("zeros", [P, SLOTS // P, C])
            ss, sd, rs = (n.sb(k, [P, NT]) for k in ("ss", "sd", "rs"))
            wrow, alpha, sq = n.sb("wrow", [P, C]), n.sb("alpha", [P, 1]), n.sb("sq", [P, C])
            xr = n.sb("xr", [P, NT, C])
            psT = n.ps("psT", [P, 2, 512])
            s_w, s_ss, s_v, s_sd, s_x, s_T, s_Tc, s_dve, s_act = (
                n.sem(k) for k in ("w", "ss", "v", "sd", "x", "T", "Tc", "dve", "act"))
            with nc.Block() as block:
                @block.sync
                def _(sync):
                    sync.dma_start(wrow[:], d["L1_norm_weight"]).then_inc(s_w, 16)
                    sync.dma_start(alpha[:], d["L1_alpha"]).then_inc(s_w, 16)

                @block.scalar
                def _(act):
                    for t in range(NT):
                        if t:
                            act.wait_ge(s_act, t)
                        nc.scalar.activation(sq[:], xn[:, t, :], ACT.Square, accum_out=ss[:, t:t + 1]
                                             ).then_inc(s_act, 1)
                    act.wait_ge(s_v, 1)
                    nc.scalar.activation(sd[:], sd[:], ACT.Sqrt).then_inc(s_sd, 1)
                    for q in range(NT // 4):
                        act.wait_ge(s_T, q + 1)
                        nc.scalar.copy(normT[:, 512 * q:512 * q + 512], psT[:, q % 2, :]).then_inc(s_Tc, 1)

                @block.vector
                def _(dve):
                    v = nc.vector
                    step = Steps(dve, s_dve)
                    dve.wait_ge(s_w, 32)
                    step.then(v.tensor_scalar(alpha[:], alpha[:], -0.5, 2.0, ALU.max, ALU.min))
                    step(v.tensor_scalar(scale[:], alpha[:], tanh_g, None, ALU.mult))
                    dve.wait_ge(s_act, NT)
                    v.tensor_scalar(sd[:], ss[:], 1.0 / C, RMS_EPS, ALU.mult, ALU.add).then_inc(s_v, 1)
                    dve.wait_ge(s_sd, 1)
                    step.then(v.reciprocal(rs[:], sd[:]))
                    for t in range(NT):
                        v.scalar_tensor_tensor(out=xr[:, t, :], in0=xn[:, t, :], scalar=rs[:, t:t + 1], in1=wrow[:],
                                               op0=ALU.mult, op1=ALU.mult).then_inc(s_x, 1)
                    for t in range(NT):
                        step(v.scalar_tensor_tensor(out=x[:, t, :], in0=xn[:, t, :], scalar=tanh_g, in1=x[:, t, :],
                                                    op0=ALU.mult, op1=ALU.add))

                @block.tensor
                def _(pe):
                    for q in range(NT // 4):
                        if q >= 2:
                            pe.wait_ge(s_Tc, q - 1)
                        pe.wait_ge(s_x, 4 * q + 4)
                        for r in range(4):
                            last = nc.tensor.transpose(psT[:, q % 2, P * r:P * r + P], xr[:, 4 * q + r, :], ident[:])
                        last.then_inc(s_T, 1)
            route(nc, "r1", xr, normT, E1, "L1_router_wT", None, scale[:, 0:1], index, weight, slots, zeros, d,
                  tile_expert)

        with ExitStack() as inner:
            f = Space(nc, inner, "gf")
            rows = [f.sb(f"rows{u}", [P, C]) for u in range(2)]
            tokT, hid = [f.sb(f"tokT{u}", [P, P]) for u in range(2)], [f.sb(f"hid{u}", [P, HID]) for u in range(2)]
            act_g = [f.sb(f"act_g{u}", [P, HID]) for u in range(2)]
            hidT = [f.sb(f"hidT{u}", [P, 3, P]) for u in range(2)]
            res = [f.sb(f"res{u}", [P, C]) for u in range(2)]
            got = [f.sb(f"got{q}", [P, C]) for q in range(4)]
            psX, psG, psU = f.ps("psX", [P, 512]), f.ps("psG", [P, 2, 512]), f.ps("psU", [P, 2, 512])
            psH, psY = f.ps("psH", [P, 512]), f.ps("psY", [P, 512])
            s_rows = [f.sem(f"rows{u}") for u in range(2)]
            s_X, s_x, s_G, s_U, s_g, s_h, s_H, s_Hc, s_Y, s_y, s_gz = (
                f.sem(k) for k in ("X", "x", "G", "U", "g", "h", "H", "Hc", "Y", "y", "gz"))
            s_res = [f.sem(f"res{u}") for u in range(2)]
            s_got, s_used = [f.sem(f"got{q}") for q in range(4)], [f.sem(f"used{q}") for q in range(4)]
            block = inner.enter_context(nc.Block())

            assert NTILE % 4 == 3

            def turns(engine, body):
                kept = body(0, 0, True, False, None)
                body(0, 1, False, False, kept)
                with engine.Fori(0, (NTILE - 7) // 4) as j:
                    kept = None
                    for r in range(4):
                        kept = body(2 * j + 1 + r // 2, r % 2, False, False, kept)
                kept = None
                for n in range(NTILE - 5, NTILE):
                    kept = body(n // 2, n % 2, False, n == NTILE - 1, kept)

            @block.sync
            def _(sync):
                def load(i, u, reuse):
                    n = 2 * i + u
                    if reuse:
                        sync.wait_ge(s_X, n - 1)
                    sync.dma_start(rows[u][:].unsqueeze(1), slots.rearrange("(i p) c -> p i c", p=P)[:, bass.ds(n, 1), :]
                                   ).then_inc(s_rows[u], 16)
                for n in range(4):
                    load(n // 2, n % 2, n >= 2)

                def body(i, u, ahead):
                    n = 2 * i + u
                    if ahead:
                        load(i + 2, u, True)
                    sync.wait_ge(s_y, n + 1)
                    sync.dma_start(results.rearrange("(i p) c -> p i c", p=P)[:, bass.ds(n, 1), :],
                                   res[u][:].unsqueeze(1)).then_inc(s_res[u], 16)
                with sync.Fori(0, NTILE // 2 - 2) as i:
                    for u in range(2):
                        body(i, u, True)
                for n in range(NTILE - 5, NTILE):
                    body(n // 2, n % 2, n + 4 < NTILE)
                for u in range(2):
                    sync.wait_ge(s_res[u], 16 * ((NTILE + 1 - u) // 2))

            @block.tensor
            def _(pe):
                def expert(n):
                    return pe.value_load(tile_expert[0:1, bass.ds(n, 1)], min_val=0, max_val=E1 - 1)

                def take(i, u):
                    n = 2 * i + u
                    pe.wait_ge(s_rows[u], 16 * i + 16)
                    if not (isinstance(n, int) and n == 0):
                        pe.wait_ge(s_x, n)
                    nc.tensor.transpose(psX[:, 0:P], rows[u][:], ident[:]).then_inc(s_X, 1)

                def up(i, u, e):
                    n = 2 * i + u
                    pe.wait_ge(s_x, n + 1)
                    if not (isinstance(n, int) and n < 2):
                        pe.wait_ge(s_h, n - 1)
                    nc.tensor.matmul(psG[:, u, 0:HID], tokT[u][:], guT[:, bass.ds(e * (2 * HID), HID)],
                                     start=True, stop=True).then_inc(s_G, 1)
                    nc.tensor.matmul(psU[:, u, 0:HID], tokT[u][:], guT[:, bass.ds(e * (2 * HID) + HID, HID)],
                                     start=True, stop=True).then_inc(s_U, 1)

                def body(i, u, first, last, kept):
                    n = 2 * i + u
                    if first:
                        pe.wait_ge(s_wt, 32)
                        take(0, 0)
                        take(0, 1)
                        up(0, 0, expert(0))
                    if not (isinstance(n, int) and n + 2 >= NTILE):
                        take(i + 1, u)
                    e = expert(n) if kept is None else kept
                    if not last:
                        next_e = expert(n + 1)
                    pe.wait_ge(s_h, n + 1)
                    if not first:
                        pe.wait_ge(s_Hc, n)
                    for q, (c0, w) in enumerate(HCH):
                        t = nc.tensor.transpose(psH[0:w, P * q:P * q + P], hid[u][:, c0:c0 + w], ident[:])
                    t.then_inc(s_H, 1)
                    if not last:
                        up(i + u, 1 - u, next_e)
                    pe.wait_ge(s_Hc, n + 1)
                    if not first:
                        pe.wait_ge(s_y, n)
                    for q, (c0, w) in enumerate(HCH):
                        t = nc.tensor.matmul(psY[:, 0:C], hidT[u][0:w, q, :], downT[0:w, bass.ds(e * (3 * C) + C * q, C)],
                                             start=(q == 0), stop=(q == 2))
                    t.then_inc(s_Y, 1)
                    return None if last else next_e
                turns(pe, body)

            @block.scalar
            def _(act):
                def silu(i, u):
                    n = 2 * i + u
                    act.wait_ge(s_G, n + 1)
                    if not (isinstance(n, int) and n < 2):
                        act.wait_ge(s_h, n - 1)
                    nc.scalar.activation(act_g[u][:], psG[:, u, 0:HID], ACT.Silu).then_inc(s_g, 1)

                def body(i, u, first, last, kept):
                    n = 2 * i + u
                    if first:
                        silu(i, u)
                    act.wait_ge(s_H, n + 1)
                    nc.scalar.copy(hidT[u][:, 0:2, :], psH[:, 0:2 * P].rearrange("p (q s) -> p q s", q=2))
                    nc.scalar.copy(hidT[u][0:HCH[2][1], 2, :], psH[0:HCH[2][1], 2 * P:3 * P]).then_inc(s_Hc, 1)
                    if not last:
                        silu(i + u, 1 - u)
                turns(act, body)

            @block.vector
            def _(dve):
                v = nc.vector
                for q in range(4):
                    t = v.memset(got[q][:], 0.0)
                t.then_inc(s_gz, 1)

                def tokens(i, u):
                    dve.wait_ge(s_X, 2 * i + u + 1)
                    v.tensor_copy(tokT[u][:], psX[:, 0:P]).then_inc(s_x, 1)

                def product(i, u):
                    n = 2 * i + u
                    dve.wait_ge(s_g, n + 1)
                    dve.wait_ge(s_U, n + 1)
                    v.tensor_tensor(hid[u][:], psU[:, u, 0:HID], act_g[u][:], ALU.mult).then_inc(s_h, 1)

                def body(i, u, first, last, kept):
                    n = 2 * i + u
                    if first:
                        tokens(0, 0)
                        tokens(0, 1)
                        product(0, 0)
                    if not (isinstance(n, int) and n + 2 >= NTILE):
                        tokens(i + 1, u)
                    if not last:
                        product(i + u, 1 - u)
                    dve.wait_ge(s_Y, n + 1)
                    if not (isinstance(n, int) and n < 2):
                        dve.wait_ge(s_res[u], 16 * i)
                    v.tensor_copy(res[u][:], psY[:, 0:C]).then_inc(s_y, 1)
                turns(dve, body)
                gather_results(nc, dve, None, x, results, index, weight, got, s_got, s_used)

            @block.gpsimd
            def _(pool):
                pool.wait_ge(s_gz, 1)
                for u in range(2):
                    pool.wait_ge(s_res[u], 16 * ((NTILE + 1 - u) // 2))
                gather_results(nc, None, pool, x, results, index, weight, got, s_got, s_used)


def build(nc, d, out, phases=4, first=0):
    with ExitStack() as ctx:
        sp = Space(nc, ctx, "all")
        x = sp.sb("x", [P, NT, C])
        ident = sp.sb("ident", [P, P])
        identb = sp.sb("identb", [P, P], BF16)
        rowmask = sp.sb("rowmask", [P, 1])
        gates = sp.sb("gates", [P, 4])
        tg = sp.sb("tg", [P, 4])
        s_zero, s_in, s_tg, s_out = (sp.sem(n) for n in ("zero", "in", "tg", "out"))

        with nc.Block() as block:
            @block.vector
            def _(dve):
                nc.vector.memset(x[:], 0.0).then_inc(s_zero, 1)
                dve.wait_ge(s_in, 16 * 6)
                nc.vector.tensor_copy(identb[:], ident[:]).then_inc(s_zero, 1)

            @block.sync
            def _(sync):
                sync.dma_start(gates[:, 0:2], d["g_xattn"]).then_inc(s_in, 16)
                sync.dma_start(gates[:, 2:4], d["g_ffn"]).then_inc(s_in, 16)
                sync.dma_start(ident[:], d["ident"]).then_inc(s_in, 16)
                sync.dma_start(rowmask[:], d["rowmask"]).then_inc(s_in, 16)
                sync.wait_ge(s_zero, 1)
                tiles = d["x"].rearrange("(t b) s c -> b s t c", b=2)
                for b, (lo, _) in enumerate(HALVES):
                    sync.dma_start(x[lo:lo + T, :, :], tiles[b]).then_inc(s_in, 16)

            @block.scalar
            def _(act):
                act.wait_ge(s_in, 16 * 6)
                nc.scalar.activation(tg[:], gates[:], ACT.Tanh).then_inc(s_tg, 1)

        if phases > 0 and first <= 0:
            with nc.sbuf_tensor("xnT0", [P, NT * P], F32) as xnT:
                with nc.sbuf_tensor("xn0", [P, NT, C], F32) as xn:
                    layer_norm(nc, "n0", x, xn, xnT, ident)
                vision_language_attention(nc, x, xnT, ident, tg[:, 0:1], rowmask[:, 0:1], d)
        if phases > 1 and first <= 1:
            with nc.sbuf_tensor("xnT1", [P, NT * P], F32) as xnT, nc.sbuf_tensor("xn1", [P, NT, C], F32) as xn:
                layer_norm(nc, "n1", x, xn, xnT, ident)
                capacity_experts(nc, x, xn, xnT, ident, tg[:, 2:3], d)
        guT = sp.sb("guT", [P, E1 * 2 * HID])
        downT = sp.sb("downT", [P, E1 * 3 * C])
        s_weights = sp.sem("weights")
        ahead = ((guT[:].rearrange("c (e h) -> c e h", e=E1), d["L1_guT"].rearrange("e c h -> c e h")),
                 (downT[:], d["L1_downT"]))
        if first > 2:
            with nc.Block() as block:
                @block.sync
                def _(sync):
                    for dst, src in ahead:
                        sync.dma_start(dst, src).then_inc(s_weights, 16)
        if phases > 2 and first <= 2:
            with nc.sbuf_tensor("xnT2", [P, NT * P], F32) as xnT:
                with nc.sbuf_tensor("xn2", [P, NT, C], F32) as xn:
                    layer_norm(nc, "n2", x, xn, xnT, ident)
                attention(nc, x, xnT, tg[:, 1:2], identb, ahead, s_weights, d)
        if phases > 3:
            with nc.sbuf_tensor("xnT3", [P, NT * P], F32) as xnT, nc.sbuf_tensor("xn3", [P, NT, C], F32) as xn:
                layer_norm(nc, "n3", x, xn, xnT, ident)
                gated_experts(nc, x, xn, xnT, ident, tg[:, 3:4], guT, downT, s_weights, d)

        with nc.Block() as block:
            @block.sync
            def _(sync):
                tiles = out.rearrange("(t b) s c -> b s t c", b=2)
                for b, (lo, _) in enumerate(HALVES):
                    sync.dma_start(tiles[b], x[lo:lo + T, :, :]).then_inc(s_out, 16)
                sync.wait_ge(s_out, 32)


def layouts(inputs):
    def col(a):
        return np.ascontiguousarray(a.reshape(-1, 1))

    def rows(a, n=P):
        return np.ascontiguousarray(np.broadcast_to(a.reshape(1, -1), (n, a.size)))

    i = {k: np.asarray(v) for k, v in inputs.items()}
    a = {"x": i["x"], "ctx": i["ctx_1024"], "ctxT": np.ascontiguousarray(i["ctx_1024"].transpose(0, 2, 1)),
         "g_xattn": rows(i["g_xattn"]), "g_ffn": rows(i["g_ffn"])}
    a["L0_W_vkT"] = np.ascontiguousarray(i["L0_xattn_W_vk"].T)
    a["L0_W_lk"] = i["L0_xattn_W_lk"]
    a["L0_W_vvT"] = np.ascontiguousarray(i["L0_xattn_W_vv"].T)
    a["L0_W_lvT"] = np.ascontiguousarray(i["L0_xattn_W_lv"].T)
    a["L0_b_vk"], a["L0_b_lk"] = col(i["L0_xattn_b_vk"]), col(i["L0_xattn_b_lk"])
    a["L0_b_vv"], a["L0_b_lv"] = rows(i["L0_xattn_b_vv"]), rows(i["L0_xattn_b_lv"])
    a["L0_router_wT"] = np.ascontiguousarray(i["L0_ffn_router_w"].T)
    a["L0_router_b"] = rows(np.tile(i["L0_ffn_router_b"], NT)).reshape(P, NT, E0)
    a["L0_w1"], a["L0_w2"] = i["L0_ffn_w1"], i["L0_ffn_w2"]
    a["L0_b1"] = np.ascontiguousarray(i["L0_ffn_b1"].reshape(E0, FC0, P).transpose(2, 0, 1))
    a["L0_b2"] = np.ascontiguousarray(i["L0_ffn_b2"].T)
    a["L1_W_qT"], a["L1_W_kT"] = (np.ascontiguousarray(i[f"L1_xattn_W{k}"].T) for k in "qk")
    a["L1_b_q"], a["L1_b_k"] = col(i["L1_xattn_bq"]), col(i["L1_xattn_bk"])
    a["L1_b_v"] = np.ascontiguousarray(np.broadcast_to(i["L1_xattn_bv"].reshape(-1, 1), (P, P)))
    a["L1_b_o"] = rows(i["L1_xattn_bo"])
    a["L1_W_vT"] = np.ascontiguousarray(np.concatenate([i["L1_xattn_Wv"].T, np.zeros((C, 16), np.float32)], 1))
    woT = np.ascontiguousarray(i["L1_xattn_Wo"].T)
    a["L1_W_oT_plain"] = woT
    placed = np.zeros((P, 2, C), np.float32)
    for h in range(H):
        s, j, r = h // 12, h // 3 % 4, h % 3
        placed[32 * j + 8 * r:32 * j + 8 * r + HD, s] = woT[HD * h:HD * h + HD]
    a["L1_W_oT"] = placed
    own, sel = np.zeros((P, 3), np.float32), np.zeros((P, 3, P), np.float32)
    for j in range(4):
        for r in range(3):
            own[32 * j + 8 * r:32 * j + 8 * r + 8, r] = 1
            sel[32 * j + 24, r, 32 * j + 8 * r:32 * j + 8 * r + 8] = 1
        sel[32 * j + 24, 0, 32 * j + 24:32 * j + 32] = 1
    a["pair_rows"] = np.zeros((P, NPAIR, 2 * T), np.float32)
    for row in range(3 * NPAIR):
        a["pair_rows"][96 + row, row % NPAIR] = 1
    a["pair_rows"] = a["pair_rows"].reshape(P, -1)
    a["own_rows"], a["sum_rows"] = own, sel
    pair = np.zeros((6, 2, HD, NPAIR, 2, T), np.float32)
    for r in range(2):
        pair[:, r, :, :, r, :] = 1
    a["pair_mask"] = pair.reshape(6 * 2 * HD, -1)
    a["L1_norm_weight"] = rows(i["L1_ffn_norm_weight"])
    a["L1_alpha"] = rows(i["L1_ffn_residual_alpha"])
    a["L1_router_wT"] = np.ascontiguousarray(i["L1_ffn_router_weight"].T)
    a["L1_guT"] = np.ascontiguousarray(i["L1_ffn_gate_up_weight"].transpose(0, 2, 1))
    down = np.zeros((P, E1, 3, C), np.float32)
    for q, (c0, w) in enumerate(HCH):
        down[:w, :, q] = i["L1_ffn_down_weight"][:, :, c0:c0 + w].transpose(2, 0, 1)
    a["L1_downT"] = down.reshape(P, -1)
    a["tile_ids"] = rows(np.repeat(np.arange(NTILE, dtype=np.float32), E1)).reshape(P, NTILE, E1)
    for e in (E0, E1):
        a[f"expert_ids{e}"] = rows(np.tile(np.arange(e, dtype=np.float32), NT)).reshape(P, NT, e)
    a["before"] = np.triu(np.ones((P, P), np.float32), 1)
    a["ones"] = np.ones((P, P), np.float32)
    a["ident"] = np.eye(P, dtype=np.float32)
    a["rowmask"] = np.array([[float(p % TP < T)] for p in range(P)], np.float32)
    return a


def kernel(**inputs):
    import concourse.bacc as bacc
    from concourse.bass_utils import run_bass_kernel_spmd

    nc = bacc.Bacc("TRN2", target_bir_lowering=False, num_devices=1)
    arrays = {f"in_{k}": v for k, v in layouts(inputs).items()}
    d = {k[3:]: nc.dram_tensor(k, v.shape, mybir.dt.from_np(v.dtype), kind="ExternalInput").ap()
         for k, v in arrays.items()}
    out = nc.dram_tensor("out", (B, T, C), F32, kind="ExternalOutput").ap()
    build(nc, d, out)
    return run_bass_kernel_spmd(nc, [arrays], core_ids=[0]).results[0]["out"]
```

```python
from contextlib import ExitStack

import numpy as np
import concourse.bass as bass
from concourse import mybir

ALU = mybir.AluOpType
ACT = mybir.ActivationFunctionType
F32 = mybir.dt.float32
BF16 = mybir.dt.bfloat16
U32 = mybir.dt.uint32
AX_X = mybir.AxisListType.X

P = 128
B, T, C, S = 32, 56, 128, 1500
TP = 64
NT = B // 2
KC, NCH = 125, 12
KT, NTH = 500, 3
HALVES = ((0, 64), (64, 128))

E0, FF0, CAP = 16, 512, 280
SLOTS = E0 * CAP
FC0 = FF0 // P
NTILE = (2 * B * T + 8 * (P - 1)) // P
GOT = 8
H, HD = 16, 8
NPAIR = H // 2
NG = 6
GW = 3 * T
E1, HID = 8, 352
HCH = ((0, 128), (128, 128), (256, 96))

LN_EPS, RMS_EPS = 1e-5, 1e-6


class Steps:

    def __init__(self, engine, sem, base=0):
        self.engine, self.sem, self.base, self.n = engine, sem, base, 0

    def __call__(self, instruction):
        self.n += 1
        instruction.then_inc(self.sem, 1)

    def wait(self):
        self.engine.wait_ge(self.sem, self.base + self.n)

    def then(self, instruction):
        self(instruction)
        self.wait()


class Space:

    def __init__(self, nc, ctx, phase):
        self.nc, self.ctx, self.phase = nc, ctx, phase
        self.sems = []
        ctx.callback(self.close)

    def close(self):
        if self.sems:
            self.nc.clear_and_free_semaphores(self.sems)
            self.nc.all_engine_barrier()

    def sb(self, name, shape, dt=F32):
        return self.ctx.enter_context(self.nc.sbuf_tensor(f"{self.phase}_{name}", shape, dt))

    def ps(self, name, shape, dt=F32):
        return self.ctx.enter_context(self.nc.psum_tensor(f"{self.phase}_{name}", shape, dt))

    def sem(self, name):
        self.sems.append(self.nc.alloc_semaphore(f"{self.phase}_{name}"))
        return self.sems[-1]


def logits(nc, pe, tokensT, router, psL, group):
    E = router.shape[-1]
    for t in range(4 * group, 4 * group + 4):
        nc.tensor.matmul(psL[:, E * t:E * t + E], tokensT[:, P * t:P * t + P], router[:], start=True, stop=True)


def layer_norm(nc, phase, x, xn, xnT, ident, router=None, router_source=None, psL=None):
    with ExitStack() as ctx:
        sp = Space(nc, ctx, phase)
        stats = sp.sb("stats", [P, NT, 6])
        mv = sp.sb("mv", [P, NT, 2])
        sd = sp.sb("sd", [P, NT])
        rs = sp.sb("rs", [P, NT])
        psT = sp.ps("psT", [P, 2, 512])
        s_dve, s_var, s_sd, s_xn, s_T, s_cp, s_rw = (
            sp.sem(n) for n in ("dve", "var", "sd", "xn", "T", "cp", "rw"))
        block = ctx.enter_context(nc.Block())

        @block.sync
        def _(sync):
            if router is not None:
                sync.dma_start(router[:], router_source).then_inc(s_rw, 16)

        @block.vector
        def _(dve):
            step = Steps(dve, s_dve)
            for t in range(NT):
                step(nc.vector.bn_stats(stats[:, t, :], x[:, t, :]))
            step.wait()
            for t in range(NT):
                step(nc.vector.bn_aggr(mv[:, t, :], stats[:, t, :]))
            step.wait()
            nc.vector.tensor_scalar(sd[:], mv[:, :, 1], 1.0, LN_EPS, ALU.mult, ALU.add).then_inc(s_var, 1)
            dve.wait_ge(s_sd, 1)
            step.then(nc.vector.reciprocal(rs[:], sd[:]))
            for t in range(NT):
                nc.vector.tensor_scalar(xn[:, t, :], x[:, t, :], mv[:, t, 0:1], rs[:, t:t + 1],
                                        ALU.subtract, ALU.mult).then_inc(s_xn, 1)

        @block.scalar
        def _(act):
            act.wait_ge(s_var, 1)
            nc.scalar.activation(sd[:], sd[:], ACT.Sqrt).then_inc(s_sd, 1)
            for q in range(NT // 4):
                act.wait_ge(s_T, q + 1)
                nc.scalar.copy(xnT[:, 512 * q:512 * q + 512], psT[:, q % 2, :]).then_inc(s_cp, 1)

        @block.tensor
        def _(pe):
            for q in range(NT // 4):
                if q >= 2:
                    pe.wait_ge(s_cp, q - 1)
                pe.wait_ge(s_xn, 4 * q + 4)
                for r in range(4):
                    last = nc.tensor.transpose(psT[:, q % 2, P * r:P * r + P], xn[:, 4 * q + r, :], ident[:])
                last.then_inc(s_T, 1)
                if router is not None and q:
                    if q == 1:
                        pe.wait_ge(s_rw, 16)
                    pe.wait_ge(s_cp, q)
                    logits(nc, pe, xnT, router, psL, q - 1)
            if router is not None:
                pe.wait_ge(s_cp, NT // 4)
                logits(nc, pe, xnT, router, psL, NT // 4 - 1)


def vision_language_attention(nc, x, xnT, ident, tanh_g, rowmask, d):
    with ExitStack() as ctx:
        sp = Space(nc, ctx, "va")
        wvkT, wlk, wvvT, wlvT = (sp.sb(n, [P, C]) for n in ("wvkT", "wlk", "wvvT", "wlvT"))
        bvk, blk = (sp.sb(n, [P, 1]) for n in ("bvk", "blk"))
        bvv, blv = (sp.sb(n, [P, C]) for n in ("bvv", "blv"))
        vkT = sp.sb("vkT", [P, NT * P])
        qT = sp.sb("qT", [P, NT * P])
        vis = sp.sb("vis", [P, NT, C])
        cb = sp.sb("cb", [P, NT])
        ctxT = [sp.sb(f"ctxT{u}", [P, 2, S]) for u in range(2)]
        side = [sp.sb(f"side{u}", [KC, 2, NCH, C + TP]) for u in range(2)]
        q_now = [sp.sb(f"q_now{u}", [P, P]) for u in range(2)]
        prob = [sp.sb(f"prob{u}", [P, S]) for u in range(2)]
        rsum = [sp.sb(f"rsum{u}", [P, 1]) for u in range(2)]
        nmax, nb0, nb1 = (sp.sb(n, [P, 1]) for n in ("nmax", "nb0", "nb1"))
        rinv, rmask = (sp.sb(n, [P, 1]) for n in ("rinv", "rmask"))
        rtg = [sp.sb(f"rtg{u}", [P, 1]) for u in range(2)]
        ac, acT, gbd = (sp.sb(n, [P, P]) for n in ("ac", "acT", "gbd"))

        psS = sp.ps("psS", [P, NTH, 512])
        psT = [sp.ps(f"psT{r}", [P, 512]) for r in range(2)]
        psA = sp.ps("psA", [P, 512])
        psM = sp.ps("psM", [P, 512])
        psV = sp.ps("psV", [P, 512])

        s_w, s_cT, s_cN = sp.sem("w"), [sp.sem(f"cT{u}") for u in range(2)], [sp.sem(f"cN{u}") for u in range(2)]
        s_vk, s_vkc, s_q, s_qc, s_v, s_vc, s_cb, s_cbc = (
            sp.sem(n) for n in ("vk", "vkc", "q", "qc", "v", "vc", "cb", "cbc"))
        s_xb, s_gz = sp.sem("xb"), sp.sem("gz")
        s_now, s_sc, s_nb, s_ex, s_T, s_Tc, s_A, s_ac, s_gb, s_aT, s_aTc, s_o, s_x = (
            sp.sem(n) for n in ("now", "sc", "nb", "ex", "T", "Tc", "A", "ac", "gb", "aT", "aTc", "o", "x"))
        s_dve = sp.sem("dve")
        SCALE = float(C) ** -0.5
        TURNS = NT // 2

        def load(sync, i, u):
            tile, first = 2 * i + u, isinstance(i, int) and i == 0
            if not first:
                sync.wait_ge(s_sc, 2 * i + u - 1)
            sync.dma_start(ctxT[u][:], d["ctxT"][bass.ds(2 * tile, 2)].rearrange("b c s -> c b s")
                           ).then_inc(s_cT[u], 16)
            if not first:
                sync.wait_ge(s_A, 2 * i + u - 1)
            for b in range(2):
                sync.dma_start(side[u][:, b, :, 0:C],
                               d["ctx"][bass.ds(2 * tile + b, 1)].rearrange("o (j k) c -> k (o j) c", k=KC)
                               ).then_inc(s_cN[u], 16)

        quarter = [psS[:, 0, :], psS[:, 1, :], psS[:, 2, :], psA[:]]
        third = [psT[0][:, 0:C], psT[1][:, 0:C], psV[:, 0:C]]
        block = nc.Block()
        with block:
            @block.sync
            def _(sync):
                for dst, src in ((wvkT, "L0_W_vkT"), (wlk, "L0_W_lk"), (wvvT, "L0_W_vvT"), (wlvT, "L0_W_lvT"),
                                 (bvk, "L0_b_vk"), (blk, "L0_b_lk"), (bvv, "L0_b_vv"), (blv, "L0_b_lv")):
                    sync.dma_start(dst[:], d[src]).then_inc(s_w, 16)
                for u in range(2):
                    load(sync, 0, u)

            @block.tensor
            def _(pe):
                pe.wait_ge(s_w, 128)
                for q in range(4):
                    nc.tensor.matmul(quarter[q], wvkT[:], xnT[:, 512 * q:512 * q + 512],
                                     start=True, stop=True).then_inc(s_vk, 1)
                for q in range(4):
                    pe.wait_ge(s_vkc, q + 1)
                    nc.tensor.matmul(quarter[q], wlk[:], vkT[:, 512 * q:512 * q + 512],
                                     start=True, stop=True).then_inc(s_q, 1)
                for t in range(NT):
                    if t >= 3:
                        pe.wait_ge(s_vc, t - 2)
                    nc.tensor.matmul(third[t % 3], xnT[:, P * t:P * t + P], wvvT[:],
                                     start=True, stop=True).then_inc(s_v, 1)
                    last = nc.tensor.matmul(psM[:, t:t + 1], vkT[:, P * t:P * t + P], blk[:], start=True, stop=True)
                last.then_inc(s_cb, 1)

            @block.scalar
            def _(act):
                act.wait_ge(s_w, 128)
                for q in range(4):
                    act.wait_ge(s_vk, q + 1)
                    nc.scalar.activation(vkT[:, 512 * q:512 * q + 512], quarter[q], ACT.Identity,
                                         bias=bvk[:, 0:1]).then_inc(s_vkc, 1)
                for q in range(4):
                    act.wait_ge(s_q, q + 1)
                    nc.scalar.mul(qT[:, 512 * q:512 * q + 512], quarter[q], SCALE).then_inc(s_qc, 1)
                act.wait_ge(s_cb, 1)
                nc.scalar.mul(cb[:], psM[:, 0:NT], SCALE).then_inc(s_cbc, 1)

            @block.vector
            def _(dve):
                step = Steps(dve, s_dve)
                nc.vector.memset(gbd[:], 0.0).then_inc(s_gz, 1)
                dve.wait_ge(s_w, 128)
                step.then(nc.vector.tensor_scalar(ac[:], blv[:], tanh_g, None, ALU.mult))
                for t in range(NT):
                    nc.vector.tensor_tensor(x[:, t, :], x[:, t, :], ac[:], ALU.add).then_inc(s_xb, 1)
                for t in range(NT):
                    dve.wait_ge(s_v, t + 1)
                    nc.vector.tensor_tensor(vis[:, t, :], third[t % 3], bvv[:], ALU.add).then_inc(s_vc, 1)

        block = nc.Block()
        with block:
            @block.sync
            def _(sync):
                with sync.Fori(1, TURNS) as i:
                    for u in range(2):
                        load(sync, i, u)

            def turns(engine, body):
                for u in range(2):
                    body(0, u, u == 0, False)
                with engine.Fori(1, TURNS - 1) as i:
                    for u in range(2):
                        body(i, u, False, False)
                for u in range(2):
                    body(TURNS - 1, u, False, u == 1)

            @block.tensor
            def _(pe):
                def scores(i, u):
                    n = 2 * i + u
                    pe.wait_ge(s_cT[u], 16 * i + 16)
                    pe.wait_ge(s_now, n + 1)
                    for th in range(NTH):
                        for b, (lo, hi) in enumerate(HALVES):
                            last = nc.tensor.matmul(psS[lo:hi, th, 0:KT], q_now[u][:, lo:hi],
                                                    ctxT[u][:, b, KT * th:KT * th + KT], start=True, stop=True)
                    last.then_inc(s_sc, 1)

                def turned(n):
                    pe.wait_ge(s_ac, n + 1)
                    if not (isinstance(n, int) and n == 0):
                        pe.wait_ge(s_aTc, n)
                    nc.tensor.transpose(psM[:, 0:P], ac[:], ident[:]).then_inc(s_aT, 1)

                def products(n):
                    pe.wait_ge(s_aTc, n + 1)
                    pe.wait_ge(s_gb, n + 1)
                    if not (isinstance(n, int) and n == 0):
                        pe.wait_ge(s_x, n)
                    nc.tensor.matmul(psV[:, 0:C], acT[:], wlvT[:], start=True, stop=False)
                    nc.tensor.matmul(psV[:, 0:C], gbd[:], vis[:, bass.ds(n, 1), :] if not isinstance(n, int)
                                     else vis[:, n, :], start=False, stop=True).then_inc(s_o, 1)

                def body(i, u, first, last_turn):
                    n = 2 * i + u
                    if first:
                        scores(i, u)
                    pe.wait_ge(s_ex, n + 1)
                    if not last_turn:
                        scores(i + u, 1 - u)
                    if not first:
                        turned(n - 1)
                    for r in range(3):
                        if r == 2 and not first:
                            products(n - 1)
                        if not (first and r < 2):
                            pe.wait_ge(s_Tc, 3 * n + r - 1)
                        for q in range(4):
                            j = 4 * r + q
                            bank = psT[(r + u) % 2]
                            last = nc.tensor.transpose(bank[0:KC, P * q:P * q + P],
                                                       prob[u][:, KC * j:KC * j + KC], ident[:])
                        last.then_inc(s_T, 1)
                    pe.wait_ge(s_cN[u], 32 * i + 32)
                    if not first:
                        pe.wait_ge(s_gb, n)
                    for r in range(3):
                        pe.wait_ge(s_Tc, 3 * n + r + 1)
                        for q in range(4):
                            j = 4 * r + q
                            for b, (lo, hi) in enumerate(HALVES):
                                last = nc.tensor.matmul(psA[lo:hi, 0:C + TP], side[u][:, b, j, C:C + TP],
                                                        side[u][:, b, j, :], start=(j == 0), stop=(j == NCH - 1))
                    last.then_inc(s_A, 1)
                turns(pe, body)
                turned(NT - 1)
                products(NT - 1)

            @block.scalar
            def _(act):
                def body(i, u, first, last_turn):
                    n = 2 * i + u
                    act.wait_ge(s_nb, n + 1)
                    if not (first or (isinstance(n, int) and n == 1)):
                        act.wait_ge(s_T, 3 * n - 3)
                    nc.scalar.activation(prob[u][:].rearrange("p (h k) -> p h k", h=NTH), psS[:, :, 0:KT], ACT.Exp,
                                         bias=nb1[:, 0:1], accum_out=rsum[u][:]).then_inc(s_ex, 1)
                turns(act, body)

            @block.vector
            def _(dve):
                AHEAD, STEPS = 3, 5

                def row(buf, t):
                    return buf[:, t:t + 1] if isinstance(t, int) else buf[:, bass.ds(t, 1)]

                def now(i, u):
                    t = 2 * i + u
                    src = qT[:, P * t:P * t + P] if isinstance(t, int) else qT[:, bass.ds(P * t, P)]
                    nc.vector.tensor_copy(q_now[u][:], src).then_inc(s_now, 1)

                def biases(i, u, step):
                    t = 2 * i + u
                    dve.wait_ge(s_sc, t + 1)
                    step.then(nc.vector.tensor_reduce(nmax[:], psS[:, :, 0:KT], axis=mybir.AxisListType.XY,
                                                      op=ALU.max, negate=True))
                    step.then(nc.vector.tensor_tensor(nb0[:], nmax[:], row(cb, t), ALU.subtract))
                    nc.vector.tensor_tensor(nb1[:], nb0[:], row(cb, t), ALU.add).then_inc(s_nb, 1)

                def turned(n):
                    dve.wait_ge(s_aT, n + 1)
                    nc.vector.tensor_copy(acT[:], psM[:, 0:P]).then_inc(s_aTc, 1)

                def add(n, u):
                    dve.wait_ge(s_o, n + 1)
                    xt = x[:, n:n + 1, :] if isinstance(n, int) else x[:, bass.ds(n, 1), :]
                    nc.vector.scalar_tensor_tensor(out=xt, in0=psV[:, 0:C].unsqueeze(1), scalar=rtg[u][:, 0:1],
                                                   in1=xt, op0=ALU.mult, op1=ALU.add).then_inc(s_x, 1)

                now(0, 0)
                now(0, 1)
                biases(0, 0, Steps(dve, s_dve, 1))

                def body(i, u, first, last_turn):
                    n = 2 * i + u
                    step = Steps(dve, s_dve, AHEAD + STEPS * n)
                    dve.wait_ge(s_ex, n + 1)
                    step.then(nc.vector.reciprocal(rinv[:], rsum[u][:]))
                    step(nc.vector.tensor_scalar(rtg[u][:], rinv[:], tanh_g, None, ALU.mult))
                    step(nc.vector.tensor_scalar(rmask[:], rinv[:], rowmask, None, ALU.mult))
                    if not first:
                        turned(n - 1)
                    for r in range(3):
                        bank = psT[(r + u) % 2]
                        dve.wait_ge(s_T, 3 * n + r + 1)
                        for b, (lo, hi) in enumerate(HALVES):
                            src = bank[0:KC, :].rearrange("p (q s) -> p q s", q=4)[:, :, lo:hi]
                            last = nc.vector.tensor_copy(side[u][:, b, 4 * r:4 * r + 4, C:C + TP], src)
                        last.then_inc(s_Tc, 1)
                    if not first:
                        add(n - 1, 1 - u)
                    if not last_turn:
                        biases(i + u, 1 - u, step)
                        if not (isinstance(n, int) and n + 2 >= NT):
                            now(i + 1, u)
                    dve.wait_ge(s_A, n + 1)
                    nc.vector.tensor_copy(ac[:], psA[:, 0:P]).then_inc(s_ac, 1)
                    step.wait()
                    for lo, hi in HALVES:
                        last = nc.vector.tensor_scalar(gbd[lo:hi, lo:hi], psA[lo:hi, C:C + TP], rmask[lo:hi, :], None,
                                                       ALU.mult)
                    last.then_inc(s_gb, 1)
                    if not last_turn:
                        assert step.n == STEPS
                turns(dve, body)
                turned(NT - 1)
                add(NT - 1, 1)


def route(nc, phase, tokens, rowmask, psL, experts_n, bias, scale, index, weight, slots, zeros, d, tile_expert=None,
          factor=None, meanwhile=None):
    E, capped = experts_n, tile_expert is None
    FAR = float(4 * SLOTS)
    with ExitStack() as ctx:
        r = Space(nc, ctx, phase)
        rb, experts = r.sb("rb", [P, NT, E]), r.sb("experts", [P, NT, E])
        before, ones = r.sb("before", [P, P]), r.sb("ones", [P, P])
        beforeb, onesb = r.sb("beforeb", [P, P], BF16), r.sb("onesb", [P, P], BF16)
        score, top = r.sb("score", [P, NT, E]), r.sb("top", [P, NT, 8])
        which = r.sb("which", [P, NT, 8], U32)
        whichf = r.sb("whichf", [P, 2, NT])
        diff, ex, den = (r.sb(n, [P, NT]) for n in ("diff", "ex", "den"))
        gate, kept, pos, slot, tmp = (r.sb(n, [P, 2, NT]) for n in ("gate", "kept", "pos", "slot", "tmp"))
        first = r.sb("first", [P, 2, NT])
        chosen = [r.sb(f"chosen{k}", [P, NT, E]) for k in range(2)]
        both = r.sb("both", [P, NT, E], BF16)
        prod = r.sb("prod", [P, NT, E])
        in_row = r.sb("in_row", [P, E])
        tiles, start, end = (r.sb(n, [P, E]) for n in ("tiles", "start", "end"))
        whole = r.sb("whole", [P, E], U32)
        tile_ids, ended = r.sb("tile_ids", [P, NTILE, E]), r.sb("ended", [P, NTILE, E])
        owner = r.sb("owner", [P, NTILE])
        psC, psN = r.ps("psC", [P, 512]), r.ps("psN", [P, 512])
        s_w, s_rb, s_both, s_C, s_d, s_ex, s_dve, s_row, s_N = (
            r.sem(n) for n in ("w", "rb", "both", "C", "d", "ex", "dve", "row", "N"))
        s_ids = r.sem("ids")
        s_zero, s_zd, s_idx, s_scat = (r.sem(n) for n in ("zero", "zd", "idx", "scat"))
        block = ctx.enter_context(nc.Block())
        sources = ((experts, f"expert_ids{E}"), (before, "before"), (ones, "ones"))

        @block.sync
        def _(sync):
            if bias is not None:
                sync.dma_start(rb[:], d[bias]).then_inc(s_rb, 16)
            for dst, src in sources:
                sync.dma_start(dst[:], d[src]).then_inc(s_w, 16)
            if not capped:
                sync.dma_start(tile_ids[:], d["tile_ids"]).then_inc(s_ids, 16)
            sync.wait_ge(s_zero, 1)
            sync.dma_start(slots.rearrange("(i p) c -> p i c", p=P), zeros[:]).then_inc(s_zd, 16)

        @block.tensor
        def _(pe):
            pe.wait_ge(s_both, 1)
            last = nc.tensor.matmul(psC[:, 0:NT * E], beforeb[:], both[:].rearrange("p t e -> p (t e)"),
                                    start=True, stop=False)
            for back in range(1, NT):
                last = nc.tensor.matmul(psC[:, E * back:NT * E], onesb[:],
                                        both[:, 0:NT - back, :].rearrange("p t e -> p (t e)"),
                                        start=False, stop=(back == NT - 1))
            last.then_inc(s_C, 1)
            if not capped:
                pe.wait_ge(s_row, 1)
                nc.tensor.matmul(psN[:, 0:E], ones[:], in_row[:], start=True, stop=True).then_inc(s_N, 1)

        @block.scalar
        def _(act):
            act.wait_ge(s_d, 1)
            nc.scalar.activation(ex[:], diff[:], ACT.Exp).then_inc(s_ex, 1)

        @block.vector
        def _(dve):
            v = nc.vector
            step = Steps(dve, s_dve)
            got = psL[:, 0:NT * E].rearrange("p (t e) -> p t e", e=E)
            if bias is not None:
                dve.wait_ge(s_rb, 16)
                step.then(v.tensor_tensor(score[:], got, rb[:], ALU.add))
            else:
                step.then(v.tensor_tensor(score[:], got, factor[:].unsqueeze(2).broadcast_to([P, NT, E]), ALU.mult))
            for t in range(NT):
                step(v.max(out=top[:, t, :], in_=score[:, t, :]))
            step.wait()
            for t in range(NT):
                step(v.max_index(out=which[:, t, :], in_max=top[:, t, :], in_values=score[:, t, :]))
            v.tensor_tensor(diff[:], top[:, :, 1], top[:, :, 0], ALU.subtract).then_inc(s_d, 1)
            step.wait()
            for k in range(2):
                step(v.tensor_copy(whichf[:, k, :], which[:, :, k]))
            step.wait()
            dve.wait_ge(s_w, 16 * len(sources))
            step(v.tensor_copy(beforeb[:], before[:]))
            step(v.tensor_copy(onesb[:], ones[:]))
            for k in range(2):
                step(v.tensor_tensor(chosen[k][:], experts[:],
                                     whichf[:, k, :].unsqueeze(2).broadcast_to([P, NT, E]), ALU.is_equal))
            step.wait()
            for k in range(2):
                step(v.tensor_scalar(chosen[k][:], chosen[k][:], rowmask, None, ALU.mult))
            step.wait()
            v.tensor_tensor(both[:], chosen[0][:], chosen[1][:], ALU.add).then_inc(s_both, 1)
            if not capped:
                dve.wait_ge(s_both, 1)
                v.reduce_sum(in_row[:], both[:].rearrange("p t e -> p e t"), axis=AX_X
                                ).then_inc(s_row, 1)
            dve.wait_ge(s_C, 1)
            place = psC[:, 0:NT * E].rearrange("p (t e) -> p t e", e=E)
            for k in range(2):
                step.then(v.tensor_tensor(prod[:], place, chosen[k][:], ALU.mult))
                step.then(v.reduce_sum(pos[:, k, :], prod[:], axis=AX_X))
            if capped:
                step.then(v.tensor_scalar(kept[:], pos[:], float(CAP), None, ALU.is_lt))
                step.then(v.tensor_scalar(kept[:], kept[:], rowmask, None, ALU.mult))
                step.then(v.tensor_scalar(first[:], whichf[:], float(CAP), None, ALU.mult))
            else:
                step(v.tensor_scalar(kept[:], pos[:], 0.0, rowmask, ALU.mult, ALU.add))
                dve.wait_ge(s_N, 1)
                step.then(v.tensor_scalar(whole[:], psN[:, 0:E], float(P - 1), None, ALU.add))
                step.then(v.tensor_scalar(whole[:], whole[:], 7, None, ALU.logical_shift_right))
                step.then(v.tensor_copy(tiles[:], whole[:]))
                step.then(v.memset(start[:, 0:1], 0.0))
                for e in range(1, E):
                    step.then(v.tensor_tensor(start[:, e:e + 1], start[:, e - 1:e], tiles[:, e - 1:e], ALU.add))
                step.then(v.tensor_tensor(end[:], start[:], tiles[:], ALU.add))
                dve.wait_ge(s_ids, 16)
                step.then(v.tensor_tensor(ended[:], tile_ids[:], end[:].unsqueeze(1).broadcast_to([P, NTILE, E]),
                                          ALU.is_ge))
                step.then(v.reduce_sum(owner[:], ended[:], axis=AX_X))
                step.then(v.tensor_scalar(tile_expert[:], owner[:], float(E - 1), None, ALU.min))
                for k in range(2):
                    step.then(v.tensor_tensor(prod[:], chosen[k][:], start[:].unsqueeze(1).broadcast_to([P, NT, E]),
                                              ALU.mult))
                    step.then(v.reduce_sum(first[:, k, :], prod[:], axis=AX_X))
                step.then(v.tensor_scalar(first[:], first[:], float(P), None, ALU.mult))
            step(v.tensor_tensor(slot[:], first[:], pos[:], ALU.add))
            step.then(v.tensor_scalar(tmp[:], kept[:], -FAR, FAR, ALU.mult, ALU.add))
            step.then(v.tensor_tensor(slot[:], slot[:], tmp[:], ALU.add))
            for k in range(2):
                v.tensor_copy(index[k][:], slot[:, k, :]).then_inc(s_idx, 1)
            dve.wait_ge(s_ex, 1)
            step.then(v.tensor_scalar(den[:], ex[:], 1.0, None, ALU.add))
            step.then(v.reciprocal(gate[:, 0, :], den[:]))
            step(v.tensor_tensor(gate[:, 1, :], gate[:, 0, :], ex[:], ALU.mult))
            step.wait()
            if capped:
                step.then(v.tensor_tensor(gate[:], gate[:], kept[:], ALU.mult))
                step.then(v.tensor_tensor(den[:], gate[:, 0, :], gate[:, 1, :], ALU.add))
                step.then(v.tensor_scalar(den[:], den[:], 1e-9, None, ALU.add))
                step.then(v.reciprocal(den[:], den[:]))
                step.then(v.tensor_tensor(gate[:], gate[:], den[:].unsqueeze(1).broadcast_to([P, 2, NT]), ALU.mult))
            step.then(v.tensor_scalar(gate[:], gate[:], scale, None, ALU.mult))
            for k in range(2):
                step(v.tensor_tensor(weight[k][:], gate[:, k, :], kept[:, k, :], ALU.mult))
            if meanwhile is not None:
                meanwhile(step)

        @block.gpsimd
        def _(pool):
            nc.gpsimd.memset(zeros[:], 0.0).then_inc(s_zero, 1)
            pool.wait_ge(s_zd, 16)
            for k in range(2):
                pool.wait_ge(s_idx, k + 1)
                for t in range(NT):
                    nc.gpsimd.indirect_dma_start(
                        out=slots, out_offset=bass.IndirectOffsetOnAxis(index[k][:, t:t + 1], 0),
                        in_=tokens[:, t, :], in_offset=None, bounds_check=SLOTS - 1, oob_is_err=False
                    ).then_inc(s_scat, 16)
            pool.wait_ge(s_scat, 16 * 2 * NT)


def gather_results(nc, dve, pool, x, results, index, weight, got, s_got, s_used, after=None, after_tiles=()):
    def take():
        for t in range(NT):
            for k in range(2):
                n = 2 * t + k
                q = n % GOT
                if n >= GOT:
                    pool.wait_ge(s_used[q], n // GOT)
                nc.gpsimd.indirect_dma_start(
                    out=got[q][:], out_offset=None, in_=results,
                    in_offset=bass.IndirectOffsetOnAxis(index[k][:, t:t + 1], 0),
                    bounds_check=SLOTS - 1, oob_is_err=False).then_inc(s_got[q], 16)

    def add():
        for t in range(NT):
            for k in range(2):
                n = 2 * t + k
                q = n % GOT
                dve.wait_ge(s_got[q], 16 * (n // GOT + 1))
                if k:
                    dve.wait_ge(s_used[(n - 1) % GOT], (n - 1) // GOT + 1)
                nc.vector.scalar_tensor_tensor(out=x[:, t, :], in0=got[q][:], scalar=weight[k][:, t:t + 1],
                                               in1=x[:, t, :], op0=ALU.mult, op1=ALU.add).then_inc(s_used[q], 1)
            if t in after_tiles:
                dve.wait_ge(s_used[q], n // GOT + 1)
                after(t)
    if dve is not None:
        add()
    else:
        take()


def capacity_experts(nc, x, xn, xnT, psL, ident, tanh_g, rowmask, d):
    with ExitStack() as ctx:
        sp = Space(nc, ctx, "ce")
        slots = nc.dram_tensor("slots", (SLOTS, C), F32, kind="Internal").ap()
        results = nc.dram_tensor("results", (SLOTS, C), F32, kind="Internal").ap()
        index = [sp.sb(f"index{k}", [P, NT], U32) for k in range(2)]
        weight = [sp.sb(f"weight{k}", [P, NT]) for k in range(2)]
        NROW = SLOTS // P
        rows = sp.sb("rows", [P, NROW, C])
        slotT = sp.sb("slotT", [P, SLOTS])

        route(nc, "r0", xn, rowmask, psL, E0, "L0_router_b", tanh_g, index, weight, slots, rows, d)

        with ExitStack() as inner:
            f = Space(nc, inner, "ff")
            w1 = [f.sb(f"w1{u}", [P, FF0]) for u in range(2)]
            w2 = [f.sb(f"w2{u}", [P, FC0, C]) for u in range(2)]
            b1, b2 = f.sb("b1", [P, E0, FC0]), f.sb("b2", [P, E0])
            b1now = [f.sb(f"b1now{u}", [P, FC0]) for u in range(2)]
            hT = [f.sb(f"hT{u}", [P, FC0, CAP]) for u in range(2)]
            outT = f.sb("outT", [P, SLOTS])
            got = [f.sb(f"got{q}", [P, C]) for q in range(GOT)]
            psT, psH = f.ps("psT", [P, 2, 512]), f.ps("psH", [P, 2, 512])
            psY = f.ps("psY", [P, 2, 512])
            warm = f.sb("warm", [P, 1])
            s_b, s_T, s_warm = (f.sem(n) for n in ("b", "T", "warm"))
            s_Tc, s_r = [f.sem(f"Tc{u}") for u in range(2)], [f.sem(f"r{u}") for u in range(2)]
            GROUPS = [(g, min(g + 12, NROW)) for g in range(0, NROW, 12)]
            s_rows = [f.sem(f"rows{g}") for g in range(len(GROUPS))]
            s_w1, s_w2 = [f.sem(f"w1{u}") for u in range(2)], [f.sem(f"w2{u}") for u in range(2)]
            s_H, s_h, s_Y, s_y, s_bn, s_R, s_st, s_gz = (
                f.sem(n) for n in ("H", "h", "Y", "y", "bn", "R", "st", "gz"))
            s_got, s_used = [f.sem(f"got{q}") for q in range(GOT)], [f.sem(f"used{q}") for q in range(GOT)]
            NORMS = (*((g, g + 4) for g in range(0, NT - 4, 4)), (NT - 4, NT - 1), (NT - 1, NT))
            stats, mv = f.sb("stats", [P, NT, 6]), f.sb("mv", [P, NT, 2])
            sd, rs = f.sb("sd", [P, NT]), f.sb("rs", [P, NT])
            s_ln, s_var, s_sd, s_xn, s_nT, s_nTc = (f.sem(n) for n in ("ln", "var", "sd", "xn", "nT", "nTc"))
            block = inner.enter_context(nc.Block())
            QT = -(-NROW // 4)

            def at(buf, n, width):
                return buf[:, width * n:width * n + width] if isinstance(n, int) else buf[:, bass.ds(width * n, width)]

            @block.sync
            def _(sync):
                for g, (lo, hi) in enumerate(GROUPS):
                    sync.dma_start(rows[:, lo:hi, :], slots.rearrange("(i p) c -> p i c", p=P)[:, lo:hi, :]
                                   ).then_inc(s_rows[g], 16)
                sync.dma_start(b1[:], d["L0_b1"]).then_inc(s_b, 16)
                sync.dma_start(b2[:], d["L0_b2"]).then_inc(s_b, 16)

                def load(i, u, first):
                    e = 2 * i + u
                    if not first:
                        sync.wait_ge(s_H, FC0 * (e - 1))
                    sync.dma_start(w1[u][:].unsqueeze(1), d["L0_w1"][bass.ds(e, 1)].rearrange("o c f -> c o f")
                                   ).then_inc(s_w1[u], 16)
                    if not first:
                        sync.wait_ge(s_Y, e - 1)
                    sync.dma_start(w2[u][:], d["L0_w2"][bass.ds(e, 1)].rearrange("o (q f) c -> f (o q) c", f=P)
                                   ).then_inc(s_w2[u], 16)
                for u in range(2):
                    load(0, u, True)
                with sync.Fori(1, E0 // 2) as i:
                    for u in range(2):
                        load(i, u, False)
                for lo, hi in GROUPS:
                    banks = -(-hi // 4)
                    sync.wait_ge(s_r[0], -(-banks // 2))
                    sync.wait_ge(s_r[1], banks // 2)
                    sync.dma_start(results.rearrange("(i p) c -> p i c", p=P)[:, lo:hi, :], rows[:, lo:hi, :]
                                   ).then_inc(s_st, 16)

            @block.tensor
            def _(pe):
                for q in range(QT):
                    if 4 * q % 12 == 0:
                        pe.wait_ge(s_rows[q // 3], 16)
                    if q >= 2:
                        pe.wait_ge(s_Tc[q % 2], q // 2)
                    for r in range(min(4, NROW - 4 * q)):
                        last = nc.tensor.transpose(psT[:, q % 2, P * r:P * r + P], rows[:, 4 * q + r, :], ident[:])
                    last.then_inc(s_T, 1)
                pe.wait_ge(s_Tc[0], -(-QT // 2))
                pe.wait_ge(s_Tc[1], QT // 2)

                def expert(i, u, first):
                    e = 2 * i + u
                    pe.wait_ge(s_w1[u], 16 * i + 16)
                    for q in range(FC0):
                        if not (first and e == 0 and q < 2):
                            pe.wait_ge(s_h, FC0 * e + q - 1)
                        nc.tensor.matmul(psH[:, q % 2, 0:CAP], w1[u][:, P * q:P * q + P], at(slotT, e, CAP),
                                         start=True, stop=True).then_inc(s_H, 1)
                    pe.wait_ge(s_w2[u], 16 * i + 16)
                    if not first:
                        pe.wait_ge(s_y, e - 1)
                    for q in range(FC0):
                        pe.wait_ge(s_h, FC0 * e + q + 1)
                        last = nc.tensor.matmul(psY[:, u, 0:CAP], w2[u][:, q, :], hT[u][:, q, :],
                                                start=(q == 0), stop=(q == FC0 - 1))
                    last.then_inc(s_Y, 1)
                for u in range(2):
                    expert(0, u, True)
                with pe.Fori(1, E0 // 2) as i:
                    for u in range(2):
                        expert(i, u, False)
                pe.wait_ge(s_y, E0)
                for q in range(QT):
                    if q >= 2:
                        pe.wait_ge(s_r[q % 2], q // 2)
                    for r in range(min(4, NROW - 4 * q)):
                        c0 = P * (4 * q + r)
                        last = nc.tensor.transpose(psT[:, q % 2, P * r:P * r + P], outT[:, c0:c0 + P], ident[:])
                    last.then_inc(s_R, 1)
                for g, (lo, hi) in enumerate(NORMS):
                    pe.wait_ge(s_xn, g + 1)
                    if g < 2:
                        pe.wait_ge(s_r[g], (QT + 1 - g) // 2)
                    else:
                        pe.wait_ge(s_nTc, g - 1)
                    for r in range(hi - lo):
                        last = nc.tensor.transpose(psT[:, g % 2, P * r:P * r + P], xn[:, lo + r, :], ident[:])
                    last.then_inc(s_nT, 1)

            @block.scalar
            def _(act):
                act.wait_ge(s_warm, 1)
                nc.scalar.activation(warm[:], warm[:], ACT.Gelu)
                for q in range(1, QT, 2):
                    n = P * min(4, NROW - 4 * q)
                    act.wait_ge(s_T, q + 1)
                    nc.scalar.copy(slotT[:, 512 * q:512 * q + n], psT[:, 1, 0:n]).then_inc(s_Tc[1], 1)

                def expert(i, u, first):
                    e = 2 * i + u
                    act.wait_ge(s_bn, e + 1)
                    if not first:
                        act.wait_ge(s_Y, e - 1)
                    for q in range(FC0):
                        act.wait_ge(s_H, FC0 * e + q + 1)
                        nc.scalar.activation(hT[u][:, q, :], psH[:, q % 2, 0:CAP], ACT.Gelu,
                                             bias=b1now[u][:, q:q + 1]).then_inc(s_h, 1)
                for u in range(2):
                    expert(0, u, True)
                with act.Fori(1, E0 // 2) as i:
                    for u in range(2):
                        expert(i, u, False)
                for q in range(1, QT, 2):
                    n = min(4, NROW - 4 * q)
                    act.wait_ge(s_R, q + 1)
                    nc.scalar.copy(rows[:, 4 * q:4 * q + n, :],
                                   psT[:, 1, 0:P * n].rearrange("p (r c) -> p r c", r=n)).then_inc(s_r[1], 1)
                for g, (lo, hi) in enumerate(NORMS):
                    act.wait_ge(s_var, g + 1)
                    nc.scalar.activation(sd[:, lo:hi], sd[:, lo:hi], ACT.Sqrt).then_inc(s_sd, 1)
                    act.wait_ge(s_nT, g + 1)
                    nc.scalar.copy(xnT[:, P * lo:P * hi], psT[:, g % 2, 0:P * (hi - lo)]).then_inc(s_nTc, 1)

            @block.vector
            def _(dve):
                v = nc.vector
                v.memset(warm[:], 0.0).then_inc(s_warm, 1)
                for q in range(GOT):
                    last = v.memset(got[q][:], 0.0)
                last.then_inc(s_gz, 1)
                for q in range(0, QT, 2):
                    n = P * min(4, NROW - 4 * q)
                    dve.wait_ge(s_T, q + 1)
                    v.tensor_copy(slotT[:, 512 * q:512 * q + n], psT[:, 0, 0:n]).then_inc(s_Tc[0], 1)
                dve.wait_ge(s_b, 32)

                def expert(i, u, first):
                    e = 2 * i + u
                    if not first:
                        dve.wait_ge(s_h, FC0 * (e - 1))
                    b1e = b1[:, e:e + 1, :] if isinstance(e, int) else b1[:, bass.ds(e, 1), :]
                    v.tensor_copy(b1now[u][:].unsqueeze(1), b1e).then_inc(s_bn, 1)

                def result(i, u):
                    e = 2 * i + u
                    dve.wait_ge(s_Y, e + 1)
                    b2e = b2[:, e:e + 1] if isinstance(e, int) else b2[:, bass.ds(e, 1)]
                    v.tensor_scalar(at(outT, e, CAP), psY[:, u, 0:CAP], b2e, None, ALU.add).then_inc(s_y, 1)
                for u in range(2):
                    expert(0, u, True)
                with dve.Fori(1, E0 // 2) as i:
                    for u in range(2):
                        result(i - 1, u)
                        expert(i, u, False)
                for u in range(2):
                    result(E0 // 2 - 1, u)
                for q in range(0, QT, 2):
                    n = min(4, NROW - 4 * q)
                    dve.wait_ge(s_R, q + 1)
                    v.tensor_copy(rows[:, 4 * q:4 * q + n, :],
                                  psT[:, 0, 0:P * n].rearrange("p (r c) -> p r c", r=n)).then_inc(s_r[0], 1)
                step = Steps(dve, s_ln)

                def normalise(t):
                    g = next(g for g, (_, hi) in enumerate(NORMS) if t < hi)
                    lo, hi = NORMS[g]
                    for t in range(lo, hi):
                        step(v.bn_stats(stats[:, t, :], x[:, t, :]))
                    step.wait()
                    for t in range(lo, hi):
                        step(v.bn_aggr(mv[:, t, :], stats[:, t, :]))
                    step.wait()
                    v.tensor_scalar(sd[:, lo:hi], mv[:, lo:hi, 1], 1.0, LN_EPS, ALU.mult, ALU.add).then_inc(s_var, 1)
                    dve.wait_ge(s_sd, g + 1)
                    step.then(v.reciprocal(rs[:, lo:hi], sd[:, lo:hi]))
                    for t in range(lo, hi):
                        last = v.tensor_scalar(xn[:, t, :], x[:, t, :], mv[:, t, 0:1], rs[:, t:t + 1],
                                               ALU.subtract, ALU.mult)
                    last.then_inc(s_xn, 1)

                gather_results(nc, dve, None, x, results, index, weight, got, s_got, s_used, normalise, [hi - 1 for _, hi in NORMS])

            @block.gpsimd
            def _(pool):
                pool.wait_ge(s_gz, 1)
                pool.wait_ge(s_st, 16 * len(GROUPS))
                gather_results(nc, None, pool, x, results, index, weight, got, s_got, s_used)


def attention(nc, x, xnT, tanh_g, identb, ahead, s_ahead, d):
    SCALE = float(HD) ** -0.5
    PARTS_Q = (0, 0, 0, 1, 1, 2)
    SR, MR = 6 * 2 * HD, 3 * NPAIR
    PW, QW = 2 * T, H * T
    MAXIMA = (1, 1, 1, 4, 4, 3, 4, 3, 3, 0, 0, 0)
    BANKS = 3
    PLACE = 3
    VALUES = 2
    qd = nc.dram_tensor("q_parts", (NPAIR, 6, 2, HD, NT * P), BF16, kind="Internal").ap()
    kd = nc.dram_tensor("k_parts", (2, NTH, NPAIR, 3, 2, HD, KT), BF16, kind="Internal").ap()

    with ExitStack() as ctx:
        sp = Space(nc, ctx, "at")
        wkT, wvT = sp.sb("wkT", [P, C]), sp.sb("wvT", [P, C])
        bk = sp.sb("bk", [P, 1])
        woT = sp.sb("woT", [P, 2, C])
        sel, own = sp.sb("sel", [P, 3, P]), sp.sb("own", [P, 3])
        qmask = sp.sb("qmask", [SR, QW], BF16)
        own_pair = sp.sb("own_pair", [P, QW])
        kst = [sp.sb(f"kst{u}", [SR + MR, NPAIR, S], BF16) for u in range(2)]
        val = [sp.sb(f"val{u}", [KC, NCH, NG, 32]) for u in range(2)]
        prob = [sp.sb(f"prob{u}", [KC, NG * GW]) for u in range(2)]
        zeros, warm = sp.sb("zeros", [P, KT]), sp.sb("warm", [P, 1])

        wqT, wo_plain, bvc = sp.sb("wqT", [P, C]), sp.sb("wo_plain", [P, C]), sp.sb("bvc", [P, P])
        bq, bqs, bo, out_b = sp.sb("bq", [P, 1]), sp.sb("bqs", [P, 1]), sp.sb("bo", [P, C]), sp.sb("out_b", [P, C])
        q32, qrest = sp.sb("q32", [P, NT * P]), sp.sb("qrest", [P, NT * P - 512])
        qparts, mask32 = sp.sb("qparts", [P, 3, NT * P], BF16), sp.sb("mask32", [SR, QW])
        s_mask, s_wq, s_wk, s_w, s_q, s_q32, s_B, s_qp, s_dve, s_bqs, s_one, s_ones, s_fill, s_warm = (
            sp.sem(n) for n in ("mask", "wq", "wk", "w", "q", "q32", "B", "qp", "dve", "bqs", "one", "ones",
                                "fill", "warm"))
        s_st = [sp.sem(f"st{part}") for part in range(2)]
        QUERIES = (slice(0, 512), slice(512, NT * P))
        loads = ((mask32, "pair_mask"), (wvT, "L1_W_vT"), (bvc, "L1_b_v"),
                 (wo_plain, "L1_W_oT_plain"), (bo, "L1_b_o"), (own_pair, "pair_rows"), (woT, "L1_W_oT"),
                 (sel, "sum_rows"), (own, "own_rows"))

        ctxT = [sp.sb(f"ctxT{u}", [P, S]) for u in range(2)]
        kparts = sp.sb("kparts", [P, NTH, 3, KT], BF16)
        krest = sp.sb("krest", [P, NTH, KT])
        qraw = [sp.sb(f"qraw{u}", [SR, NPAIR, 2, T], BF16) for u in range(2)]
        qmx = [sp.sb(f"qmx{u}", [SR, QW], BF16) for u in range(2)]
        qst = [sp.sb(f"qst{u}", [SR + MR, QW], BF16) for u in range(2)]
        mx, nmx, mrest = sp.sb("mx", [PW, NTH, NPAIR]), sp.sb("nmx", [PW, NPAIR]), sp.sb("mrest", [PW, NPAIR])
        mparts = sp.sb("mparts", [PW, 3, NPAIR], BF16)
        sums = sp.sb("sums", [P, 2, 3, T])
        mine, recip, attn = (sp.sb(n, [P, 2, T]) for n in ("mine", "recip", "attn"))

        psS = sp.ps("psS", [P, 2, 2, 512])
        psO = sp.ps("psO", [P, 512])
        psR = [sp.ps(f"psR{r}", [P, 512]) for r in range(BANKS)]

        s_ctx, s_ql = [sp.sem(f"ctx{u}") for u in range(2)], [sp.sem(f"ql{u}") for u in range(2)]
        s_kw, s_kl = [sp.sem(f"kw{i}") for i in range(NTH)], [sp.sem(f"kl{i}") for i in range(NTH)]
        s_free = [sp.sem(f"free{r}") for r in range(BANKS)]
        s_mid, s_kp = [sp.sem(f"mid{i}") for i in range(NTH)], [sp.sem(f"kp{i}") for i in range(NTH)]
        s_full, s_hi, s_qm, s_qs, s_mp, s_S, s_exp, s_PV, s_ou, s_on, s_dm, s_do, s_set = (
            sp.sem(n) for n in ("full", "hi", "qm", "qs", "mp", "S", "exp", "PV", "ou", "on", "dm", "do", "set"))

        def ring(b):
            known = isinstance(b, int)
            keys, maxima, ends = (not known or b <= B - 3), (not known or -1 <= b <= B - 2), (not known or b >= 1)
            units, m = [[] for _ in range(NCH)], 0
            for j in range(NCH):
                if keys and j < NTH:
                    units[j].append(("keys", j))
                if ends and j == 2:
                    units[j].append(("sums", 0))
                if maxima:
                    units[j] += [("max", m + r) for r in range(MAXIMA[j])]
                    m += MAXIMA[j]
                if maxima and 0 <= j - VALUES < 6:
                    units[j].insert(PLACE, ("values", j - VALUES))
                if ends and j == 5:
                    units[j].append(("out", 0))
                if maxima and j == 10:
                    units[j].append(("rows", 0))
            return units

        def size(b):
            return sum(len(u) for u in ring(b))

        UNITS = size(2)
        FIRST = sum(size(b) for b in range(-2, 2))
        assert UNITS % BANKS == 0

        class Unit:

            def __init__(self, kind, idx, b, local):
                self.kind, self.idx = kind, idx
                if isinstance(b, int):
                    n = sum(size(c) for c in range(-2, b)) + local
                    self.before, self.turn, self.new = n, n // BANKS, n < BANKS
                else:
                    n = FIRST - 2 * UNITS + local
                    self.before, self.turn, self.new = b * UNITS + n, b * (UNITS // BANKS) + n // BANKS, False
                self.bank, self.ps = n % BANKS, psR[n % BANKS]

            def free(self, engine):
                if not self.new:
                    engine.wait_ge(s_free[self.bank], self.turn)

            def full(self, engine):
                engine.wait_ge(s_full, self.before + 1)

            def read(self, engine):
                engine.wait_ge(s_free[self.bank], self.turn + 1)

        def units_of(b):
            local, out = 0, []
            for row in ring(b):
                out.append([Unit(kind, idx, b, local + r) for r, (kind, idx) in enumerate(row)])
                local += len(row)
            return out

        def the_unit(b, kind, idx=0):
            return next(unit for row in units_of(b) for unit in row if (unit.kind, unit.idx) == (kind, idx))

        def steps(engine, body, queries):
            for b in range(-2, 2):
                if b < 0:
                    queries(b + 2)
                body(b // 2, b % 2)
            with engine.Fori(1, B // 2 - 1) as k:
                for u in range(2):
                    body(k, u)
            for b in range(B - 2, B + 1):
                body(b // 2, b % 2)

        def has(b, lo, hi):
            return not isinstance(b, int) or lo <= b <= hi

        block = ctx.enter_context(nc.Block())

        @block.sync
        def _(sync):
            def load_ctx(c, u):
                sync.dma_start(ctxT[u][:].unsqueeze(1), d["ctxT"][bass.ds(c, 1)].rearrange("o c s -> c o s")
                               ).then_inc(s_ctx[u], 16)

            def fill_ones():
                sync.wait_ge(s_one, 1)
                for u in range(2):
                    rest = kst[u][SR:SR + MR, 1 - u:NPAIR, :]
                    sync.dma_start(rest, kst[0][SR:SR + MR, 0:1, :].broadcast_to([MR, NPAIR - 1 + u, S])
                                   ).then_inc(s_ones, 16)

            def load_queries(b, u):
                if has(b, 0, B):
                    sync.wait_ge(s_qm, b + 1)
                for r in range(2):
                    src = qd.rearrange("p c r d t -> (c r d) p t")[:, :, bass.ds((b + 2) * TP, T)]
                    sync.dma_start(qraw[u][:, :, r, :], src).then_inc(s_ql[u], 16)

            def body(k, u):
                b, w = 2 * k + u, 1 - u

                def store(i):
                    sync.wait_ge(s_kp[i], 3 * b + 9)
                    for c in range(3):
                        sync.dma_start(kd[u, i, :, c], kparts[:, i, c, :]).then_inc(s_kw[i], 16)
                if has(b, -1, B - 3):
                    for i in range(NTH):
                        if has(b, 0, B):
                            sync.wait_ge(s_kl[i], 48 * (b + 1))
                        store(i)
                    load_queries(b, u)

                def stack(i):
                    if has(b, 0, B):
                        sync.wait_ge(s_S, NCH * b + 4 * i + 4)
                    sync.wait_ge(s_kw[i], 48 * (b + 3))
                    for n, row in ((3, 0), (2, 48), (1, 80)):
                        src = kd[u, i][:, 0:n].rearrange("p c r d k -> (c r d) p k")
                        sync.dma_start(kst[u][row:row + 16 * n, :, KT * i:KT * i + KT], src).then_inc(s_kl[i], 16)
                if isinstance(b, int) and b == -2:
                    store(0)
                    sync.wait_ge(s_st[0], 16 * 6)
                    load_queries(b, u)
                    store(1)
                    stack(0)
                    store(2)
                elif has(b, -1, B - 3):
                    stack(0)
                if has(b, -1, B - 4):
                    the_unit(b, "values", 5).read(sync)
                    load_ctx(b + 3, w)
                if has(b, -2, B - 3):
                    stack(1)
                if has(b, -2, B - 3):
                    stack(2)

            for dst, src, sem in ((wqT, "L1_W_qT", s_wq), (bq, "L1_b_q", s_wq), (wkT, "L1_W_kT", s_wk),
                                  (bk, "L1_b_k", s_wk)):
                sync.dma_start(dst[:], d[src]).then_inc(sem, 16)
            load_ctx(0, 0)
            for dst, src in loads:
                sync.dma_start(dst[:], d[src]).then_inc(s_w, 16)
            for k in range(3):
                sync.wait_ge(s_qp, k + 1)
                for c in range(6):
                    if PARTS_Q[c] == k:
                        sync.dma_start(qd[:, c, :, :, QUERIES[0]], qparts[:, k, QUERIES[0]]).then_inc(s_st[0], 16)
            load_ctx(1, 1)
            for b in range(-2, 2):
                body(b // 2, b % 2)
                if b == -2:
                    fill_ones()
            sync.wait_ge(s_st[1], 16 * 6)
            for dst, src in ahead:
                sync.dma_start(dst, src).then_inc(s_ahead, 16)
            with sync.Fori(1, B // 2 - 2) as k:
                for u in range(2):
                    body(k, u)
            for b in range(B - 4, B + 1):
                body(b // 2, b % 2)

        @block.tensor
        def _(pe):
            def queries(part):
                if part == 0:
                    pe.wait_ge(s_wq, 32)
                    for k in range(4):
                        nc.tensor.matmul(psS[:, k // 2, k % 2, :], wqT[:], xnT[:, 512 * k:512 * k + 512],
                                         start=True, stop=True).then_inc(s_q, 1)
                    return
                pe.wait_ge(s_w, 16 * len(loads))
                nc.tensor.matmul(psO[:, 0:C], bvc[:], wo_plain[:], start=True, stop=True).then_inc(s_B, 1)
                pe.wait_ge(s_q32, 4)
                pe.wait_ge(s_set, 1)

            def body(k, u):
                b, w = 2 * k + u, 1 - u
                units = units_of(b)
                def form(unit):
                    unit.free(pe)
                    R, kind, idx = unit.ps, unit.kind, unit.idx
                    if kind == "keys":
                        if isinstance(b, int) and b == -2 and idx == 0:
                            pe.wait_ge(s_wk, 32)
                        if idx == 0:
                            pe.wait_ge(s_ctx[u], 16 * (k + 2))
                        last = nc.tensor.matmul(R[:, 0:KT], wkT[:], ctxT[u][:, KT * idx:KT * idx + KT],
                                                start=True, stop=True)
                    elif kind == "max":
                        i, p = idx // NPAIR, idx % NPAIR
                        if p == 0:
                            pe.wait_ge(s_kl[i], 48 * (b + 2))
                        if idx == 0:
                            pe.wait_ge(s_qm, b + 2)
                        last = nc.tensor.matmul(R[0:PW, 0:KT], qmx[w][:, PW * p:PW * p + PW],
                                                kst[w][0:SR, p, KT * i:KT * i + KT], start=True, stop=True)
                    elif kind == "values":
                        for r in range(2):
                            c0 = KC * (2 * idx + r)
                            last = nc.tensor.matmul(R[0:KC, C * r:C * r + C], ctxT[w][:, c0:c0 + KC], wvT[:],
                                                    start=True, stop=True)
                    elif kind == "sums":
                        pe.wait_ge(s_ou, b)
                        for r in range(3):
                            last = nc.tensor.matmul(R[:, 0:2 * T].rearrange("p (s t) -> p s t", s=2),
                                                    sel[:, r, :], sums[:, :, r, :], start=(r == 0), stop=(r == 2))
                    elif kind == "out":
                        pe.wait_ge(s_on, b)
                        for s in range(2):
                            last = nc.tensor.matmul(R[64 * w:64 * w + T, 0:C], attn[:, s, :], woT[:, s, :],
                                                    start=(s == 0), stop=(s == 1))
                    else:
                        pe.wait_ge(s_mp, b + 2)
                        last = nc.tensor.matmul(R[SR:SR + MR, 0:PW], mparts[:].rearrange("q c p -> q (c p)"),
                                                identb[0:PW, 0:PW], start=True, stop=True)
                    last.then_inc(s_full, 1)

                for j in range(NCH):
                    g = NCH * b + j
                    if has(b, 0, B - 1):
                        if isinstance(b, int) and b == 0 and j == 0:
                            pe.wait_ge(s_ones, 32)
                        if j == 0:
                            pe.wait_ge(s_qs, b + 1)
                            the_unit(b - 1, "rows").read(pe)
                        if has(b, 1, B) or j >= 2:
                            pe.wait_ge(s_exp, g - 1)
                        for p in range(NPAIR):
                            last = nc.tensor.matmul(psS[0:KC, j % 2, p // 4, PW * (p % 4):PW * (p % 4) + PW],
                                                    kst[u][:, p, KC * j:KC * j + KC], qst[u][:, PW * p:PW * p + PW],
                                                    start=True, stop=True)
                        last.then_inc(s_S, 1)
                    waiting = list(units[j])
                    if j < 10 and waiting:
                        form(waiting.pop(0))
                    if (j > 0 and has(b, 0, B - 1)) or (j == 0 and has(b, 1, B)):
                        jj, uu = (j - 1, u) if j else (NCH - 1, w)
                        pe.wait_ge(s_exp, g)
                        if jj == 0:
                            the_unit(b - 1, "values", 5).read(pe)
                            if has(b, 1, B):
                                pe.wait_ge(s_ou, b)
                        for G in range(NG):
                            r, s = G % 4, G // 4
                            if G == 4 and j < 10 and waiting:
                                form(waiting.pop(0))
                            last = nc.tensor.matmul(psO[32 * r:32 * r + 32, GW * s:GW * s + GW],
                                                    val[uu][:, jj, G, :], prob[jj % 2][:, GW * G:GW * G + GW],
                                                    start=(jj == 0 and s == 0), stop=(jj == NCH - 1),
                                                    skip_group_check=True)
                        last.then_inc(s_PV, 1)
                    for unit in waiting:
                        form(unit)
            steps(pe, body, queries)

        @block.scalar
        def _(act):
            def queries(part):
                if part == 0:
                    act.wait_ge(s_warm, 1)
                    nc.scalar.activation(warm[:], warm[:], ACT.Exp)
                    act.wait_ge(s_bqs, 1)
                    for k in range(4):
                        act.wait_ge(s_q, k + 1)
                        nc.scalar.activation(q32[:, 512 * k:512 * k + 512], psS[:, k // 2, k % 2, :], ACT.Identity,
                                             scale=SCALE, bias=bqs[:, 0:1]).then_inc(s_q32, 1)
                    act.wait_ge(s_wk, 32)
                    act.wait_ge(s_fill, 3)

            def store_queries():
                for k in range(3):
                    act.wait_ge(s_qp, 3 + k + 1)
                    for c in range(6):
                        if PARTS_Q[c] == k:
                            act.dma_start(qd[:, c, :, :, QUERIES[1]], qparts[:, k, QUERIES[1]]).then_inc(s_st[1], 16)

            def body(k, u):
                b, w = 2 * k + u, 1 - u
                if isinstance(b, int) and b == 0:
                    store_queries()
                units = units_of(b)
                for j in range(NCH):
                    g = NCH * b + j
                    if has(b, 0, B - 1):
                        act.wait_ge(s_S, g + 1)
                        if has(b, 1, B) or j >= 2:
                            act.wait_ge(s_PV, g - 1)
                        nc.scalar.activation(prob[j % 2][:, 0:QW].rearrange("p (a q) -> p a q", a=2),
                                             psS[0:KC, j % 2, :, 0:QW // 2], ACT.Exp).then_inc(s_exp, 1)
                    for unit in units[j]:
                        idx = unit.idx
                        if unit.kind == "keys":
                            unit.full(act)
                            if has(b, -1, B):
                                act.wait_ge(s_kw[idx], 48 * (b + 2))
                            nc.scalar.activation(kparts[:, idx, 0, :], unit.ps[:, 0:KT], ACT.Identity,
                                                 bias=bk[:, 0:1]).then_inc(s_hi, 1)
                        if unit.kind == "values":
                            unit.full(act)
                            if idx == 0 and has(b, 1, B):
                                act.wait_ge(s_PV, NCH * b)
                            got = unit.ps[0:KC, 0:2 * C].rearrange("p (r c) -> p r c", r=2)
                            dst, whole = val[w][:, 2 * idx:2 * idx + 2], 24 * (NG - 1)
                            nc.scalar.copy(dst[:, :, 0:NG - 1, 0:24],
                                           got[:, :, 0:whole].rearrange("p r (g e) -> p r g e", e=24))
                            nc.scalar.copy(dst[:, :, NG - 1, 0:HD], got[:, :, whole:C]).then_inc(s_free[unit.bank], 1)
            steps(act, body, queries)

        @block.vector
        def _(dve):
            v = nc.vector
            step = Steps(dve, s_dve)
            v.memset(warm[:], 0.0).then_inc(s_warm, 1)
            v.memset(kst[0][SR:SR + MR, 0, :], 1.0).then_inc(s_one, 1)
            for u in range(2):
                v.memset(prob[u][:, QW:NG * GW], 1.0)

            def queries(part):
                if part == 0:
                    dve.wait_ge(s_wq, 32)
                    v.tensor_scalar(bqs[:], bq[:], SCALE, None, ALU.mult).then_inc(s_bqs, 1)
                    dve.wait_ge(s_q32, 1)
                else:
                    dve.wait_ge(s_w, 16 * len(loads))
                    v.tensor_copy(qmask[:], mask32[:]).then_inc(s_mask, 1)
                    dve.wait_ge(s_q32, 4)
                at, n = QUERIES[part], 3 * part
                rest = qrest[:, 0:at.stop - at.start]
                v.tensor_copy(qparts[:, 0, at], q32[:, at]).then_inc(s_qp, 1)
                dve.wait_ge(s_qp, n + 1)
                step.then(v.tensor_tensor(rest, q32[:, at], qparts[:, 0, at], ALU.subtract))
                v.tensor_copy(qparts[:, 1, at], rest).then_inc(s_qp, 1)
                dve.wait_ge(s_qp, n + 2)
                v.tensor_tensor(qparts[:, 2, at], rest, qparts[:, 1, at], ALU.subtract).then_inc(s_qp, 1)
                dve.wait_ge(s_qp, n + 3)
                if part == 0:
                    dve.wait_ge(s_wk, 32)
                    return
                dve.wait_ge(s_B, 1)
                step.then(v.tensor_tensor(out_b[:], psO[:, 0:C], bo[:], ALU.add))
                v.memset(psO[:], 1.0).then_inc(s_set, 1)

            def body(k, u):
                b, w = 2 * k + u, 1 - u
                units = units_of(b)
                for j in range(NCH):
                    if j == 0 and has(b, 1, B):
                        dve.wait_ge(s_PV, NCH * b)
                        v.tensor_copy(sums[:], psO[:, 0:2 * GW].rearrange("p (s r t) -> p s r t", s=2, r=3)
                                      ).then_inc(s_ou, 1)
                    if j == 1 and has(b, 1, B):
                        dve.wait_ge(s_ou, b)
                        v.tensor_scalar(mine[:], sums[:, :, 0, :], own[:, 0:1], None, ALU.mult).then_inc(s_do, 1)
                        for r in (1, 2):
                            dve.wait_ge(s_do, 3 * (b - 1) + r)
                            v.scalar_tensor_tensor(out=mine[:], in0=sums[:, :, r, :], scalar=own[:, r:r + 1],
                                                   in1=mine[:], op0=ALU.mult, op1=ALU.add).then_inc(s_do, 1)
                    if isinstance(b, int) and b == -1 and j == NCH - 1:
                        for t in range(NT):
                            step(v.scalar_tensor_tensor(out=x[:, t, :], in0=out_b[:], scalar=tanh_g, in1=x[:, t, :],
                                                        op0=ALU.mult, op1=ALU.add))
                        step.wait()
                    for unit in units[j]:
                        R, kind, idx, freed = unit.ps, unit.kind, unit.idx, s_free[unit.bank]
                        if kind == "values":
                            continue
                        if kind == "keys":
                            dve.wait_ge(s_hi, 3 * (b + 2) + idx + 1)
                            if has(b, -1, B):
                                dve.wait_ge(s_kp[idx], 3 * b + 6)
                            v.scalar_tensor_tensor(out=krest[:, idx, :], in0=R[:, 0:KT], scalar=bk[:, 0:1],
                                                   in1=kparts[:, idx, 0, :], op0=ALU.add, op1=ALU.subtract
                                                   ).then_inc(freed, 1)
                            if isinstance(b, int) and b == -2 and idx == NTH - 1:
                                the_unit(b, "keys", 1).read(dve)
                                v.tensor_copy(kparts[:, 1, 1, :], krest[:, 1, :]).then_inc(s_mid[1], 1)
                                dve.wait_ge(s_mid[1], 1)
                                v.tensor_tensor(kparts[:, 1, 2, :], krest[:, 1, :], kparts[:, 1, 1, :],
                                                ALU.subtract).then_inc(s_kp[1], 3)
                            continue
                        unit.full(dve)
                        if kind == "max":
                            i, p = idx // NPAIR, idx % NPAIR
                            v.reduce_max(mx[:, i, p:p + 1], R[0:PW, 0:KT], axis=AX_X).then_inc(freed, 1)
                        elif kind == "sums":
                            v.reciprocal(recip[:], R[:, 0:2 * T].rearrange("p (s t) -> p s t", s=2)
                                         ).then_inc(freed, 1)
                            unit.read(dve)
                            dve.wait_ge(s_do, 3 * b)
                            v.tensor_tensor(attn[:], mine[:], recip[:], ALU.mult).then_inc(s_on, 1)
                        elif kind == "out":
                            t = k - 1 if u == 0 else k
                            rows = slice(64 * w, 64 * w + T)
                            xt = x[rows, bass.ds(t, 1), :] if not isinstance(t, int) else x[rows, t:t + 1, :]
                            v.scalar_tensor_tensor(out=xt, in0=R[rows, 0:C].unsqueeze(1), scalar=tanh_g[rows, :],
                                                   in1=xt, op0=ALU.mult, op1=ALU.add).then_inc(freed, 1)
                        else:
                            rows = R[SR:SR + MR, 0:PW].unsqueeze(1).broadcast_to([MR, NPAIR, PW])
                            v.tensor_tensor(qst[w][SR:SR + MR, :].rearrange("q (p t) -> q p t", p=NPAIR), rows,
                                            own_pair[SR:SR + MR, :].rearrange("q (p t) -> q p t", p=NPAIR),
                                            ALU.mult).then_inc(freed, 1)
                        if kind == "max" and idx == 3 * NPAIR - 1:
                            unit.read(dve)
                            at = 4 * (b + 1)
                            v.tensor_reduce(nmx[:], mx[:].rearrange("q i p -> q p i"), axis=AX_X, op=ALU.max,
                                            negate=True).then_inc(s_dm, 1)
                            dve.wait_ge(s_dm, at + 1)
                            v.tensor_copy(mparts[:, 0, :], nmx[:]).then_inc(s_dm, 1)
                            dve.wait_ge(s_dm, at + 2)
                            v.tensor_tensor(mrest[:], nmx[:], mparts[:, 0, :], ALU.subtract).then_inc(s_dm, 1)
                            dve.wait_ge(s_dm, at + 3)
                            v.tensor_copy(mparts[:, 1, :], mrest[:]).then_inc(s_dm, 1)
                            dve.wait_ge(s_dm, at + 4)
                            v.tensor_tensor(mparts[:, 2, :], mrest[:], mparts[:, 1, :], ALU.subtract
                                            ).then_inc(s_mp, 1)
                    if j == 6 and has(b, -1, B - 2):
                        if has(b, 1, B):
                            dve.wait_ge(s_S, NCH * b)
                        dve.wait_ge(s_qm, b + 2)
                        v.tensor_copy(qst[w][0:SR, :], qmx[w][:]).then_inc(s_qs, 1)
            steps(dve, body, queries)

        @block.gpsimd
        def _(pool):
            fill = Steps(pool, s_fill)
            fill.then(nc.gpsimd.memset(zeros[:], 0.0))
            for u in range(2):
                fill.then(nc.gpsimd.memset(val[u][:], 1.0))

            def queries(part):
                pass

            def body(k, u):
                b, w = 2 * k + u, 1 - u
                if not has(b, -2, B - 3):
                    return
                for units in units_of(b):
                    for unit in units:
                        idx = unit.idx
                        if unit.kind == "keys" and not (isinstance(b, int) and b == -2 and idx == 1):
                            unit.read(pool)
                            if has(b, -1, B):
                                pool.wait_ge(s_kw[idx], 48 * (b + 2))
                            nc.gpsimd.tensor_tensor(kparts[:, idx, 1, :], krest[:, idx, :], zeros[:], ALU.add
                                                    ).then_inc(s_mid[idx], 1)
                            pool.wait_ge(s_mid[idx], b + 3)
                            nc.gpsimd.tensor_tensor(kparts[:, idx, 2, :], krest[:, idx, :], kparts[:, idx, 1, :],
                                                    ALU.subtract).then_inc(s_kp[idx], 3)
                if isinstance(b, int) and b == -2:
                    pool.wait_ge(s_mask, 1)
                pool.wait_ge(s_ql[u], 32 * (k + 2))
                if has(b, 0, B):
                    pool.wait_ge(s_S, NCH * b + 1)
                    pool.wait_ge(s_qs, b + 1)
                nc.gpsimd.tensor_tensor(qmx[u][:], qraw[u][:].rearrange("q p r t -> q (p r t)"), qmask[:], ALU.mult
                                        ).then_inc(s_qm, 1)
            steps(pool, body, queries)


def gated_experts(nc, x, xn, psL, ident, tanh_g, rowmask, guT, downT, s_wt, out, d):
    with ExitStack() as ctx:
        sp = Space(nc, ctx, "ge")
        slots = nc.dram_tensor("slots1", (SLOTS, C), F32, kind="Internal").ap()
        results = nc.dram_tensor("results1", (SLOTS, C), F32, kind="Internal").ap()
        index = [sp.sb(f"index{k}", [P, NT], U32) for k in range(2)]
        weight = [sp.sb(f"weight{k}", [P, NT]) for k in range(2)]
        tile_expert = sp.sb("tile_expert", [P, NTILE], U32)
        scale = sp.sb("scale", [P, 1])

        with ExitStack() as inner:
            n = Space(nc, inner, "norm")
            xnT = n.sb("xnT", [P, NT * P])
            zeros = n.sb("zeros", [P, SLOTS // P, C])
            stats, mv = n.sb("stats", [P, NT, 6]), n.sb("mv", [P, NT, 2])
            sd, rs = n.sb("sd", [P, NT]), n.sb("rs", [P, NT])
            square, sums = [n.sb(f"square{u}", [P, C]) for u in range(2)], n.sb("sums", [P, NT])
            root, inverse = n.sb("root", [P, NT]), n.sb("inverse", [P, NT])
            router, weighted = n.sb("router", [P, E1]), n.sb("weighted", [P, E1])
            wrow, wcol, alpha = n.sb("wrow", [P, C]), n.sb("wcol", [P, 1]), n.sb("alpha", [P, 1])
            eps = n.sb("eps", [P, 1])
            xr = n.sb("xr", [P, NT, C])
            psT = n.ps("psT", [P, 2, 512])
            s_w, s_rw, s_eps, s_dve, s_var, s_sd, s_xn, s_wr, s_T, s_Tc, s_sq, s_rms = (n.sem(k) for k in (
                "w", "rw", "eps", "dve", "var", "sd", "xn", "wr", "T", "Tc", "sq", "rms"))
            with nc.Block() as block:
                @block.sync
                def _(sync):
                    sync.dma_start(router[:], d["L1_router_wT"]).then_inc(s_rw, 16)
                    sync.dma_start(wcol[:], d["L1_norm_weight_col"]).then_inc(s_rw, 16)
                    sync.dma_start(wrow[:], d["L1_norm_weight"]).then_inc(s_w, 16)
                    sync.dma_start(alpha[:], d["L1_alpha"]).then_inc(s_w, 16)

                @block.scalar
                def _(act):
                    act.wait_ge(s_var, 1)
                    nc.scalar.activation(sd[:], sd[:], ACT.Sqrt).then_inc(s_sd, 1)
                    act.wait_ge(s_eps, 1)
                    for g in range(NT // 4):
                        act.wait_ge(s_T, g + 1)
                        nc.scalar.copy(xnT[:, 512 * g:512 * g + 512], psT[:, g % 2, :]).then_inc(s_Tc, 1)
                        act.wait_ge(s_xn, 4 * g + 4)
                        for t in range(4 * g, 4 * g + 4):
                            if t >= 2:
                                act.wait_ge(s_sq, t - 1)
                            nc.scalar.activation(square[t % 2][:], xn[:, t, :], ACT.Square,
                                                 accum_out=sums[:, t:t + 1]).then_inc(s_sq, 1)
                        act.wait_ge(s_sq, 4 * g + 4)
                        four = slice(4 * g, 4 * g + 4)
                        nc.scalar.activation(root[:, four], sums[:, four], ACT.Sqrt, scale=1.0 / C, bias=eps[:, 0:1]
                                             ).then_inc(s_rms, 1)

                @block.vector
                def _(dve):
                    v = nc.vector
                    step = Steps(dve, s_dve)
                    v.memset(eps[:], RMS_EPS).then_inc(s_eps, 1)
                    for t in range(NT):
                        step(v.bn_stats(stats[:, t, :], x[:, t, :]))
                    step.wait()
                    for t in range(NT):
                        step(v.bn_aggr(mv[:, t, :], stats[:, t, :]))
                    step.wait()
                    v.tensor_scalar(sd[:], mv[:, :, 1], 1.0, LN_EPS, ALU.mult, ALU.add).then_inc(s_var, 1)
                    dve.wait_ge(s_rw, 32)
                    v.tensor_scalar(weighted[:], router[:], wcol[:, 0:1], None, ALU.mult).then_inc(s_wr, 1)
                    dve.wait_ge(s_sd, 1)
                    step.then(v.reciprocal(rs[:], sd[:]))
                    for t in range(NT):
                        v.tensor_scalar(xn[:, t, :], x[:, t, :], mv[:, t, 0:1], rs[:, t:t + 1],
                                        ALU.subtract, ALU.mult).then_inc(s_xn, 1)
                    dve.wait_ge(s_w, 32)
                    step.then(v.tensor_scalar(alpha[:], alpha[:], -0.5, 2.0, ALU.max, ALU.min))
                    step(v.tensor_scalar(scale[:], alpha[:], tanh_g, None, ALU.mult))
                    dve.wait_ge(s_xn, NT)
                    for g in range(NT // 4):
                        four = slice(4 * g, 4 * g + 4)
                        dve.wait_ge(s_rms, g + 1)
                        step.then(v.reciprocal(inverse[:, four], root[:, four]))
                        for t in range(4 * g, 4 * g + 4):
                            step(v.scalar_tensor_tensor(out=xr[:, t, :], in0=xn[:, t, :], scalar=inverse[:, t:t + 1],
                                                        in1=wrow[:], op0=ALU.mult, op1=ALU.mult))

                @block.tensor
                def _(pe):
                    for q in range(NT // 4):
                        if q >= 2:
                            pe.wait_ge(s_Tc, q - 1)
                        pe.wait_ge(s_xn, 4 * q + 4)
                        for r in range(4):
                            last = nc.tensor.transpose(psT[:, q % 2, P * r:P * r + P], xn[:, 4 * q + r, :], ident[:])
                        last.then_inc(s_T, 1)
                        if q:
                            if q == 1:
                                pe.wait_ge(s_wr, 1)
                            pe.wait_ge(s_Tc, q)
                            logits(nc, pe, xnT, weighted, psL, q - 1)
                    pe.wait_ge(s_Tc, NT // 4)
                    logits(nc, pe, xnT, weighted, psL, NT // 4 - 1)

            def residual(step):
                for t in range(NT):
                    step(nc.vector.scalar_tensor_tensor(out=x[:, t, :], in0=xn[:, t, :], scalar=tanh_g,
                                                        in1=x[:, t, :], op0=ALU.mult, op1=ALU.add))

            route(nc, "r1", xr, rowmask, psL, E1, None, scale[:, 0:1], index, weight, slots, zeros, d,
                  tile_expert, inverse, residual)

        with ExitStack() as inner:
            f = Space(nc, inner, "gf")
            rows = [f.sb(f"rows{u}", [P, C]) for u in range(2)]
            tokT, hid = [f.sb(f"tokT{u}", [P, P]) for u in range(2)], [f.sb(f"hid{u}", [P, HID]) for u in range(2)]
            act_g = [f.sb(f"act_g{u}", [P, HID]) for u in range(2)]
            hidT = [f.sb(f"hidT{u}", [P, 3, P]) for u in range(2)]
            res = [f.sb(f"res{u}", [P, C]) for u in range(2)]
            got = [f.sb(f"got{q}", [P, C]) for q in range(GOT)]
            psX, psG, psU = f.ps("psX", [P, 512]), f.ps("psG", [P, 2, 512]), f.ps("psU", [P, 2, 512])
            psH, psY = f.ps("psH", [P, 512]), f.ps("psY", [P, 512])
            s_rows = [f.sem(f"rows{u}") for u in range(2)]
            s_X, s_x, s_G, s_U, s_g, s_h, s_H, s_Hc, s_Y, s_y, s_gz = (
                f.sem(k) for k in ("X", "x", "G", "U", "g", "h", "H", "Hc", "Y", "y", "gz"))
            s_res, s_out = [f.sem(f"res{u}") for u in range(2)], f.sem("out")
            s_got, s_used = [f.sem(f"got{q}") for q in range(GOT)], [f.sem(f"used{q}") for q in range(GOT)]
            block = inner.enter_context(nc.Block())

            assert NTILE % 4 == 3

            def turns(engine, body):
                kept = body(0, 0, True, False, None)
                body(0, 1, False, False, kept)
                with engine.Fori(0, (NTILE - 7) // 4) as j:
                    kept = None
                    for r in range(4):
                        kept = body(2 * j + 1 + r // 2, r % 2, False, False, kept)
                kept = None
                for n in range(NTILE - 5, NTILE):
                    kept = body(n // 2, n % 2, False, n == NTILE - 1, kept)

            @block.sync
            def _(sync):
                def load(i, u, reuse):
                    n = 2 * i + u
                    if reuse:
                        sync.wait_ge(s_X, n - 1)
                    tiles = slots.rearrange("(i p) c -> p i c", p=P)
                    sync.dma_start(rows[u][:].unsqueeze(1), tiles[:, bass.ds(n, 1), :]).then_inc(s_rows[u], 16)
                for n in range(4):
                    load(n // 2, n % 2, n >= 2)

                def body(i, u, ahead):
                    n = 2 * i + u
                    if ahead:
                        load(i + 2, u, True)
                    sync.wait_ge(s_y, n + 1)
                    sync.dma_start(results.rearrange("(i p) c -> p i c", p=P)[:, bass.ds(n, 1), :],
                                   res[u][:].unsqueeze(1)).then_inc(s_res[u], 16)
                with sync.Fori(0, NTILE // 2 - 2) as i:
                    for u in range(2):
                        body(i, u, True)
                for n in range(NTILE - 5, NTILE):
                    body(n // 2, n % 2, n + 4 < NTILE)
                for u in range(2):
                    sync.wait_ge(s_res[u], 16 * ((NTILE + 1 - u) // 2))
                tiles = out.rearrange("(t b) s c -> b s t c", b=2)
                for t in range(4, NT + 1, 4):
                    for q in range(GOT):
                        sync.wait_ge(s_used[q], 2 * t // GOT)
                    for b, (lo, _) in enumerate(HALVES):
                        sync.dma_start(tiles[b][:, t - 4:t, :], x[lo:lo + T, t - 4:t, :]).then_inc(s_out, 16)
                sync.wait_ge(s_out, 16 * 2 * NT // 4)

            @block.tensor
            def _(pe):
                def expert(n):
                    return pe.value_load(tile_expert[0:1, bass.ds(n, 1)], min_val=0, max_val=E1 - 1)

                def take(i, u):
                    n = 2 * i + u
                    pe.wait_ge(s_rows[u], 16 * i + 16)
                    if not (isinstance(n, int) and n == 0):
                        pe.wait_ge(s_x, n)
                    nc.tensor.transpose(psX[:, 0:P], rows[u][:], ident[:]).then_inc(s_X, 1)

                def up(i, u, e):
                    n = 2 * i + u
                    pe.wait_ge(s_x, n + 1)
                    if not (isinstance(n, int) and n < 2):
                        pe.wait_ge(s_h, n - 1)
                    nc.tensor.matmul(psG[:, u, 0:HID], tokT[u][:], guT[:, bass.ds(e * (2 * HID), HID)],
                                     start=True, stop=True).then_inc(s_G, 1)
                    nc.tensor.matmul(psU[:, u, 0:HID], tokT[u][:], guT[:, bass.ds(e * (2 * HID) + HID, HID)],
                                     start=True, stop=True).then_inc(s_U, 1)

                def body(i, u, first, last, kept):
                    n = 2 * i + u
                    if first:
                        pe.wait_ge(s_wt, 32)
                        take(0, 0)
                        take(0, 1)
                        up(0, 0, expert(0))
                    if not (isinstance(n, int) and n + 2 >= NTILE):
                        take(i + 1, u)
                    e = expert(n) if kept is None else kept
                    if not last:
                        next_e = expert(n + 1)
                    pe.wait_ge(s_h, n + 1)
                    if not first:
                        pe.wait_ge(s_Hc, n)
                    for q, (c0, w) in enumerate(HCH):
                        t = nc.tensor.transpose(psH[0:w, P * q:P * q + P], hid[u][:, c0:c0 + w], ident[:])
                    t.then_inc(s_H, 1)
                    if not last:
                        up(i + u, 1 - u, next_e)
                    pe.wait_ge(s_Hc, n + 1)
                    if not first:
                        pe.wait_ge(s_y, n)
                    for q, (c0, w) in enumerate(HCH):
                        t = nc.tensor.matmul(psY[:, 0:C], hidT[u][0:w, q, :],
                                             downT[0:w, bass.ds(e * (3 * C) + C * q, C)],
                                             start=(q == 0), stop=(q == 2))
                    t.then_inc(s_Y, 1)
                    return None if last else next_e
                turns(pe, body)

            @block.scalar
            def _(act):
                def silu(i, u):
                    n = 2 * i + u
                    act.wait_ge(s_G, n + 1)
                    if not (isinstance(n, int) and n < 2):
                        act.wait_ge(s_h, n - 1)
                    nc.scalar.activation(act_g[u][:], psG[:, u, 0:HID], ACT.Silu).then_inc(s_g, 1)

                def body(i, u, first, last, kept):
                    n = 2 * i + u
                    if first:
                        silu(i, u)
                    act.wait_ge(s_H, n + 1)
                    nc.scalar.copy(hidT[u][:, 0:2, :], psH[:, 0:2 * P].rearrange("p (q s) -> p q s", q=2))
                    nc.scalar.copy(hidT[u][0:HCH[2][1], 2, :], psH[0:HCH[2][1], 2 * P:3 * P]).then_inc(s_Hc, 1)
                    if not last:
                        silu(i + u, 1 - u)
                turns(act, body)

            @block.vector
            def _(dve):
                v = nc.vector
                for q in range(GOT):
                    t = v.memset(got[q][:], 0.0)
                t.then_inc(s_gz, 1)

                def tokens(i, u):
                    dve.wait_ge(s_X, 2 * i + u + 1)
                    v.tensor_copy(tokT[u][:], psX[:, 0:P]).then_inc(s_x, 1)

                def product(i, u):
                    n = 2 * i + u
                    dve.wait_ge(s_g, n + 1)
                    dve.wait_ge(s_U, n + 1)
                    v.tensor_tensor(hid[u][:], psU[:, u, 0:HID], act_g[u][:], ALU.mult).then_inc(s_h, 1)

                def body(i, u, first, last, kept):
                    n = 2 * i + u
                    if first:
                        tokens(0, 0)
                        tokens(0, 1)
                        product(0, 0)
                    if not (isinstance(n, int) and n + 2 >= NTILE):
                        tokens(i + 1, u)
                    if not last:
                        product(i + u, 1 - u)
                    dve.wait_ge(s_Y, n + 1)
                    if not (isinstance(n, int) and n < 2):
                        dve.wait_ge(s_res[u], 16 * i)
                    v.tensor_copy(res[u][:], psY[:, 0:C]).then_inc(s_y, 1)
                turns(dve, body)
                gather_results(nc, dve, None, x, results, index, weight, got, s_got, s_used)

            @block.gpsimd
            def _(pool):
                pool.wait_ge(s_gz, 1)
                for u in range(2):
                    pool.wait_ge(s_res[u], 16 * ((NTILE + 1 - u) // 2))
                gather_results(nc, None, pool, x, results, index, weight, got, s_got, s_used)


def build(nc, d, out):
    with ExitStack() as ctx:
        sp = Space(nc, ctx, "all")
        x = sp.sb("x", [P, NT, C])
        ident = sp.sb("ident", [P, P])
        identb = sp.sb("identb", [P, P], BF16)
        rowmask = sp.sb("rowmask", [P, 1])
        gates = sp.sb("gates", [P, 4])
        tg = sp.sb("tg", [P, 4])
        s_zero, s_in, s_tg = (sp.sem(n) for n in ("zero", "in", "tg"))

        with nc.Block() as block:
            @block.vector
            def _(dve):
                nc.vector.memset(x[:], 0.0).then_inc(s_zero, 1)
                dve.wait_ge(s_in, 16 * 6)
                nc.vector.tensor_copy(identb[:], ident[:]).then_inc(s_zero, 1)

            @block.sync
            def _(sync):
                sync.dma_start(gates[:, 0:2], d["g_xattn"]).then_inc(s_in, 16)
                sync.dma_start(gates[:, 2:4], d["g_ffn"]).then_inc(s_in, 16)
                sync.dma_start(ident[:], d["ident"]).then_inc(s_in, 16)
                sync.dma_start(rowmask[:], d["rowmask"]).then_inc(s_in, 16)
                sync.wait_ge(s_zero, 1)
                tiles = d["x"].rearrange("(t b) s c -> b s t c", b=2)
                for b, (lo, _) in enumerate(HALVES):
                    sync.dma_start(x[lo:lo + T, :, :], tiles[b]).then_inc(s_in, 16)

            @block.scalar
            def _(act):
                act.wait_ge(s_in, 16 * 6)
                nc.scalar.activation(tg[:], gates[:], ACT.Tanh).then_inc(s_tg, 1)

        with nc.sbuf_tensor("xnT0", [P, NT * P], F32) as xnT:
            with nc.sbuf_tensor("xn0", [P, NT, C], F32) as xn:
                layer_norm(nc, "n0", x, xn, xnT, ident)
            vision_language_attention(nc, x, xnT, ident, tg[:, 0:1], rowmask[:, 0:1], d)
        xnT = sp.sb("xnT1", [P, NT * P])
        with nc.sbuf_tensor("xn1", [P, NT, C], F32) as xn, nc.sbuf_tensor("router0", [P, E0], F32) as router, \
                nc.psum_tensor("psL0", [P, 512], F32) as psL:
            layer_norm(nc, "n1", x, xn, xnT, ident, router=router, router_source=d["L0_router_wT"], psL=psL)
            capacity_experts(nc, x, xn, xnT, psL, ident, tg[:, 2:3], rowmask[:, 0:1], d)

        guT = sp.sb("guT", [P, E1 * 2 * HID])
        downT = sp.sb("downT", [P, E1 * 3 * C])
        s_weights = sp.sem("weights")
        ahead = ((guT[:].rearrange("c (e h) -> c e h", e=E1), d["L1_guT"].rearrange("e c h -> c e h")),
                 (downT[:], d["L1_downT"]))
        attention(nc, x, xnT, tg[:, 1:2], identb, ahead, s_weights, d)
        with nc.sbuf_tensor("xn3", [P, NT, C], F32) as xn, nc.psum_tensor("psL1", [P, 512], F32) as psL:
            gated_experts(nc, x, xn, psL, ident, tg[:, 3:4], rowmask[:, 0:1], guT, downT,
                          s_weights, out, d)


def layouts(inputs):
    def col(a):
        return np.ascontiguousarray(a.reshape(-1, 1))

    def rows(a, n=P):
        return np.ascontiguousarray(np.broadcast_to(a.reshape(1, -1), (n, a.size)))

    i = {k: np.asarray(v) for k, v in inputs.items()}
    a = {"x": i["x"], "ctx": i["ctx_1024"], "ctxT": np.ascontiguousarray(i["ctx_1024"].transpose(0, 2, 1)),
         "g_xattn": rows(i["g_xattn"]), "g_ffn": rows(i["g_ffn"])}
    a["L0_W_vkT"] = np.ascontiguousarray(i["L0_xattn_W_vk"].T)
    a["L0_W_lk"] = i["L0_xattn_W_lk"]
    a["L0_W_vvT"] = np.ascontiguousarray(i["L0_xattn_W_vv"].T)
    a["L0_W_lvT"] = np.ascontiguousarray(i["L0_xattn_W_lv"].T)
    a["L0_b_vk"], a["L0_b_lk"] = col(i["L0_xattn_b_vk"]), col(i["L0_xattn_b_lk"])
    a["L0_b_vv"], a["L0_b_lv"] = rows(i["L0_xattn_b_vv"]), rows(i["L0_xattn_b_lv"])
    a["L0_router_wT"] = np.ascontiguousarray(i["L0_ffn_router_w"].T)
    a["L0_router_b"] = rows(np.tile(i["L0_ffn_router_b"], NT)).reshape(P, NT, E0)
    a["L0_w1"], a["L0_w2"] = i["L0_ffn_w1"], i["L0_ffn_w2"]
    a["L0_b1"] = np.ascontiguousarray(i["L0_ffn_b1"].reshape(E0, FC0, P).transpose(2, 0, 1))
    a["L0_b2"] = np.ascontiguousarray(i["L0_ffn_b2"].T)
    a["L1_W_qT"], a["L1_W_kT"] = (np.ascontiguousarray(i[f"L1_xattn_W{k}"].T) for k in "qk")
    a["L1_b_q"], a["L1_b_k"] = col(i["L1_xattn_bq"]), col(i["L1_xattn_bk"])
    a["L1_b_v"] = np.ascontiguousarray(np.broadcast_to(i["L1_xattn_bv"].reshape(-1, 1), (P, P)))
    a["L1_b_o"] = rows(i["L1_xattn_bo"])
    a["L1_W_vT"] = np.ascontiguousarray(i["L1_xattn_Wv"].T)
    woT = np.ascontiguousarray(i["L1_xattn_Wo"].T)
    a["L1_W_oT_plain"] = woT
    placed = np.zeros((P, 2, C), np.float32)
    for h in range(H):
        s, j, r = h // 12, h // 3 % 4, h % 3
        placed[32 * j + 8 * r:32 * j + 8 * r + HD, s] = woT[HD * h:HD * h + HD]
    a["L1_W_oT"] = placed
    own, sel = np.zeros((P, 3), np.float32), np.zeros((P, 3, P), np.float32)
    for j in range(4):
        for r in range(3):
            own[32 * j + 8 * r:32 * j + 8 * r + 8, r] = 1
            sel[32 * j + 24, r, 32 * j + 8 * r:32 * j + 8 * r + 8] = 1
        sel[32 * j + 24, 0, 32 * j + 24:32 * j + 32] = 1
    a["pair_rows"] = np.zeros((P, NPAIR, 2 * T), np.float32)
    for row in range(3 * NPAIR):
        a["pair_rows"][96 + row, row % NPAIR] = 1
    a["pair_rows"] = a["pair_rows"].reshape(P, -1)
    a["own_rows"], a["sum_rows"] = own, sel
    pair = np.zeros((6, 2, HD, NPAIR, 2, T), np.float32)
    for r in range(2):
        pair[:, r, :, :, r, :] = 1
    a["pair_mask"] = pair.reshape(6 * 2 * HD, -1)
    a["L1_norm_weight"] = rows(i["L1_ffn_norm_weight"])
    a["L1_norm_weight_col"] = col(i["L1_ffn_norm_weight"])
    a["L1_alpha"] = rows(i["L1_ffn_residual_alpha"])
    a["L1_router_wT"] = np.ascontiguousarray(i["L1_ffn_router_weight"].T)
    a["L1_guT"] = np.ascontiguousarray(i["L1_ffn_gate_up_weight"].transpose(0, 2, 1))
    down = np.zeros((P, E1, 3, C), np.float32)
    for q, (c0, w) in enumerate(HCH):
        down[:w, :, q] = i["L1_ffn_down_weight"][:, :, c0:c0 + w].transpose(2, 0, 1)
    a["L1_downT"] = down.reshape(P, -1)
    a["tile_ids"] = rows(np.repeat(np.arange(NTILE, dtype=np.float32), E1)).reshape(P, NTILE, E1)
    for e in (E0, E1):
        a[f"expert_ids{e}"] = rows(np.tile(np.arange(e, dtype=np.float32), NT)).reshape(P, NT, e)
    a["before"] = np.triu(np.ones((P, P), np.float32), 1)
    a["ones"] = np.ones((P, P), np.float32)
    a["ident"] = np.eye(P, dtype=np.float32)
    a["rowmask"] = np.array([[float(p % TP < T)] for p in range(P)], np.float32)
    return a


def kernel(**inputs):
    import concourse.bacc as bacc
    from concourse.bass_utils import run_bass_kernel_spmd

    nc = bacc.Bacc("TRN2", target_bir_lowering=False, num_devices=1)
    arrays = {f"in_{k}": v for k, v in layouts(inputs).items()}
    d = {k[3:]: nc.dram_tensor(k, v.shape, mybir.dt.from_np(v.dtype), kind="ExternalInput").ap()
         for k, v in arrays.items()}
    out = nc.dram_tensor("out", (B, T, C), F32, kind="ExternalOutput").ap()
    build(nc, d, out)
    return run_bass_kernel_spmd(nc, [arrays], core_ids=[0]).results[0]["out"]
```
